# Optimizing a Trainium2 kernel written in Bass

```python
import numpy as np
import jax
import jax.numpy as jnp

def _softmax(x, axis=-1):
    return jax.nn.softmax(x, axis=axis)

def _gelu(x):
    return jax.nn.gelu(x, approximate=True)

def _silu(x):
    return jax.nn.silu(x)

def _sigmoid(x):
    return jax.nn.sigmoid(x)

def _layernorm(x, axis=-1, eps=1e-05):
    m = jnp.mean(x, axis=axis, keepdims=True)
    v = jnp.var(x, axis=axis, keepdims=True)
    return (x - m) / jnp.sqrt(v + eps)

def _scatter_add(tgt, idx, src, axis=0):
    return tgt.at[idx].add(src)

def _segment_sum(src, seg, n):
    return jax.ops.segment_sum(src, seg, n)
kernel_name = 'mk_adaln_d1_jaxref_r4_b2df3d'

def setup_inputs(seed: int=0):
    np.random.seed(seed)
    _w = jnp.asarray

    def _L0_attn_setup():
        import jax, jax.numpy as jnp
        import numpy as np
        EMBED = 256
        HEADS = 16
        HEAD_DIM = EMBED // HEADS
        RANK = 8
        ALPHA = 16
        SCALE_LORA = ALPHA / RANK

        def _lora_linear(x, W, b, A, B):
            return x @ W.T + b + SCALE_LORA * (x @ A.T @ B.T)
        key = jax.random.key(seed)
        ks = jax.random.split(key, 17)
        d = {'x': jax.random.normal(ks[0], (2, 512, EMBED), dtype=jnp.float32)}
        names = ['q', 'k', 'v', 'o']
        i = 1
        for n in names:
            d[f'W{n}'] = jax.random.normal(ks[i], (EMBED, EMBED), dtype=jnp.float32) * 0.02
            i += 1
            d[f'b{n}'] = jnp.zeros((EMBED,), dtype=jnp.float32)
            d[f'A{n}'] = jax.random.normal(ks[i], (RANK, EMBED), dtype=jnp.float32) * 0.02
            i += 1
            d[f'B{n}'] = jax.random.normal(ks[i], (EMBED, RANK), dtype=jnp.float32) * 0.02
            i += 1
        return d
    _L0_attn_in = _L0_attn_setup()

    def _L0_ffn_setup():
        import jax, jax.numpy as jnp
        import numpy as np
        B, S, H, F, E = (1, 512, 256, 512, 8)

        def _swiglu(x, wg, wu, wd):
            return jax.nn.silu(x @ wg.T) * (x @ wu.T) @ wd.T
        key = jax.random.key(seed)
        ks = jax.random.split(key, 8)
        sc = 1.0 / np.sqrt(H)
        scf = 1.0 / np.sqrt(F)
        return {'hidden_states': jax.random.normal(ks[0], (B, S, H), jnp.float32), 'gate_w': jax.random.normal(ks[1], (E, H), jnp.float32) * sc, 'shared_gate': jax.random.normal(ks[2], (F, H), jnp.float32) * sc, 'shared_up': jax.random.normal(ks[3], (F, H), jnp.float32) * sc, 'shared_down': jax.random.normal(ks[4], (H, F), jnp.float32) * scf, 'r_gate': jax.random.normal(ks[5], (E, F, H), jnp.float32) * sc, 'r_up': jax.random.normal(ks[6], (E, F, H), jnp.float32) * sc, 'r_down': jax.random.normal(ks[7], (E, H, F), jnp.float32) * scf}
    _L0_ffn_in = _L0_ffn_setup()
    _L0_c = _w((lambda *s: np.random.randn(*s).astype(np.float32) * 0.05)(2, 256))
    _L0_wmod = _w((lambda *s: np.random.randn(*s).astype(np.float32) * 0.05)(256, 6 * 256) * 256 ** (-0.5))
    _d = {'L0_attn_x': _L0_attn_in['x'], 'L0_attn_Wq': _L0_attn_in['Wq'], 'L0_attn_bq': _L0_attn_in['bq'], 'L0_attn_Aq': _L0_attn_in['Aq'], 'L0_attn_Bq': _L0_attn_in['Bq'], 'L0_attn_Wk': _L0_attn_in['Wk'], 'L0_attn_bk': _L0_attn_in['bk'], 'L0_attn_Ak': _L0_attn_in['Ak'], 'L0_attn_Bk': _L0_attn_in['Bk'], 'L0_attn_Wv': _L0_attn_in['Wv'], 'L0_attn_bv': _L0_attn_in['bv'], 'L0_attn_Av': _L0_attn_in['Av'], 'L0_attn_Bv': _L0_attn_in['Bv'], 'L0_attn_Wo': _L0_attn_in['Wo'], 'L0_attn_bo': _L0_attn_in['bo'], 'L0_attn_Ao': _L0_attn_in['Ao'], 'L0_attn_Bo': _L0_attn_in['Bo'], 'L0_ffn_gate_w': _L0_ffn_in['gate_w'], 'L0_ffn_shared_gate': _L0_ffn_in['shared_gate'], 'L0_ffn_shared_up': _L0_ffn_in['shared_up'], 'L0_ffn_shared_down': _L0_ffn_in['shared_down'], 'L0_ffn_r_gate': _L0_ffn_in['r_gate'], 'L0_ffn_r_up': _L0_ffn_in['r_up'], 'L0_ffn_r_down': _L0_ffn_in['r_down'], 'L0_c': _L0_c, 'L0_wmod': _L0_wmod}
    _x0 = _d['L0_attn_x']
    _d['L0_attn_x'] = jax.random.normal(jax.random.fold_in(jax.random.key(seed), 1), (2, 2048, 256), dtype=_x0.dtype)
    del _x0
    return _d

def reference(L0_attn_x, L0_attn_Wq, L0_attn_bq, L0_attn_Aq, L0_attn_Bq, L0_attn_Wk, L0_attn_bk, L0_attn_Ak, L0_attn_Bk, L0_attn_Wv, L0_attn_bv, L0_attn_Av, L0_attn_Bv, L0_attn_Wo, L0_attn_bo, L0_attn_Ao, L0_attn_Bo, L0_ffn_gate_w, L0_ffn_shared_gate, L0_ffn_shared_up, L0_ffn_shared_down, L0_ffn_r_gate, L0_ffn_r_up, L0_ffn_r_down, L0_c, L0_wmod):

    def _L0_attn_ref(x, Wq, bq, Aq, Bq, Wk, bk, Ak, Bk, Wv, bv, Av, Bv, Wo, bo, Ao, Bo):
        import jax, jax.numpy as jnp
        import numpy as np
        EMBED = 256
        HEADS = 16
        HEAD_DIM = EMBED // HEADS
        RANK = 8
        ALPHA = 16
        SCALE_LORA = ALPHA / RANK

        def _lora_linear(x, W, b, A, B):
            return x @ W.T + b + SCALE_LORA * (x @ A.T @ B.T)
        N, S, _ = x.shape
        Q = _lora_linear(x, Wq, bq, Aq, Bq).reshape(N, S, HEADS, HEAD_DIM)
        K = _lora_linear(x, Wk, bk, Ak, Bk).reshape(N, S, HEADS, HEAD_DIM)
        V = _lora_linear(x, Wv, bv, Av, Bv).reshape(N, S, HEADS, HEAD_DIM)
        energy = jnp.einsum('nqhd,nkhd->nhqk', Q, K) / jnp.sqrt(jnp.float32(HEAD_DIM))
        attn = jax.nn.softmax(energy, axis=-1)
        out = jnp.einsum('nhqk,nkhd->nqhd', attn, V).reshape(N, S, EMBED)
        return _lora_linear(out, Wo, bo, Ao, Bo)

    def _L0_ffn_ref(hidden_states, gate_w, shared_gate, shared_up, shared_down, r_gate, r_up, r_down):
        import jax, jax.numpy as jnp
        import numpy as np
        B, S, H, F, E = (1, 512, 256, 512, 8)

        def _swiglu(x, wg, wu, wd):
            return jax.nn.silu(x @ wg.T) * (x @ wu.T) @ wd.T
        b, s, h = hidden_states.shape
        x = hidden_states.reshape(-1, h)
        shared_out = _swiglu(x, shared_gate, shared_up, shared_down)
        logits = x @ gate_w.T
        top_id = jnp.argmax(logits, axis=-1)
        score = jax.nn.sigmoid(jnp.max(logits, axis=-1))
        xs = x * score[:, None]

        def body(acc, ws):
            wg, wu, wd, e = ws
            xe = jnp.where((top_id == e)[:, None], xs, 0.0)
            return (acc + _swiglu(xe, wg, wu, wd), None)
        acc0 = jnp.zeros_like(x)
        routed_out, _ = jax.lax.scan(body, acc0, (r_gate, r_up, r_down, jnp.arange(E)))
        return (shared_out + routed_out).reshape(b, s, h)
    x = L0_attn_x
    mod = (_silu(L0_c) @ L0_wmod).reshape(L0_c.shape[0], 6, 1, -1)
    sa, ca, ga, sb, cb, gb = (mod[:, 0], mod[:, 1], mod[:, 2], mod[:, 3], mod[:, 4], mod[:, 5])
    ga = (2 * (ga >= 0) - 1) * jnp.maximum(jnp.abs(ga), 0.25)
    gb = (2 * (gb >= 0) - 1) * jnp.maximum(jnp.abs(gb), 0.25)
    h = _layernorm(x, axis=-1) * (1 + ca) + sa
    x = x + ga * _L0_attn_ref(h, L0_attn_Wq, L0_attn_bq, L0_attn_Aq, L0_attn_Bq, L0_attn_Wk, L0_attn_bk, L0_attn_Ak, L0_attn_Bk, L0_attn_Wv, L0_attn_bv, L0_attn_Av, L0_attn_Bv, L0_attn_Wo, L0_attn_bo, L0_attn_Ao, L0_attn_Bo)
    h = _layernorm(x, axis=-1) * (1 + cb) + sb
    x = x + gb * _L0_ffn_ref(h, L0_ffn_gate_w, L0_ffn_shared_gate, L0_ffn_shared_up, L0_ffn_shared_down, L0_ffn_r_gate, L0_ffn_r_up, L0_ffn_r_down)
    return x

_drawn_inputs = setup_inputs


def setup_inputs(seed=0):
    import zlib

    import numpy as np

    out = dict(_drawn_inputs(seed))
    spreads = {'L0_attn_bq': (0.0, 0.8),
     'L0_attn_bk': (0.0, 2.0),
     'L0_attn_bv': (0.0, 0.755),
     'L0_attn_bo': (0.0, 0.758)}
    factors = {'L0_attn_Wq': 8.0,
     'L0_attn_Aq': 8.0,
     'L0_attn_Bq': 8.0,
     'L0_attn_Wk': 8.0,
     'L0_attn_Ak': 8.0,
     'L0_attn_Bk': 8.0,
     'L0_attn_Wv': 8.0,
     'L0_attn_Av': 8.0,
     'L0_attn_Bv': 8.0,
     'L0_attn_Wo': 6.094,
     'L0_attn_Ao': 8.0,
     'L0_attn_Bo': 8.0}
    for name, (base, spread) in spreads.items():
        noise = np.random.default_rng([zlib.crc32(name.encode()), seed]).standard_normal(out[name].shape)
        drawn = base * np.exp(spread * noise) if base else spread * noise
        out[name] = jnp.asarray(drawn.astype(out[name].dtype))
    for name, factor in factors.items():
        out[name] = (out[name] * factor).astype(out[name].dtype)
    return out
```

```python
from contextlib import ExitStack

import numpy as np

import concourse.bass as bass
from concourse import mybir

F32 = mybir.dt.float32
BF16 = mybir.dt.bfloat16
U32 = mybir.dt.uint32
ALU = mybir.AluOpType
ACT = mybir.ActivationFunctionType
AX = mybir.AxisListType

P = 128
B, S, D = 2, 2048, 256
H, DH = 16, 16
R = 8
LORA_SCALE = 2.0
F, E = 512, 8
T = B * S
HALF = D // P
FC = F // P
CH = 512
NCH = T // CH
CPB = S // CH
TPC = CH // P
NT = T // P
KT = S // P
NH = B * H
ROWS = 6 * DH
NTILE = NT + E - 1
NSLOT = NTILE * P
EPS = 1e-5
AHEAD = 2
Q_RUNS = ((0, 0, 3), (3, 0, 2), (5, 0, 1))
K_RUNS = ((0, 0, 3), (3, 1, 2), (5, 2, 1))
MAX_UNITS = [5] * 8 + [4] * 6 + [0] * 2
UNITS = KT * CPB
MAXIMA = UNITS + 1
RING = 3
NG = 4
NB = 3


def wait(eng, semaphore, n):
    if not isinstance(n, int) or n > 0:
        eng.wait_ge(semaphore, n)


class Region:

    def __init__(self, nc, start, end):
        self.nc, self.at, self.end = nc, start, end

    def __call__(self, name, shape, dt=F32):
        size = int(np.prod(shape[1:])) * (2 if dt == BF16 else 4)
        t = self.nc.alloc_sbuf_tensor_at(name, shape, dt, offset=self.at)
        self.at += -(-size // 32) * 32
        assert self.at <= self.end, name
        return t


class Steps:

    def __init__(self, eng, sem):
        self.eng, self.sem, self.count, self.loop = eng, sem, 0, None

    def __call__(self, ins):
        ins.then_inc(self.sem, 1)
        self.count += 1
        self.eng.wait_ge(self.sem, self.count if self.loop is None else self.loop + self.count)

    def turns(self, index, per):
        self.loop, self.first = index * per, self.count

    def close(self, trips, per):
        assert self.count == self.first + per, (self.count, self.first, per)
        self.count, self.loop = self.first + trips * per, None


def buffers(name, shape, dt, region, n=2):
    return [region(f"{name}{i}", shape, dt) for i in range(n)]


def block_kernel(nc, io, out):
    with ExitStack() as ctx:
        names = {}

        def sem(name):
            names[name] = ctx.enter_context(nc.semaphore(name))
            return names[name]

        ps = ctx.enter_context(nc.psum_tensor("ps", [P, 8, 512], F32))

        def scratch(name, shape, dt=F32):
            return nc.dram_tensor(name, shape, dt, kind="Internal").ap()

        qk_dram = scratch("qk_parts", (2, 3, B * D, S), BF16)
        o_dram = scratch("head_out", (NH, P, CH))
        h2_dram = scratch("h2_rows", (T, D))
        x1_dram = scratch("x1_rows", (T, D))
        x2_dram = scratch("x2_rows", (T, D))
        xs_dram = scratch("sorted_in", (NSLOT, D))
        ys_dram = scratch("sorted_out", (NSLOT, D))

        top = nc.sbuf_usable_end // 32 * 32
        expert_bytes = E * 4 * (2 * HALF * F + FC * D)
        experts_at = top - expert_bytes
        held = Region(nc, -(-nc.sbuf_base // 32) * 32, experts_at)
        ident = held("ident", [P, P])
        before = held("before", [P, P])
        eps = held("eps", [P, 1])
        woT = held("woT", [P, HALF, D])
        gateT = held("gateT", [P, HALF, E])
        rowmod = held("rowmod", [P, B, 4, D])
        gbo = held("gbo", [P, B, D])
        wgT = held("wgT", [P, HALF, F])
        wuT = held("wuT", [P, HALF, F])
        wdT = held("wdT", [P, FC, D])
        ones = held("ones", [P, P])
        zero_row = held("zero_row", [P, D])
        logits = held("logits", [P, NT, E])
        iotas = held("iotas", [P, E + NT + 40])
        stage_at = held.at

        r = Region(nc, stage_at, experts_at)
        v_all = r("v_all", [P, NT, D])
        qs = buffers("qs", [P, S], BF16, r, NB)
        ks = buffers("ks", [P, S], BF16, r, NB)
        vs = buffers("vs", [P, KT, 32], F32, r, NB)
        mb = buffers("mb", [KT, 2, P], BF16, r, NB)
        head_out = r("head_out_sb", [P, CH])
        prob = r("prob", [P, 2, S])
        mx = r("mx", [P, KT, CPB])
        mneg = r("mneg", [P, KT])

        r = Region(nc, experts_at, top)
        cT = r("cT", [P, HALF, B])
        cS = r("cS", [P, HALF, B])
        cB = r("cB", [P, HALF, B, P])
        wmod = r("wmod", [P, HALF, 6 * D])
        loA = r("loA", [R, 4, D])
        loB = r("loB", [R, 4, D])
        wT = r("wT", [P, 4, HALF, D])
        wqkv = r("wqkv", [P, 3, HALF, D])
        bqk = r("bqk", [P, 4])
        bqk_in = r("bqk_in", [P, 4])
        bv_row = r("bv_row", [P, D])
        bo_row = r("bo_row", [P, D])
        colmod = r("colmod", [P, 2, HALF, B])
        gtmp = r("gtmp", [P, 3, B, 2, D])
        x_t = buffers("x_t", [P, TPC, D], F32, r)
        xn = buffers("xn", [P, TPC, D], F32, r)
        hT = buffers("hT", [P, HALF, CH], F32, r)
        qf = buffers("qf", [P, CH], F32, r)
        rest = buffers("rest", [P, CH], F32, r)
        parts = buffers("parts", [P, 3, CH], BF16, r)
        stats = r("stats", [P, TPC, 6])
        mv = r("mv", [P, TPC, 2])
        std = r("std", [P, TPC])

        r = Region(nc, experts_at, top)
        rgT = r("rgT", [P, E, HALF, F])
        ruT = r("ruT", [P, E, HALF, F])
        rdT = r("rdT", [P, E, FC, D])

        r = Region(nc, stage_at, experts_at)
        h2T = r("h2T", [P, HALF, T])
        after_h2T = r.at
        o_in = buffers("o_in", [P, HALF, CH], F32, r)
        l_in = buffers("l_in", [P, HALF, CH], F32, r)
        x_in = buffers("x_in", [P, TPC, D], F32, r)
        x1 = buffers("x1", [P, TPC, D], F32, r)
        h2 = buffers("h2", [P, TPC, D], F32, r)
        h2Tc = buffers("h2Tc", [P, HALF, CH], F32, r)
        stats2 = r("stats2", [P, TPC, 6])
        mv2 = r("mv2", [P, TPC, 2])
        std2 = r("std2", [P, TPC])

        r = Region(nc, after_h2T, experts_at)
        onehot = r("onehot", [P, NT, E])
        ra = r("ra", [P, NT, E])
        rb = r("rb", [P, NT, E])
        rt = r("rt", [P, NT, E])
        rmax = r("rmax", [P, NT])
        rix = r("rix", [P, NT])
        score = r("score", [P, NT])
        slot = r("slot", [P, NT], U32)
        cmp8 = r("cmp8", [P, E, NT])
        segs = r("segs", [P, 4, E])
        tcmp = r("tcmp", [P, 40, E])
        tile_f = r("tile_f", [P, 40])
        tile_e = r("tile_e", [P, 40], U32)
        sc_x = buffers("sc_x", [P, D], F32, r)
        sc_in = buffers("sc_in", [P, D], F32, r)
        sc_ix = buffers("sc_ix", [P, 1], U32, r)
        sc_s = buffers("sc_s", [P, 1], F32, r)
        route_end = r.at
        sgate = buffers("sgate", [P, CH], F32, r)
        hid = buffers("hid", [P, FC, CH], F32, r)
        ymod = r("ymod", [P, TPC, D])
        xr = buffers("xr", [P, TPC, D], F32, r)

        r = Region(nc, stage_at, experts_at)
        xs = buffers("xs", [P, D], F32, r)
        xsT = buffers("xsT", [P, HALF, P], F32, r)
        esig = buffers("esig", [P, F], F32, r)
        ehid = buffers("ehid", [P, F], F32, r)
        ehT = buffers("ehT", [P, FC, P], F32, r)
        eout = buffers("eout", [P, D], F32, r)
        cy = buffers("cy", [P, D], F32, r, NG)
        cx = buffers("cx", [P, D], F32, r, NG)
        cix = buffers("cix", [P, 1], U32, r, NG)

        block = ctx.enter_context(nc.Block())

        s_chain = {e: sem(f"chain_{e}") for e in ("dve", "act", "pool")}
        s_hold = sem("s_hold")
        s_const = sem("s_const")
        s_shared = sem("s_shared")
        s_csilu = sem("s_csilu")
        s_crow = sem("s_crow")
        s_lora = sem("s_lora")
        s_weff = sem("s_weff")
        s_mrow = sem("s_mrow")
        s_mcol = sem("s_mcol")
        s_mod = sem("s_mod")
        s_x = [sem(f"s_xin{u}") for u in range(2)]
        s_var = sem("s_var")
        s_std = sem("s_std")
        s_norm = sem("s_norm")
        s_xn_free = sem("s_xn_free")
        s_hT = sem("s_hT")
        s_unit = sem("s_unit")
        s_qbank_free = sem("s_qbank_free")
        s_qf_free = sem("s_qf_free")
        s_parts = [sem(f"s_parts{u}") for u in range(2)]
        s_v = sem("s_v")
        s_vbank_free = sem("s_vbank_free")
        s_stack = [sem(f"s_stack{p}") for p in range(NB)]
        s_ones = sem("s_ones")
        s_vs = sem("s_vs")
        s_max = sem("s_max")
        s_ring = sem("s_ring")
        s_neg = sem("s_neg")
        s_mrows = [sem(f"s_mrows{p}") for p in range(NB)]
        s_score = sem("s_score")
        s_exp_free = sem("s_exp_free")
        s_prob_free = sem("s_prob_free")
        s_head = sem("s_head")
        s_hstore = sem("s_hstore")
        s_expert = sem("s_expert")
        s_zero = sem("s_zero")
        s_oin = [sem(f"s_oin{u}") for u in range(2)]
        s_on = sem("s_on")
        s_op = sem("s_op")
        s_xb = sem("s_xb")
        s_x1 = sem("s_x1")
        s_x1st = [sem(f"s_x1st{u}") for u in range(2)]
        s_var2 = sem("s_var2")
        s_std2 = sem("s_std2")
        s_n2 = sem("s_n2")
        s_h2 = sem("s_h2")
        s_h2st = [sem(f"s_h2st{u}") for u in range(2)]
        s_h2_free = sem("s_h2_free")
        s_h2T = sem("s_h2T")
        s_lgp = sem("s_lgp")
        s_lg = sem("s_lg")
        s_oh = sem("s_oh")
        s_rank = sem("s_rank")
        s_route = sem("s_route")
        s_sig = sem("s_sig")
        s_scx = [sem(f"s_scx{u}") for u in range(2)]
        s_scx_free = sem("s_scx_free")
        s_scat = [sem(f"s_scat{u}") for u in range(2)]
        s_xr = [sem(f"s_xr{u}") for u in range(2)]
        s_gu = sem("s_gu")
        s_silu = sem("s_silu")
        s_gu_free = sem("s_gu_free")
        s_y = sem("s_y")
        s_x2 = sem("s_x2")
        s_x2st = [sem(f"s_x2st{u}") for u in range(2)]
        s_xs = [sem(f"s_xs{u}") for u in range(2)]
        s_xs_free = sem("s_xs_free")
        s_xsT = sem("s_xsT")
        s_egu = sem("s_egu")
        s_esig = sem("s_esig")
        s_ehid = sem("s_ehid")
        s_ehTp = sem("s_ehTp")
        s_ehT = sem("s_ehT")
        s_ey = sem("s_ey")
        s_eout = sem("s_eout")
        s_est = [sem(f"s_est{u}") for u in range(2)]
        s_cx = [sem(f"s_cx{u}") for u in range(NG)]
        s_cy = [sem(f"s_cy{u}") for u in range(NG)]
        s_out = sem("s_out")
        s_ost = [sem(f"s_ost{u}") for u in range(NG)]

        def hold(eng):
            eng.sem_inc(s_hold, 1)

        const_loads = [
            (ident, io["ident"]), (before, io["before"]), (iotas, io["iotas"]), (cT, io["cT"]),
            (wmod, io["wmod"]), (loA, io["loA"]), (loB, io["loB"]), (wT, io["wT"]),
            (bqk_in, io["bqk"]), (gateT, io["gateT"]),
            (bv_row, io["bv"].partition_broadcast(P)), (bo_row, io["bo"].partition_broadcast(P)),
        ]
        CONST = 16 * len(const_loads)
        rows = lambda dram, t, n: dram[bass.ds(t * P, n * P), :].rearrange("(t p) d -> p t d", p=P)

        def setup_sync(sp):
            for dst, src in const_loads:
                sp.dma_start(dst[:], src).then_inc(s_const, 16)
            for dst, name in ((wgT, "wgT"), (wuT, "wuT"), (wdT, "wdT")):
                sp.dma_start(dst[:], io[name]).then_inc(s_shared, 16)

        def setup_scalar(act):
            act.wait_ge(s_const, CONST)
            act.activation(cS[:], cT[:], ACT.Silu).then_inc(s_csilu, 1)

        def setup_tensor(pe):
            pe.wait_ge(s_const, CONST)
            for m in range(4):
                for k in range(HALF):
                    mm = pe.matmul(ps[:, m, k * D:(k + 1) * D], loA[:, m, k * P:(k + 1) * P], loB[:, m, :],
                                   start=True, stop=True)
            mm.then_inc(s_lora, 1)
            pe.wait_ge(s_crow, 1)
            for b in range(B):
                for c in range(2):
                    for k in range(HALF):
                        mm = pe.matmul(ps[:, 4 + 2 * b + c, :], cB[:, k, b, :],
                                       wmod[:, k, (c + 1) * 512:(c + 2) * 512], start=(k == 0), stop=(k == 1))
            mm.then_inc(s_mrow, 1)
            pe.wait_ge(s_weff, 1)
            for v in range(2 * HALF):
                for k in range(HALF):
                    mm = pe.matmul(ps[:, 0, v * B:(v + 1) * B], wmod[:, k, v * P:(v + 1) * P], cS[:, k, :],
                                   start=(k == 0), stop=(k == 1))
            mm.then_inc(s_mcol, 1)

        def setup_vector(dve, step):
            dve.memset(eps[:], EPS)
            dve.memset(ones[:], 1.0)
            dve.memset(zero_row[:], 0.0)
            dve.wait_ge(s_csilu, 1)
            dve.tensor_copy(cB[:], cS[:].unsqueeze(3).to_broadcast([P, HALF, B, P])).then_inc(s_crow, 1)
            dve.tensor_scalar(bqk[:, 0:2], bqk_in[:, 0:2], 0.25, None, ALU.mult)
            dve.tensor_copy(bqk[:, 2:4], bqk_in[:, 2:4])
            dve.wait_ge(s_lora, 1)
            for m in range(4):
                dst = wqkv[:, m] if m < 3 else woT[:]
                w = dve.scalar_tensor_tensor(dst.rearrange("p k d -> p (k d)"), ps[:, m, :], LORA_SCALE,
                                             wT[:, m].rearrange("p k d -> p (k d)"), ALU.mult, ALU.add)
            w.then_inc(s_weff, 1)
            dve.wait_ge(s_mrow, 1)
            step(dve.tensor_copy(rowmod[:].rearrange("p b v d -> p (b v d)"),
                                 ps[:, 4:8, :].rearrange("p c n -> p (c n)")))
            dve.tensor_scalar(rowmod[:, :, 2, :], rowmod[:, :, 2, :], 1.0, None, ALU.add)
            for v in (0, 3):
                g, mag, sign = rowmod[:, :, v, :], gtmp[:, 0, :, v // 3, :], gtmp[:, 1, :, v // 3, :]
                dve.tensor_scalar(sign, g, 0.0, 2.0, ALU.is_ge, ALU.mult)
                step(dve.tensor_scalar(mag, g, -1.0, None, ALU.mult))
                step(dve.tensor_tensor(mag, mag, g, ALU.max))
                step(dve.tensor_scalar(mag, mag, 0.25, None, ALU.max))
                step(dve.scalar_tensor_tensor(g, sign, -1.0, mag, ALU.add, ALU.mult))
            dve.tensor_tensor(gbo[:], rowmod[:, :, 0, :], bo_row[:].unsqueeze(1).to_broadcast([P, B, D]), ALU.mult)
            dve.wait_ge(s_mcol, 1)
            step(dve.tensor_copy(colmod[:].rearrange("p v k b -> p (v k b)"), ps[:, 0, 0:2 * HALF * B]))
            dve.tensor_scalar(colmod[:, 1], colmod[:, 1], 1.0, None, ALU.add).then_inc(s_mod, 1)

        def project_sync(sp):
            def load(g, u):
                sp.dma_start(x_t[u][:], rows(io["x"], g * TPC, TPC)).then_inc(s_x[u], 16)

            def store(g, b, j):
                for o in range(4):
                    u = o % 2
                    sp.wait_ge(s_qf_free, AHEAD + 4 * g + o + 1)
                    dst = qk_dram[o // 2].rearrange("s (b c) t -> c s b t", b=B)
                    sp.dma_start(dst[u * P:(u + 1) * P, :, bass.ds(b, 1), bass.ds(j * CH, CH)].squeeze(2),
                                 parts[u][:]).then_inc(s_parts[u], 16)

            load(0, 0)
            load(1, 1)
            with sp.Fori(0, NCH // 2 - 1) as i:
                for u in range(2):
                    sp.wait_ge(s_norm, 2 * i + u + 1)
                    load(2 * i + u + 2, u)
                    store(2 * i + u, i // 2, (i % 2) * 2 + u)
            for g in range(NCH - 2, NCH):
                store(g, g // CPB, g % CPB)

        def project_tensor(pe):
            pe.sem_inc(s_xn_free, AHEAD)
            pe.sem_inc(s_v, 1)

            def turn(g, u):
                pe.wait_ge(s_norm, g + 1)
                pe.wait_ge(s_hT, g)
                for k in range(HALF):
                    for t in range(TPC):
                        mm = pe.transpose(ps[:, k, t * P:(t + 1) * P], xn[u][:, t, k * P:(k + 1) * P], ident[:])
                mm.then_inc(s_xn_free, 1)

            def proj(g, u):
                pe.wait_ge(s_hT, g + 1)
                for o in range(4):
                    pe.wait_ge(s_qbank_free, 4 * g + o + 1)
                    for k in range(HALF):
                        mm = pe.matmul(ps[:, 2 + o % 2, :], wqkv[:, o // 2, k, (o % 2) * P:(o % 2 + 1) * P],
                                       hT[u][:, k, :], start=(k == 0), stop=(k == 1))
                    mm.then_inc(s_unit, 1)
                for t in range(TPC):
                    pe.wait_ge(s_vbank_free, TPC * g + t + 1)
                    for k in range(HALF):
                        mm = pe.matmul(ps[:, 4 + t % 2, 0:D], hT[u][:, k, t * P:(t + 1) * P], wqkv[:, 2, k, :],
                                       start=(k == 0), stop=(k == 1))
                    mm.then_inc(s_v, 1)

            pe.wait_ge(s_mod, 1)
            turn(0, 0)
            with pe.Fori(0, NCH // 2 - 1) as i:
                for u in range(2):
                    turn(2 * i + u + 1, 1 - u)
                    proj(2 * i + u, u)
            turn(NCH - 1, 1)
            proj(NCH - 2, 0)
            proj(NCH - 1, 1)

        def project_scalar(act):
            act.sem_inc(s_qbank_free, AHEAD)
            for u in range(2):
                act.sem_inc(s_parts[u], 16)
            act.wait_ge(s_mod, 1)

            def root(g):
                act.wait_ge(s_var, g + 1)
                act.activation(std[:], mv[:, :, 1], ACT.Sqrt, bias=eps[:, 0:1]).then_inc(s_std, 1)

            def modulate(g, u, b):
                act.wait_ge(s_xn_free, AHEAD + g + 1)
                for k in range(HALF):
                    a = act.activation(hT[u][:, k, :], ps[:, k, :], ACT.Identity,
                                       bias=colmod[:, 0, k, bass.ds(b, 1)], scale=colmod[:, 1, k, bass.ds(b, 1)])
                a.then_inc(s_hT, 1)

            def take(g):
                for o in range(4):
                    u, scale = o % 2, 0.25 if o < 2 else 1.0
                    act.wait_ge(s_unit, 4 * g + o + 1)
                    act.wait_ge(s_qf_free, 4 * g + o + 1)
                    act.activation(qf[u][:], ps[:, 2 + u, :], ACT.Identity, bias=bqk[:, o:o + 1], scale=scale)
                    act.wait_ge(s_parts[u], 16 * (2 * g + o // 2 + 1))
                    act.activation(parts[u][:, 0, :], ps[:, 2 + u, :], ACT.Identity, bias=bqk[:, o:o + 1],
                                   scale=scale).then_inc(s_qbank_free, 1)

            root(0)
            modulate(0, 0, 0)
            with act.Fori(0, NCH // 2 - 1) as i:
                for u in range(2):
                    root(2 * i + u + 1)
                    act.wait_ge(s_v, 1 + TPC * (2 * i + u))
                    modulate(2 * i + u + 1, 1 - u, (i * 2 + u + 1) // CPB)
                    take(2 * i + u)
            root(NCH - 1)
            act.wait_ge(s_v, 1 + TPC * (NCH - 2))
            modulate(NCH - 1, 1, B - 1)
            take(NCH - 2)
            take(NCH - 1)

        def project_vector(dve, step):
            dve.sem_inc(s_qf_free, AHEAD)
            dve.sem_inc(s_vbank_free, AHEAD)

            def norm(g, u, nth):
                dve.wait_ge(s_x[u], 16 * (nth + 1))
                for t in range(TPC):
                    st = dve.bn_stats(stats[:, t, :], x_t[u][:, t, :])
                step(st)
                hold(dve)
                for t in range(TPC):
                    a = dve.bn_aggr(mv[:, t, :], stats[:, t, :])
                a.then_inc(s_var, 1)
                dve.wait_ge(s_std, g + 1)
                step(dve.reciprocal(std[:], std[:]))
                dve.wait_ge(s_xn_free, g + 1)
                for t in range(TPC):
                    a = dve.tensor_scalar(xn[u][:, t, :], x_t[u][:, t, :], mv[:, t, 0:1], std[:, t:t + 1],
                                          ALU.subtract, ALU.mult)
                a.then_inc(s_norm, 1)

            def cut(g):
                for o in range(4):
                    u = o % 2
                    dve.wait_ge(s_qbank_free, AHEAD + 4 * g + o + 1)
                    step(dve.tensor_tensor(rest[u][:], qf[u][:], parts[u][:, 0, :], ALU.subtract))
                    step(dve.tensor_copy(parts[u][:, 1, :], rest[u][:]))
                    dve.tensor_tensor(parts[u][:, 2, :], rest[u][:], parts[u][:, 1, :],
                                      ALU.subtract).then_inc(s_qf_free, 1)
                for t in range(TPC):
                    dve.wait_ge(s_v, 1 + TPC * g + t + 1)
                    dve.tensor_tensor(v_all[:, bass.ds(TPC * g + t, 1), :].squeeze(1), ps[:, 4 + t % 2, 0:D],
                                      bv_row[:], ALU.add).then_inc(s_vbank_free, 1)

            norm(0, 0, 0)
            per = 2 * (2 + 8)
            with dve.Fori(0, NCH // 2 - 1) as i:
                step.turns(i, per)
                for u in range(2):
                    norm(2 * i + u + 1, 1 - u, i + u)
                    cut(2 * i + u)
            step.close(NCH // 2 - 1, per)
            norm(NCH - 1, 1, NCH // 2 - 1)
            cut(NCH - 2)
            cut(NCH - 1)

        num = lambda h: NB * h[0] + h[1]
        nth = lambda h: h[0] + h[1] // NB
        buf = lambda h: h[1] % NB
        plus = lambda h, k: (h[0], h[1] + k)
        half_bank = lambda h: slice(2 * h, 2 * h + 2)

        def attend_sync(sp):
            for u in range(2):
                sp.wait_ge(s_parts[u], 16 * (2 * NCH + 1))

            def stack(h):
                p = buf(h)
                for which, runs, tile in ((0, Q_RUNS, qs[p]), (1, K_RUNS, ks[p])):
                    for group, part, n in runs:
                        src = qk_dram[which]
                        if which == 0:
                            src = src[part:part + n]
                        else:
                            src = src[part:part + 1].to_broadcast([n, B * D, S])
                        sp.dma_start(tile[group * DH:(group + n) * DH, :],
                                     src[:, bass.ds(num(h) * DH, DH), :]).then_inc(s_stack[p], 16)

            def maxima(h):
                p = buf(h)
                sp.wait_ge(s_ring, MAXIMA * (num(h) + 1))
                for m in range(2):
                    sp.dma_start(qs[p][ROWS + m:ROWS + m + 1, :].rearrange("a (t c) -> a t c", t=KT),
                                 mb[p][:, m, :]).then_inc(s_mrows[p], 16)

            def head_store(h):
                sp.wait_ge(s_head, num(h) + 1)
                sp.dma_start(o_dram[bass.ds(num(h), 1)].squeeze(0), head_out[:]).then_inc(s_hstore, 16)

            def turn(h, last):
                if last >= 2:
                    sp.wait_ge(s_score, 2 * KT * num(h))
                    stack(plus(h, 2))
                head_store(plus(h, -1))
                if last >= 1:
                    maxima(plus(h, 1))

            for n in range(NB):
                stack((0, n))
            sp.wait_ge(s_mod, 1)
            sp.dma_start(xs_dram.rearrange("(n p) d -> p n d", p=P),
                         zero_row[:].unsqueeze(1).to_broadcast([P, NTILE, D])).then_inc(s_zero, 16)
            maxima((0, 0))
            maxima((0, 1))
            trips = (NH - 5) // NB
            with sp.Fori(0, trips) as i:
                for u in range(NB):
                    turn((i, 1 + u), 2)
            for n in range(1 + NB * trips, NH):
                turn((0, n), NH - 1 - n)
            head_store((0, NH - 1))

        def attend_tensor(pe):
            pe.sem_inc(s_prob_free, AHEAD)
            pe.wait_ge(s_ones, 1)
            pe.wait_ge(s_qbank_free, AHEAD + 4 * NCH)
            pe.wait_ge(s_vbank_free, AHEAD + NT)

            def unit(h, k):
                p, t, c = buf(h), k // CPB, k % CPB
                if k == 0:
                    pe.wait_ge(s_stack[p], 96 * (nth(h) + 1))
                if k < RING:
                    pe.wait_ge(s_ring, MAXIMA * num(h))
                else:
                    pe.wait_ge(s_ring, MAXIMA * num(h) + k - RING + 1)
                pe.matmul(ps[:, 4 + k % RING, :], qs[p][0:ROWS, t * P:(t + 1) * P],
                          ks[p][0:ROWS, c * CH:(c + 1) * CH], start=True, stop=True).then_inc(s_max, 1)

            def turn_maxima(h):
                pe.wait_ge(s_neg, num(h) + 1)
                pe.transpose(ps[0:KT, 4 + UNITS % RING, 0:P], mneg[:, :], ident[:]).then_inc(s_max, 1)

            def scores(h, kt, half):
                p = buf(h)
                if kt == 0 and half == 0:
                    pe.wait_ge(s_mrows[p], 32 * (nth(h) + 2))
                pe.wait_ge(s_exp_free, 2 * KT * num(h) + 2 * kt + half + 1)
                for c in range(2):
                    q = (2 * half + c) * CH
                    mm = pe.matmul(ps[:, 2 * half + c, :], ks[p][0:ROWS + 2, kt * P:(kt + 1) * P],
                                   qs[p][0:ROWS + 2, q:q + CH], start=True, stop=True)
                mm.then_inc(s_score, 1)

            def weigh(h, kt):
                if kt == 0:
                    pe.wait_ge(s_vs, num(h) + 1)
                    pe.wait_ge(s_head, num(h))
                pe.wait_ge(s_exp_free, AHEAD + 2 * KT * num(h) + 2 * kt + 2)
                for j in range(CPB):
                    mm = pe.matmul(ps[32 * j:32 * j + 32, 7, :], vs[buf(h)][:, kt, :],
                                   prob[:, kt % 2, j * CH:(j + 1) * CH], start=(kt == 0), stop=(kt == KT - 1))
                mm.then_inc(s_prob_free, 1)

            def turn(h, first=False, last=False):
                k = 0
                for kt in range(KT):
                    n = 0 if last else MAX_UNITS[kt]
                    scores(h, kt, 0)
                    for _ in range(n // 2):
                        unit(plus(h, 1), k)
                        k += 1
                    scores(h, kt, 1)
                    for _ in range(n - n // 2):
                        unit(plus(h, 1), k)
                        k += 1
                    if kt or not first:
                        weigh(*((h, kt - 1) if kt else (plus(h, -1), KT - 1)))
                    if kt == KT - 2 and not last:
                        turn_maxima(plus(h, 1))

            for k in range(UNITS):
                unit((0, 0), k)
            turn_maxima((0, 0))
            turn((0, 0), first=True)
            with pe.Fori(0, (NH - 2) // NB) as i:
                for u in range(NB):
                    turn((i, 1 + u))
            turn((0, NH - 1), last=True)
            weigh((0, NH - 1), KT - 1)

        def attend_vector(dve, step):
            def head(h):
                n = num(h)
                for k in range(UNITS):
                    dve.wait_ge(s_max, MAXIMA * n + k + 1)
                    dve.tensor_reduce(mx[:, k // CPB, k % CPB:k % CPB + 1], ps[:, 4 + k % RING, :], AX.X,
                                      ALU.max).then_inc(s_ring, 1)
                dve.wait_ge(s_ring, MAXIMA * n + UNITS)
                dve.tensor_reduce(mneg[:], mx[:], AX.X, ALU.max, negate=True).then_inc(s_neg, 1)
                dve.wait_ge(s_max, MAXIMA * n + UNITS + 1)
                dve.wait_ge(s_mrows[buf(h)], 32 * (nth(h) + 1))
                turned = ps[0:KT, 4 + UNITS % RING, 0:P]
                step(dve.tensor_copy(mb[buf(h)][:, 0, :], turned))
                dve.tensor_tensor(mb[buf(h)][:, 1, :], turned, mb[buf(h)][:, 0, :],
                                  ALU.subtract).then_inc(s_ring, 1)

            for p in range(NB):
                dve.sem_inc(s_mrows[p], 32)
            with dve.Fori(0, NH // NB) as i:
                step.turns(i, NB)
                for u in range(NB):
                    head((i, u))
            step.close(NH // NB, NB)
            for n in range(NH // NB * NB, NH):
                head((0, n))

        def attend_scalar(act):
            act.sem_inc(s_exp_free, AHEAD)
            act.sem_inc(s_hstore, 16)

            def exps(n, kt):
                act.wait_ge(s_prob_free, KT * n + kt + 1)
                for half in range(2):
                    act.wait_ge(s_score, 2 * KT * n + 2 * kt + half + 1)
                    act.activation(prob[:, kt % 2, half * 2 * CH:(half + 1) * 2 * CH],
                                   ps[:, half_bank(half), :].rearrange("p c n -> p (c n)"),
                                   ACT.Exp).then_inc(s_exp_free, 1)

            def head_copy(n):
                act.wait_ge(s_prob_free, AHEAD + KT * (n + 1))
                act.wait_ge(s_hstore, 16 * (n + 1))
                act.copy(head_out[:], ps[:, 7, :]).then_inc(s_head, 1)

            for kt in range(KT):
                exps(0, kt)
            with act.Fori(1, NH) as n:
                for kt in range(KT):
                    exps(n, kt)
                    if kt == 0:
                        head_copy(n - 1)
            head_copy(NH - 1)

        def attend_gpsimd(pool, step):
            for p in range(NB):
                step(pool.memset(ks[p][ROWS:ROWS + 2, :], 1.0))
                step(pool.memset(vs[p][:], 0.0))
                step(pool.memset(vs[p][:, :, DH:DH + 1], 1.0))
            pool.sem_inc(s_ones, 1)
            pool.wait_ge(s_vbank_free, AHEAD + NT)

            def stage(h):
                n = num(h)
                pool.tensor_copy(vs[buf(h)][:, :, 0:DH],
                                 v_all[:, bass.ds(n // H * KT, KT), bass.ds(n % H * DH, DH)]).then_inc(s_vs, 1)

            for n in range(NB):
                stage((0, n))
            for u in range(2):
                pool.wait_ge(s_parts[u], 16 * (2 * NCH + 1))
            for dst, name in ((rgT, "rgT"), (ruT, "ruT"), (rdT, "rdT")):
                pool.dma_start(dst[:], io[name]).then_inc(s_expert, 16)
            with pool.Fori(0, NH // NB - 1) as i:
                for u in range(NB):
                    pool.wait_ge(s_prob_free, AHEAD + KT * (NB * i + u + 1))
                    stage((i, NB + u))
            for n in range(NH // NB * NB, NH):
                pool.wait_ge(s_prob_free, AHEAD + KT * (n - NB + 1))
                stage((0, n))

        def merge_sync(sp):
            sp.wait_ge(s_hstore, 16 * (NH + 1))

            def load(g, u, b, j):
                for k in range(HALF):
                    heads = o_dram[bass.ds(b * H + k * (H // HALF), H // HALF)]
                    rows_of = heads[:, bass.ds(32 * j, 32), :]
                    sp.dma_start(o_in[u][:, k, :], rows_of[:, 0:DH, :]).then_inc(s_oin[u], 16)
                    sp.dma_start(l_in[u][:, k, :], rows_of[:, DH:DH + 1, :].to_broadcast(
                        [H // HALF, DH, CH])).then_inc(s_oin[u], 16)
                sp.dma_start(x_in[u][:], rows(io["x"], g * TPC, TPC)).then_inc(s_oin[u], 16)

            def store(g, u):
                sp.wait_ge(s_x1, g + 1)
                sp.dma_start(rows(x1_dram, g * TPC, TPC), x1[u][:]).then_inc(s_x1st[u], 16)
                sp.wait_ge(s_h2, g + 1)
                sp.dma_start(rows(h2_dram, g * TPC, TPC), h2[u][:]).then_inc(s_h2st[u], 16)

            load(0, 0, 0, 0)
            load(1, 1, 0, 1)
            with sp.Fori(0, NCH // 2 - 1) as i:
                for u in range(2):
                    sp.wait_ge(s_x1, 2 * i + u + 1)
                    load(2 * i + u + 2, u, (i + 1) // 2, (i + 1) % 2 * 2 + u)
                    store(2 * i + u, u)
            store(NCH - 2, 0)
            store(NCH - 1, 1)

        def merge_tensor(pe):
            pe.sem_inc(s_h2_free, AHEAD)
            pe.wait_ge(s_exp_free, AHEAD + 2 * KT * NH)
            pe.wait_ge(s_ring, MAXIMA * NH)

            def out_proj(g, u):
                pe.wait_ge(s_on, g + 1)
                pe.wait_ge(s_x1, g)
                for t in range(TPC):
                    for k in range(HALF):
                        mm = pe.matmul(ps[:, t // 2, t % 2 * D:(t % 2 + 1) * D], o_in[u][:, k, t * P:(t + 1) * P],
                                       woT[:, k, :], start=(k == 0), stop=(k == 1))
                mm.then_inc(s_op, 1)

            def turn(g, u):
                pe.wait_ge(s_h2, g + 1)
                pe.wait_ge(s_h2T, g + 1)
                for k in range(HALF):
                    for t in range(TPC):
                        mm = pe.transpose(ps[:, 2 + k, t * P:(t + 1) * P], h2[u][:, t, k * P:(k + 1) * P], ident[:])
                mm.then_inc(s_h2_free, 1)
                pe.wait_ge(s_h2T, g + 2)
                pe.wait_ge(s_lg, g + 1)
                for t in range(TPC):
                    for k in range(HALF):
                        mm = pe.matmul(ps[:, 4, t * E:(t + 1) * E], h2Tc[u][:, k, t * P:(t + 1) * P],
                                       gateT[:, k, :], start=(k == 0), stop=(k == 1))
                mm.then_inc(s_lgp, 1)

            out_proj(0, 0)
            with pe.Fori(0, NCH // 2 - 1) as i:
                for u in range(2):
                    out_proj(2 * i + u + 1, 1 - u)
                    turn(2 * i + u, u)
            out_proj(NCH - 1, 1)
            turn(NCH - 2, 0)
            turn(NCH - 1, 1)

        def merge_vector(dve, step):
            def divide(g, u, nth):
                dve.wait_ge(s_oin[u], 80 * (nth + 1))
                step(dve.reciprocal(l_in[u][:], l_in[u][:]))
                dve.tensor_tensor(o_in[u][:], o_in[u][:], l_in[u][:], ALU.mult).then_inc(s_on, 1)

            def residual(g, u, nth, b):
                dve.wait_ge(s_op, g + 1)
                dve.wait_ge(s_x1st[u], 16 * (nth + 1))
                step(dve.tensor_tensor(x1[u][:], ps[:, 0:2, :].rearrange("p c (t d) -> p (c t) d", d=D),
                                       rowmod[:, bass.ds(b, 1), 0, :].to_broadcast([P, TPC, D]), ALU.mult))
                dve.wait_ge(s_xb, g + 1)
                dve.tensor_tensor(x1[u][:], x1[u][:], x_in[u][:], ALU.add).then_inc(s_x1, 1)
                dve.wait_ge(s_x1, g + 1)
                for t in range(TPC):
                    st = dve.bn_stats(stats2[:, t, :], x1[u][:, t, :])
                step(st)
                hold(dve)
                for t in range(TPC):
                    a = dve.bn_aggr(mv2[:, t, :], stats2[:, t, :])
                a.then_inc(s_var2, 1)
                dve.wait_ge(s_std2, g + 1)
                step(dve.reciprocal(std2[:], std2[:]))
                dve.wait_ge(s_h2_free, g + 1)
                dve.wait_ge(s_h2st[u], 16 * (nth + 1))
                for t in range(TPC):
                    a = dve.tensor_scalar(h2[u][:, t, :], x1[u][:, t, :], mv2[:, t, 0:1], std2[:, t:t + 1],
                                          ALU.subtract, ALU.mult)
                a.then_inc(s_n2, 1)

            for u in range(2):
                dve.sem_inc(s_x1st[u], 16)
                dve.sem_inc(s_h2st[u], 16)
            divide(0, 0, 0)
            per = 2 * 4
            with dve.Fori(0, NCH // 2 - 1) as i:
                step.turns(i, per)
                for u in range(2):
                    divide(2 * i + u + 1, 1 - u, i + u)
                    residual(2 * i + u, u, i, i // 2)
            step.close(NCH // 2 - 1, per)
            divide(NCH - 1, 1, NCH // 2 - 1)
            residual(NCH - 2, 0, NCH // 2 - 1, B - 1)
            residual(NCH - 1, 1, NCH // 2 - 1, B - 1)

        def merge_gpsimd(pool, step):
            def bias(g, u, nth, b):
                pool.wait_ge(s_oin[u], 80 * (nth + 1))
                hold(pool)
                pool.tensor_tensor(x_in[u][:], x_in[u][:], gbo[:, bass.ds(b, 1), :].to_broadcast([P, TPC, D]),
                                   ALU.add).then_inc(s_xb, 1)

            def modulate(g, u, b):
                pool.wait_ge(s_n2, g + 1)
                hold(pool)
                step(pool.tensor_tensor(h2[u][:], h2[u][:], rowmod[:, bass.ds(b, 1), 2, :].to_broadcast(
                    [P, TPC, D]), ALU.mult))
                hold(pool)
                pool.tensor_tensor(h2[u][:], h2[u][:], rowmod[:, bass.ds(b, 1), 1, :].to_broadcast(
                    [P, TPC, D]), ALU.add).then_inc(s_h2, 1)

            bias(0, 0, 0, 0)
            with pool.Fori(0, NCH // 2 - 1) as i:
                step.turns(i, 2)
                for u in range(2):
                    bias(2 * i + u + 1, 1 - u, i + u, (2 * i + u + 1) // CPB)
                    modulate(2 * i + u, u, i // 2)
            step.close(NCH // 2 - 1, 2)
            bias(NCH - 1, 1, NCH // 2 - 1, B - 1)
            modulate(NCH - 2, 0, B - 1)
            modulate(NCH - 1, 1, B - 1)

        def merge_scalar(act):
            act.sem_inc(s_h2T, 1)
            act.sem_inc(s_lg, 1)
            with act.Fori(0, NCH // 2) as i:
                for u in range(2):
                    g = 2 * i + u
                    act.wait_ge(s_var2, g + 1)
                    act.activation(std2[:], mv2[:, :, 1], ACT.Sqrt, bias=eps[:, 0:1]).then_inc(s_std2, 1)
                    act.wait_ge(s_h2_free, AHEAD + g + 1)
                    for k in range(HALF):
                        act.copy(h2T[:, k, bass.ds(g * CH, CH)], ps[:, 2 + k, :])
                        a = act.copy(h2Tc[u][:, k, :], ps[:, 2 + k, :])
                    a.then_inc(s_h2T, 1)
                    act.wait_ge(s_lgp, g + 1)
                    act.copy(logits[:, bass.ds(TPC * g, TPC), :].rearrange("p t e -> p (t e)"),
                             ps[:, 4, 0:TPC * E]).then_inc(s_lg, 1)

        def route_vector(dve, step):
            by_tile = lambda a: a.unsqueeze(2).to_broadcast([P, NT, E])
            by_expert = lambda a: a.unsqueeze(1).to_broadcast([P, NT, E])
            less8, firsts, count40 = iotas[:, 0:E], iotas[:, E:E + NT], iotas[:, E + NT:E + NT + 40]
            dve.wait_ge(s_lg, NCH + 1)
            for u in range(2):
                dve.wait_ge(s_x1st[u], 16 * (NCH // 2 + 1))
                dve.wait_ge(s_h2st[u], 16 * (NCH // 2 + 1))
            step(dve.tensor_reduce(rmax[:], logits[:], AX.X, ALU.max))
            step(dve.tensor_tensor(rt[:], logits[:], by_tile(rmax[:]), ALU.is_ge))
            step(dve.tensor_tensor(rt[:], rt[:], by_expert(less8), ALU.mult))
            step(dve.tensor_reduce(rix[:], rt[:], AX.X, ALU.min))
            dve.tensor_tensor(onehot[:], by_expert(less8), by_tile(rix[:]), ALU.is_equal).then_inc(s_oh, 1)
            dve.wait_ge(s_rank, 1)
            in_tile = ps[:, 0, 0:NT * E].rearrange("p (t e) -> p t e", e=E)
            totals = ps[:, 1, 0:NT * E].rearrange("p (t e) -> p t e", e=E)
            a, b = ra, rb
            step(dve.tensor_copy(a[:], totals))
            for s in (1, 2, 4, 8, 16):
                dve.tensor_copy(b[:, 0:s, :], a[:, 0:s, :])
                step(dve.tensor_tensor(b[:, s:, :], a[:, s:, :], a[:, :NT - s, :], ALU.add))
                a, b = b, a
            step(dve.tensor_tensor(cmp8[:], a[:, NT - 1, :].unsqueeze(2).to_broadcast([P, E, NT]),
                                   firsts.unsqueeze(1).to_broadcast([P, E, NT]), ALU.is_gt))
            need, p, q, at = (segs[:, k, :] for k in range(4))
            step(dve.tensor_reduce(need, cmp8[:], AX.X, ALU.add))
            step(dve.tensor_copy(p, need))
            for s in (1, 2, 4):
                dve.tensor_copy(q[:, 0:s], p[:, 0:s])
                step(dve.tensor_tensor(q[:, s:], p[:, s:], p[:, :E - s], ALU.add))
                p, q = q, p
            step(dve.tensor_tensor(at, p, need, ALU.subtract))
            step(dve.tensor_scalar(at, at, float(P), None, ALU.mult))
            step(dve.tensor_tensor(rt[:], a[:], totals, ALU.subtract))
            step(dve.tensor_tensor(rt[:], rt[:], in_tile, ALU.add))
            step(dve.tensor_tensor(rt[:], rt[:], by_expert(at), ALU.add))
            step(dve.tensor_tensor(rt[:], rt[:], onehot[:], ALU.mult))
            step(dve.tensor_reduce(rix[:], rt[:], AX.X, ALU.add))
            dve.tensor_copy(slot[:], rix[:])
            step(dve.tensor_tensor(tcmp[:], count40.unsqueeze(2).to_broadcast([P, 40, E]),
                                   p.unsqueeze(1).to_broadcast([P, 40, E]), ALU.is_ge))
            step(dve.tensor_reduce(tile_f[:], tcmp[:], AX.X, ALU.add))
            dve.tensor_scalar(tile_e[:], tile_f[:], float(E - 1), None, ALU.min).then_inc(s_route, 1)

        def route_tensor(pe):
            pe.wait_ge(s_oh, 1)
            pe.matmul(ps[:, 0, 0:NT * E], before[:], onehot[:].rearrange("p t e -> p (t e)"), start=True, stop=True)
            pe.matmul(ps[:, 1, 0:NT * E], ones[:], onehot[:].rearrange("p t e -> p (t e)"),
                      start=True, stop=True).then_inc(s_rank, 1)

        def route_scalar(act):
            act.wait_ge(s_oh, 1)
            act.activation(score[:], rmax[:], ACT.Sigmoid).then_inc(s_sig, 1)

        def shared_sync(sp):
            sp.wait_ge(s_route, 1)
            for u in range(2):
                sp.wait_ge(s_h2st[u], 16 * (NCH // 2 + 1))
                sp.wait_ge(s_x1st[u], 16 * (NCH // 2 + 1))

            def load(g, u):
                sp.dma_start(xr[u][:], rows(x1_dram, g * TPC, TPC)).then_inc(s_xr[u], 16)

            def token_rows(t, u):
                sp.wait_ge(s_scx_free, t + 1)
                sp.dma_start(sc_x[u][:], h2_dram[bass.ds(t * P, P), :]).then_inc(s_scx[u], 16)

            load(0, 0)
            load(1, 1)
            with sp.Fori(0, NT // 2) as i:
                for u in range(2):
                    token_rows(2 * i + u, u)
            with sp.Fori(0, NCH // 2 - 1) as i:
                for u in range(2):
                    g = 2 * i + u
                    sp.wait_ge(s_x2, g + 2)
                    sp.dma_start(rows(x2_dram, g * TPC, TPC), xr[u][:]).then_inc(s_x2st[u], 16)
                    sp.wait_ge(s_x2st[u], 16 * (i + 1))
                    load(g + 2, u)
            for u in range(2):
                g = NCH - 2 + u
                sp.wait_ge(s_x2, g + 2)
                sp.dma_start(rows(x2_dram, g * TPC, TPC), xr[u][:]).then_inc(s_x2st[u], 16)

        def scatter_gpsimd(pool, step):
            pool.sem_inc(s_scx_free, AHEAD)
            pool.wait_ge(s_route, 1)
            pool.wait_ge(s_sig, 1)
            pool.wait_ge(s_zero, 16)

            def scatter(i, u):
                t = 2 * i + u
                pool.wait_ge(s_scx[u], 16 * (i + 1))
                wait(pool, s_scat[u], 16 * i)
                hold(pool)
                pool.tensor_copy(sc_ix[u][:], slot[:, bass.ds(t, 1)])
                step(pool.tensor_copy(sc_s[u][:], score[:, bass.ds(t, 1)]))
                hold(pool)
                pool.tensor_scalar(sc_in[u][:], sc_x[u][:], sc_s[u][:, 0:1], None,
                                   ALU.mult).then_inc(s_scx_free, 1)
                pool.wait_ge(s_scx_free, AHEAD + t + 1)
                hold(pool)
                pool.indirect_dma_start(xs_dram, bass.IndirectOffsetOnAxis(sc_ix[u][:, 0:1], 0), sc_in[u][:],
                                        None).then_inc(s_scat[u], 16)

            for u in range(2):
                scatter(0, u)
            with pool.Fori(1, NT // 2) as i:
                step.turns(i - 1, 2)
                for u in range(2):
                    scatter(i, u)
            step.close(NT // 2 - 1, 2)

        def shared_tensor(pe):
            pe.wait_ge(s_shared, 48)
            pe.sem_inc(s_gu_free, AHEAD)
            pe.wait_ge(s_lg, NCH + 1)

            def gate_up(g):
                for fc in range(FC):
                    pe.wait_ge(s_gu_free, FC * g + fc + 1)
                    for w, bank in ((wgT, 2 + 2 * (fc % 2)), (wuT, 3 + 2 * (fc % 2))):
                        for k in range(HALF):
                            mm = pe.matmul(ps[:, bank, :], w[:, k, fc * P:(fc + 1) * P],
                                           h2T[:, k, bass.ds(g * CH, CH)], start=(k == 0), stop=(k == 1))
                    mm.then_inc(s_gu, 1)

            def down(g, u):
                pe.wait_ge(s_gu_free, AHEAD + FC * (g + 1))
                pe.wait_ge(s_x2, g + 1)
                for t in range(TPC):
                    for fc in range(FC):
                        mm = pe.matmul(ps[:, 6 + t // 2, t % 2 * D:(t % 2 + 1) * D], hid[u][:, fc, t * P:(t + 1) * P],
                                       wdT[:, fc, :], start=(fc == 0), stop=(fc == FC - 1))
                mm.then_inc(s_y, 1)

            gate_up(0)
            with pe.Fori(0, NCH // 2 - 1) as i:
                for u in range(2):
                    gate_up(2 * i + u + 1)
                    down(2 * i + u, u)
            gate_up(NCH - 1)
            down(NCH - 2, 0)
            down(NCH - 1, 1)

        def shared_scalar(act):
            act.wait_ge(s_route, 1)
            with act.Fori(0, NCH) as g:
                for fc in range(FC):
                    u = fc % 2
                    act.wait_ge(s_gu, FC * g + fc + 1)
                    act.wait_ge(s_gu_free, FC * g + fc + 1)
                    act.activation(sgate[u][:], ps[:, 2 + 2 * u, :], ACT.Silu).then_inc(s_silu, 1)

        def shared_vector(dve, step):
            def hidden(g, u):
                for fc in range(FC):
                    dve.wait_ge(s_silu, FC * g + fc + 1)
                    if fc == 0:
                        wait(dve, s_y, g - 1)
                    dve.tensor_tensor(hid[u][:, fc, :], sgate[fc % 2][:], ps[:, 3 + 2 * (fc % 2), :],
                                      ALU.mult).then_inc(s_gu_free, 1)

            def residual(g, u, nth, b):
                dve.wait_ge(s_y, g + 1)
                step(dve.tensor_tensor(ymod[:], ps[:, 6:8, :].rearrange("p c (t d) -> p (c t) d", d=D),
                                       rowmod[:, bass.ds(b, 1), 3, :].to_broadcast([P, TPC, D]), ALU.mult))
                dve.wait_ge(s_xr[u], 16 * (nth + 1))
                dve.tensor_tensor(xr[u][:], xr[u][:], ymod[:], ALU.add).then_inc(s_x2, 1)
                dve.wait_ge(s_x2, g + 2)

            dve.sem_inc(s_x2, 1)
            hidden(0, 0)
            hidden(1, 1)
            with dve.Fori(0, NCH // 2 - 1) as i:
                step.turns(i, 2)
                for u in range(2):
                    residual(2 * i + u, u, i, i // 2)
                    hidden(2 * i + u + 2, u)
            step.close(NCH // 2 - 1, 2)
            residual(NCH - 2, 0, NCH // 2 - 1, B - 1)
            residual(NCH - 1, 1, NCH // 2 - 1, B - 1)

        LAST = NTILE - 3

        def routed_sync(sp):
            for u in range(2):
                sp.wait_ge(s_scat[u], 16 * (NT // 2))
            sp.wait_ge(s_y, NCH)

            def load(k, u):
                sp.wait_ge(s_xs_free, k + 1)
                sp.dma_start(xs[u][:], xs_dram[bass.ds(k * P, P), :]).then_inc(s_xs[u], 16)

            def store(k, u):
                sp.wait_ge(s_eout, k + 2)
                sp.dma_start(ys_dram[bass.ds(k * P, P), :], eout[u][:]).then_inc(s_est[u], 16)

            load(0, 0)
            load(1, 1)
            load(2, 0)
            with sp.Fori(0, LAST // 2) as i:
                for u in range(2):
                    load(2 * i + u + 3, 1 - u)
                    store(2 * i + u, u)
            for k in range(LAST, NTILE):
                store(k, k % 2)

        def routed_tensor(pe):
            pe.sem_inc(s_xs_free, AHEAD)
            pe.wait_ge(s_x2, NCH + 1)
            pe.wait_ge(s_expert, 48)

            def turn_in(k, u, nth):
                pe.wait_ge(s_xs[u], 16 * (nth + 1))
                pe.wait_ge(s_xsT, k)
                for c in range(HALF):
                    mm = pe.transpose(ps[:, 0, c * P:(c + 1) * P], xs[u][:, c * P:(c + 1) * P], ident[:])
                mm.then_inc(s_xs_free, 1)

            def gate_up(k, u):
                e = pe.value_load(tile_e[0:1, bass.ds(k, 1)], min_val=0, max_val=E - 1)
                pe.wait_ge(s_xsT, k + 1)
                wait(pe, s_ehid, k)
                for w, bank in ((rgT, 1 + 2 * u), (ruT, 2 + 2 * u)):
                    for c in range(HALF):
                        mm = pe.matmul(ps[:, bank, :], xsT[u][:, c, :], w[:, bass.ds(e, 1), c, :].squeeze(1),
                                       start=(c == 0), stop=(c == 1))
                mm.then_inc(s_egu, 1)
                return e

            def turn_hidden(k, u):
                pe.wait_ge(s_ehid, k + 2)
                pe.wait_ge(s_ehT, k + 1)
                for c in range(FC):
                    mm = pe.transpose(ps[:, 5, c * P:(c + 1) * P], ehid[u][:, c * P:(c + 1) * P], ident[:])
                mm.then_inc(s_ehTp, 1)

            def down(k, u):
                e = pe.value_load(tile_e[0:1, bass.ds(k, 1)], min_val=0, max_val=E - 1)
                pe.wait_ge(s_ehT, k + 2)
                pe.wait_ge(s_eout, k + 1)
                for c in range(FC):
                    mm = pe.matmul(ps[:, 6, 0:D], ehT[u][:, c, :], rdT[:, bass.ds(e, 1), c, :].squeeze(1),
                                   start=(c == 0), stop=(c == FC - 1))
                mm.then_inc(s_ey, 1)

            turn_in(0, 0, 0)
            gate_up(0, 0)
            turn_in(1, 1, 0)
            with pe.Fori(0, LAST // 2) as i:
                for u in range(2):
                    gate_up(2 * i + u + 1, 1 - u)
                    turn_hidden(2 * i + u, u)
                    turn_in(2 * i + u + 2, u, i + 1)
                    down(2 * i + u, u)
            for k in range(LAST, NTILE):
                if k + 1 < NTILE:
                    gate_up(k + 1, (k + 1) % 2)
                turn_hidden(k, k % 2)
                if k + 2 < NTILE:
                    turn_in(k + 2, k % 2, (k + 2) // 2)
                down(k, k % 2)

        def routed_scalar(act):
            def silu(k, u):
                act.wait_ge(s_egu, k + 1)
                wait(act, s_ehid, k)
                act.activation(esig[u][:], ps[:, 1 + 2 * u, :], ACT.Silu).then_inc(s_esig, 1)

            def take(k, u):
                act.wait_ge(s_ehTp, k + 1)
                wait(act, s_ey, k - 1)
                act.copy(ehT[u][:].rearrange("p c n -> p (c n)"), ps[:, 5, :]).then_inc(s_ehT, 1)

            act.sem_inc(s_ehT, 1)
            silu(0, 0)
            silu(1, 1)
            take(0, 0)
            silu(2, 0)
            take(1, 1)
            with act.Fori(1, LAST // 2) as i:
                for u in range(2):
                    silu(2 * i + u + 1, 1 - u)
                    take(2 * i + u, u)
            for k in range(LAST, NTILE):
                if k + 1 < NTILE:
                    silu(k + 1, (k + 1) % 2)
                take(k, k % 2)

        def routed_vector(dve):
            dve.wait_ge(s_x2, NCH + 1)
            dve.sem_inc(s_ehid, 1)
            dve.sem_inc(s_eout, 1)

            def rows_in(k, u):
                dve.wait_ge(s_xs_free, AHEAD + k + 1)
                wait(dve, s_egu, k - 1)
                dve.tensor_copy(xsT[u][:].rearrange("p c n -> p (c n)"), ps[:, 0, 0:D]).then_inc(s_xsT, 1)

            def hidden(k, u):
                dve.wait_ge(s_esig, k + 1)
                wait(dve, s_ehTp, k - 1)
                dve.tensor_tensor(ehid[u][:], esig[u][:], ps[:, 2 + 2 * u, :], ALU.mult).then_inc(s_ehid, 1)

            def take(k, u, nth):
                dve.wait_ge(s_ey, k + 1)
                dve.wait_ge(s_est[u], 16 * nth)
                dve.tensor_copy(eout[u][:], ps[:, 6, 0:D]).then_inc(s_eout, 1)

            rows_in(0, 0)
            rows_in(1, 1)
            hidden(0, 0)
            hidden(1, 1)
            rows_in(2, 0)
            take(0, 0, 0)
            hidden(2, 0)
            rows_in(3, 1)
            take(1, 1, 0)
            with dve.Fori(1, LAST // 2) as i:
                for u in range(2):
                    hidden(2 * i + u + 1, 1 - u)
                    rows_in(2 * i + u + 2, u)
                    take(2 * i + u, u, i)
            for k in range(LAST, NTILE):
                if k + 1 < NTILE:
                    hidden(k + 1, (k + 1) % 2)
                if k + 2 < NTILE:
                    rows_in(k + 2, k % 2)
                take(k, k % 2, k // 2)

        def combine_sync(sp):
            for u in range(2):
                sp.wait_ge(s_x2st[u], 16 * NCH // 2)

            def load(i, u):
                sp.dma_start(cx[u][:], x2_dram[bass.ds((NG * i + u) * P, P), :]).then_inc(s_cx[u], 16)

            def store(i, u):
                sp.wait_ge(s_out, NG + NG * i + u + 1)
                sp.dma_start(out[bass.ds((NG * i + u) * P, P), :], cx[u][:]).then_inc(s_ost[u], 16)

            for u in range(NG):
                load(0, u)
            with sp.Fori(1, NT // NG) as i:
                for u in range(NG):
                    store(i - 1, u)
                for u in range(NG):
                    sp.wait_ge(s_ost[u], 16 * i)
                    load(i, u)
            for u in range(NG):
                store(NT // NG - 1, u)
            for u in range(NG):
                sp.wait_ge(s_ost[u], 16 * (NT // NG))
                sp.wait_ge(s_est[u % 2], 16 * ((NTILE + 1 - u % 2) // 2))

        def combine_gpsimd(pool, step):
            for u in range(2):
                pool.wait_ge(s_est[u], 16 * ((NTILE + 1 - u) // 2))
            with pool.Fori(0, NT // NG) as i:
                step.turns(i, NG)
                for u in range(NG):
                    pool.wait_ge(s_out, NG * i + u + 1)
                    step(pool.tensor_copy(cix[u][:], slot[:, bass.ds(NG * i + u, 1)]))
                    hold(pool)
                    pool.indirect_dma_start(cy[u][:], None, ys_dram,
                                            bass.IndirectOffsetOnAxis(cix[u][:, 0:1], 0)).then_inc(s_cy[u], 16)
            step.close(NT // NG, NG)

        def combine_vector(dve, step):
            dve.sem_inc(s_out, NG)
            with dve.Fori(0, NT // NG) as i:
                step.turns(i, NG)
                for u in range(NG):
                    dve.wait_ge(s_cy[u], 16 * (i + 1))
                    step(dve.tensor_tensor(cy[u][:], cy[u][:], rowmod[:, bass.ds(i // (NT // NG // B), 1), 3, :]
                                           .squeeze(1), ALU.mult))
                    dve.wait_ge(s_cx[u], 16 * (i + 1))
                    dve.tensor_tensor(cx[u][:], cx[u][:], cy[u][:], ALU.add).then_inc(s_out, 1)
            step.close(NT // NG, NG)

        @block.sync
        def _(sp):
            setup_sync(sp)
            project_sync(sp)
            attend_sync(sp)
            merge_sync(sp)
            shared_sync(sp)
            routed_sync(sp)
            combine_sync(sp)

        @block.tensor
        def _(pe):
            setup_tensor(pe)
            project_tensor(pe)
            attend_tensor(pe)
            merge_tensor(pe)
            route_tensor(pe)
            shared_tensor(pe)
            routed_tensor(pe)

        @block.scalar
        def _(act):
            setup_scalar(act)
            project_scalar(act)
            attend_scalar(act)
            merge_scalar(act)
            route_scalar(act)
            shared_scalar(act)
            routed_scalar(act)

        @block.vector
        def _(dve):
            step = Steps(dve, s_chain["dve"])
            setup_vector(dve, step)
            project_vector(dve, step)
            attend_vector(dve, step)
            merge_vector(dve, step)
            route_vector(dve, step)
            shared_vector(dve, step)
            routed_vector(dve)
            combine_vector(dve, step)

        @block.gpsimd
        def _(pool):
            step = Steps(pool, s_chain["pool"])
            attend_gpsimd(pool, step)
            merge_gpsimd(pool, step)
            scatter_gpsimd(pool, step)
            combine_gpsimd(pool, step)


def laid_out(a):
    def by_rows(w):
        return w.T.reshape(-1, P, w.shape[0]).transpose(1, 0, 2)

    def experts(w):
        return w.transpose(2, 0, 1).reshape(-1, P, E, w.shape[1]).transpose(1, 2, 0, 3)

    names = ("q", "k", "v", "o")
    at = lambda n: a["L0_attn_" + n]
    ffn = lambda n: a["L0_ffn_" + n]
    return {
        "x": at("x").reshape(T, D),
        "cT": a["L0_c"].T.reshape(HALF, P, B).transpose(1, 0, 2),
        "wmod": a["L0_wmod"].reshape(HALF, P, 6 * D).transpose(1, 0, 2),
        "loA": np.stack([at("A" + n) for n in names], 1),
        "loB": np.stack([at("B" + n).T for n in names], 1),
        "wT": np.stack([by_rows(at("W" + n)) for n in names], 1),
        "bqk": np.concatenate([at("bq").reshape(HALF, P), at("bk").reshape(HALF, P)]).T,
        "bv": at("bv"),
        "bo": at("bo"),
        "gateT": by_rows(ffn("gate_w")),
        "wgT": by_rows(ffn("shared_gate")),
        "wuT": by_rows(ffn("shared_up")),
        "wdT": by_rows(ffn("shared_down")),
        "rgT": experts(ffn("r_gate")),
        "ruT": experts(ffn("r_up")),
        "rdT": experts(ffn("r_down")),
        "ident": np.eye(P, dtype=np.float32),
        "before": np.triu(np.ones((P, P), np.float32), 1),
        "iotas": np.tile(np.concatenate([np.arange(E) - E, P * np.arange(NT), np.arange(40)]), (P, 1)).astype(np.float32),
    }


def kernel(**inputs):
    import concourse.bacc as bacc
    from concourse.bass_utils import run_bass_kernel_spmd

    nc = bacc.Bacc("TRN2", target_bir_lowering=False, num_devices=1)
    arrays, io = {}, {}
    for name, a in laid_out({k: np.asarray(v) for k, v in inputs.items()}).items():
        a = np.ascontiguousarray(a)
        arrays["in_" + name] = a
        io[name] = nc.dram_tensor("in_" + name, a.shape, mybir.dt.from_np(a.dtype), kind="ExternalInput").ap()
    out = nc.dram_tensor("out", (T, D), F32, kind="ExternalOutput").ap()
    block_kernel(nc, io, out)
    got = run_bass_kernel_spmd(nc, [arrays], core_ids=[0]).results[0]["out"]
    return got.reshape(B, S, D)
```

```python
from contextlib import ExitStack

import numpy as np

import concourse.bass as bass
from concourse import mybir

F32 = mybir.dt.float32
BF16 = mybir.dt.bfloat16
U32 = mybir.dt.uint32
ALU = mybir.AluOpType
ACT = mybir.ActivationFunctionType
AX = mybir.AxisListType

P = 128
B, S, D = 2, 2048, 256
H, DH = 16, 16
R = 8
LORA_SCALE = 2.0
F, E = 512, 8
T = B * S
HALF = D // P
FC = F // P
CH = 512
NCH = T // CH
CPB = S // CH
TPC = CH // P
NT = T // P
KT = S // P
NH = B * H
ROWS = 6 * DH
NTILE = NT + E - 1
NSLOT = NTILE * P
ZERO = 3
EPS = 1e-5
AHEAD = 2
Q_RUNS = ((0, 0, 3), (3, 0, 2), (5, 0, 1))
K_RUNS = ((0, 0, 3), (3, 1, 2), (5, 2, 1))
UNITS = KT * CPB
LEAD = 4 * CPB
UQ = 2 * D // P
XW = D + 1
MAXIMA = UNITS + 1
RING = 3
NSC = 4
NG = 8
NB = 3


def wait(eng, semaphore, n):
    if not isinstance(n, int) or n > 0:
        eng.wait_ge(semaphore, n)


class Region:

    def __init__(self, nc, start, end):
        self.nc, self.at, self.end = nc, start, end

    def __call__(self, name, shape, dt=F32):
        size = int(np.prod(shape[1:])) * (2 if dt == BF16 else 4)
        t = self.nc.alloc_sbuf_tensor_at(name, shape, dt, offset=self.at)
        self.at += -(-size // 32) * 32
        assert self.at <= self.end, name
        return t


class Steps:

    def __init__(self, eng, sem):
        self.eng, self.sem, self.count, self.loop = eng, sem, 0, None

    def __call__(self, ins):
        ins.then_inc(self.sem, 1)
        self.count += 1
        self.eng.wait_ge(self.sem, self.count if self.loop is None else self.loop + self.count)

    def turns(self, index, per):
        self.loop, self.first = index * per, self.count

    def close(self, trips, per):
        assert self.count == self.first + per, (self.count, self.first, per)
        self.count, self.loop = self.first + trips * per, None


def buffers(name, shape, dt, region, n=2):
    return [region(f"{name}{i}", shape, dt) for i in range(n)]


def block_kernel(nc, io, out):
    with ExitStack() as ctx:
        names = {}

        def sem(name):
            names[name] = ctx.enter_context(nc.semaphore(name))
            return names[name]

        ps = ctx.enter_context(nc.psum_tensor("ps", [P, 8, 512], F32))

        def scratch(name, shape, dt=F32):
            return nc.dram_tensor(name, shape, dt, kind="Internal").ap()

        qk_dram = scratch("qk_parts", (2, 3, B * D, S), BF16)
        o_dram = scratch("head_out", (NH, P, CH))
        rl_dram = scratch("inverse_sums", (NH * CPB, CH))
        h2_dram = scratch("h2_rows", (T, D))
        x1_dram = scratch("x1_rows", (T, D))
        x2_dram = scratch("x2_rows", (T, D))
        xs_dram = scratch("sorted_in", (NSLOT, XW))
        ys_dram = scratch("sorted_out", (NSLOT, D))

        top = nc.sbuf_usable_end // 32 * 32
        expert_bytes = E * 4 * (2 * HALF * F + FC * D)
        experts_at = top - expert_bytes
        held = Region(nc, -(-nc.sbuf_base // 32) * 32, experts_at)
        ident = held("ident", [P, P])
        before = held("before", [P, P])
        eps = held("eps", [P, 1])
        woT = held("woT", [P, HALF, D])
        gateT = held("gateT", [P, HALF, E])
        rowmod = held("rowmod", [P, B, 4, D])
        gbo = held("gbo", [P, B, D])
        wgT = held("wgT", [P, HALF, F])
        wuT = held("wuT", [P, HALF, F])
        wdT = held("wdT", [P, FC, D])
        ones = held("ones", [P, P])
        zero_row = held("zero_row", [P, XW])
        sums = held("sums", [P, CH])
        logits = held("logits", [P, NT, E])
        iotas = held("iotas", [P, E + NT + 40])
        stage_at = held.at

        r = Region(nc, stage_at, experts_at)
        v_all = r("v_all", [P, NT, D])
        qs = buffers("qs", [P, S], BF16, r, NB)
        ks = buffers("ks", [P, S], BF16, r, NB)
        vs = buffers("vs", [P, KT, 32], F32, r, NB)
        mb = buffers("mb", [KT, 2, P], BF16, r, NB)
        head_out = r("head_out_sb", [P, CH])
        prob_at = r.at
        prob = r("prob", [P, 2, S])
        mx = r("mx", [P, KT, CPB])
        mneg = r("mneg", [P, KT])

        r = Region(nc, experts_at, top)
        cT = r("cT", [P, HALF, B])
        cS = r("cS", [P, HALF, B])
        cB = r("cB", [P, HALF, B, P])
        wmod = r("wmod", [P, HALF, 6 * D])
        loA = r("loA", [R, 4, D])
        loB = r("loB", [R, 4, D])
        wT = r("wT", [P, 4, HALF, D])
        wqkv = r("wqkv", [P, 3, HALF, D])
        bqk = r("bqk", [P, 4])
        bqk_in = r("bqk_in", [P, 4])
        bv_row = r("bv_row", [P, D])
        bo_row = r("bo_row", [P, D])
        colmod = r("colmod", [P, 2, HALF, B])
        gtmp = r("gtmp", [P, 3, B, 2, D])
        x_t = buffers("x_t", [P, TPC, D], F32, r)
        xn = buffers("xn", [P, TPC, D], F32, r)
        hT = buffers("hT", [P, HALF, CH], F32, r)
        qf = buffers("qf", [P, CH], F32, r, UQ)
        parts = buffers("parts", [P, 3, CH], BF16, r, UQ)
        stats = r("stats", [P, TPC, 6])
        mv = r("mv", [P, TPC, 2])
        std = r("std", [P, TPC])

        rest = buffers("rest", [P, CH], F32, Region(nc, prob_at, experts_at), UQ)

        r = Region(nc, experts_at, top)
        rgT = r("rgT", [P, E, HALF, F])
        ruT = r("ruT", [P, E, HALF, F])
        rdT = r("rdT", [P, E, FC, D])

        r = Region(nc, stage_at, experts_at)
        h2T = r("h2T", [P, HALF, T])
        after_h2T = r.at
        o_in = buffers("o_in", [P, HALF, CH], F32, r)
        l_in = buffers("l_in", [P, HALF, CH], F32, r)
        x_in = buffers("x_in", [P, TPC, D], F32, r)
        x1 = buffers("x1", [P, TPC, D], F32, r)
        h2 = buffers("h2", [P, TPC, D], F32, r)
        h2Tc = buffers("h2Tc", [P, HALF, CH], F32, r)
        stats2 = r("stats2", [P, TPC, 6])
        mv2 = r("mv2", [P, TPC, 2])
        std2 = r("std2", [P, TPC])

        r = Region(nc, after_h2T, experts_at)
        onehot = r("onehot", [P, NT, E])
        ra = r("ra", [P, NT, E])
        rb = r("rb", [P, NT, E])
        rt = r("rt", [P, NT, E])
        rmax = r("rmax", [P, NT])
        rix = r("rix", [P, NT])
        score = r("score", [P, NT])
        slot = r("slot", [P, NT], U32)
        cmp8 = r("cmp8", [P, E, NT])
        segs = r("segs", [P, 4, E])
        tcmp = r("tcmp", [P, 40, E])
        tile_f = r("tile_f", [P, 40])
        tile_e = r("tile_e", [P, 40], U32)
        sc_x = buffers("sc_x", [P, XW], F32, r, NSC)
        sc_ix = buffers("sc_ix", [P, 1], U32, r, NSC)
        route_end = r.at
        sgate = buffers("sgate", [P, CH], F32, r)
        hid = buffers("hid", [P, FC, CH], F32, r)
        ymod = r("ymod", [P, TPC, D])
        xr = buffers("xr", [P, TPC, D], F32, r)

        r = Region(nc, stage_at, experts_at)
        xs = buffers("xs", [P, XW], F32, r)
        xsT = buffers("xsT", [P, HALF, P], F32, r)
        esig = buffers("esig", [P, F], F32, r)
        ehid = buffers("ehid", [P, F], F32, r)
        ehT = buffers("ehT", [P, FC, P], F32, r)
        eout = buffers("eout", [P, D], F32, r)
        cx = buffers("cx", [P, D], F32, r, NG)
        cix = buffers("cix", [P, 1], U32, r, NG)
        assert r.at <= after_h2T
        r = Region(nc, experts_at, top)
        cy = buffers("cy", [P, D], F32, r, NG)

        block = ctx.enter_context(nc.Block())

        s_chain = {e: sem(f"chain_{e}") for e in ("dve", "act", "pool")}
        s_hold = sem("s_hold")
        s_eps = sem("s_eps")
        s_const = sem("s_const")
        s_shared = sem("s_shared")
        s_csilu = sem("s_csilu")
        s_crow = sem("s_crow")
        s_lora = sem("s_lora")
        s_weff = sem("s_weff")
        s_mrow = sem("s_mrow")
        s_mcol = sem("s_mcol")
        s_mod = sem("s_mod")
        s_gates = sem("s_gates")
        s_x = [sem(f"s_xin{u}") for u in range(2)]
        s_var = sem("s_var")
        s_std = sem("s_std")
        s_norm = sem("s_norm")
        s_xn_free = sem("s_xn_free")
        s_hT = sem("s_hT")
        s_unit = sem("s_unit")
        s_qbank_free = sem("s_qbank_free")
        s_rest = sem("s_rest")
        s_qf_free = sem("s_qf_free")
        s_parts = [sem(f"s_parts{o}") for o in range(UQ)]
        s_v = sem("s_v")
        s_vbank_free = sem("s_vbank_free")
        s_stack = [sem(f"s_stack{p}") for p in range(NB)]
        s_ones = sem("s_ones")
        s_vs = sem("s_vs")
        s_max = sem("s_max")
        s_ring = sem("s_ring")
        s_neg = sem("s_neg")
        s_mrows = [sem(f"s_mrows{p}") for p in range(NB)]
        s_score = sem("s_score")
        s_exp_free = sem("s_exp_free")
        s_prob_free = sem("s_prob_free")
        s_head = sem("s_head")
        s_hstore = sem("s_hstore")
        s_expert = sem("s_expert")
        s_zero = sem("s_zero")
        s_sums = sem("s_sums")
        s_rl = sem("s_rl")
        s_rlst = sem("s_rlst")
        s_oin = [sem(f"s_oin{u}") for u in range(2)]
        s_on = sem("s_on")
        s_op = sem("s_op")
        s_xb = sem("s_xb")
        s_x1 = sem("s_x1")
        s_x1st = [sem(f"s_x1st{u}") for u in range(2)]
        s_var2 = sem("s_var2")
        s_std2 = sem("s_std2")
        s_n2 = sem("s_n2")
        s_h2 = sem("s_h2")
        s_h2st = [sem(f"s_h2st{u}") for u in range(2)]
        s_h2_free = sem("s_h2_free")
        s_h2T = sem("s_h2T")
        s_lgp = sem("s_lgp")
        s_lg = sem("s_lg")
        s_oh = sem("s_oh")
        s_rank = sem("s_rank")
        s_route = sem("s_route")
        s_sig = sem("s_sig")
        s_scx = [sem(f"s_scx{u}") for u in range(NSC)]
        s_scat = [sem(f"s_scat{u}") for u in range(NSC)]
        s_xr = [sem(f"s_xr{u}") for u in range(2)]
        s_gu = sem("s_gu")
        s_silu = sem("s_silu")
        s_gu_free = sem("s_gu_free")
        s_y = sem("s_y")
        s_x2 = sem("s_x2")
        s_x2st = [sem(f"s_x2st{u}") for u in range(2)]
        s_xsc = sem("s_xsc")
        s_xs = [sem(f"s_xs{u}") for u in range(2)]
        s_xs_free = sem("s_xs_free")
        s_xsT = sem("s_xsT")
        s_egu = sem("s_egu")
        s_esig = sem("s_esig")
        s_ehid = sem("s_ehid")
        s_ehTp = sem("s_ehTp")
        s_ehT = sem("s_ehT")
        s_ey = sem("s_ey")
        s_eout = sem("s_eout")
        s_est = [sem(f"s_est{u}") for u in range(2)]
        s_cx = [sem(f"s_cx{u}") for u in range(NG)]
        s_cy = [sem(f"s_cy{u}") for u in range(NG)]
        s_ix = sem("s_ix")
        s_out = sem("s_out")
        s_ost = [sem(f"s_ost{u}") for u in range(NG)]

        def hold(eng):
            eng.sem_inc(s_hold, 1)

        sync_loads = [
            (loA, io["loA"]), (loB, io["loB"]), (ident, io["ident"]), (bqk_in, io["bqk"]),
            (bv_row, io["bv"].partition_broadcast(P)), (bo_row, io["bo"].partition_broadcast(P)),
            (gateT, io["gateT"]), (before, io["before"]), (iotas, io["iotas"]),
        ]
        scalar_loads = [(cT, io["cT"]), (wT, io["wT"]), (wmod, io["wmod"])]
        CONST = 16 * len(sync_loads + scalar_loads)
        rows = lambda dram, t, n: dram[bass.ds(t * P, n * P), :].rearrange("(t p) d -> p t d", p=P)

        def root(act, g):
            act.wait_ge(s_var, g + 1)
            act.activation(std[:], mv[:, :, 1], ACT.Sqrt, bias=eps[:, 0:1]).then_inc(s_std, 1)

        def normalize(dve, step, g, u, nth):
            dve.wait_ge(s_x[u], 16 * (nth + 1))
            for t in range(TPC):
                st = dve.bn_stats(stats[:, t, :], x_t[u][:, t, :])
            step(st)
            hold(dve)
            for t in range(TPC):
                a = dve.bn_aggr(mv[:, t, :], stats[:, t, :])
            a.then_inc(s_var, 1)
            dve.wait_ge(s_std, g + 1)
            step(dve.reciprocal(std[:], std[:]))
            wait(dve, s_xn_free, g - 1)
            for t in range(TPC):
                a = dve.tensor_scalar(xn[u][:, t, :], x_t[u][:, t, :], mv[:, t, 0:1], std[:, t:t + 1],
                                      ALU.subtract, ALU.mult)
            a.then_inc(s_norm, 1)

        def setup_sync(sp):
            for u in range(2):
                sp.dma_start(x_t[u][:], rows(io["x"], u * TPC, TPC)).then_inc(s_x[u], 16)
            for dst, src in sync_loads:
                sp.dma_start(dst[:], src).then_inc(s_const, 16)
            for dst, name in ((wgT, "wgT"), (wuT, "wuT"), (wdT, "wdT")):
                sp.dma_start(dst[:], io[name]).then_inc(s_shared, 16)

        def setup_scalar(act):
            for dst, src in scalar_loads:
                act.dma_start(dst[:], src).then_inc(s_const, 16)
            act.wait_ge(s_eps, 1)
            root(act, 0)
            root(act, 1)
            act.wait_ge(s_const, CONST)
            act.activation(cS[:], cT[:], ACT.Silu).then_inc(s_csilu, 1)

        def setup_tensor(pe):
            pe.wait_ge(s_const, CONST)
            for m in range(4):
                for k in range(HALF):
                    mm = pe.matmul(ps[:, m, k * D:(k + 1) * D], loA[:, m, k * P:(k + 1) * P], loB[:, m, :],
                                   start=True, stop=True)
            mm.then_inc(s_lora, 1)
            pe.wait_ge(s_csilu, 1)
            for v in range(2 * HALF):
                for k in range(HALF):
                    mm = pe.matmul(ps[:, 4, v * B:(v + 1) * B], wmod[:, k, v * P:(v + 1) * P], cS[:, k, :],
                                   start=(k == 0), stop=(k == 1))
            mm.then_inc(s_mcol, 1)
            pe.wait_ge(s_crow, 1)
            pe.wait_ge(s_weff, 1)
            for b in range(B):
                for c in range(2):
                    for k in range(HALF):
                        mm = pe.matmul(ps[:, 2 * b + c, :], cB[:, k, b, :],
                                       wmod[:, k, (c + 1) * 512:(c + 2) * 512], start=(k == 0), stop=(k == 1))
            mm.then_inc(s_mrow, 1)

        def setup_vector(dve, step):
            step(dve.memset(eps[:], EPS))
            dve.memset(ones[:], 1.0)
            step(dve.memset(zero_row[:], 0.0))
            dve.sem_inc(s_eps, 1)
            normalize(dve, step, 0, 0, 0)
            normalize(dve, step, 1, 1, 0)
            dve.wait_ge(s_csilu, 1)
            dve.tensor_copy(cB[:], cS[:].unsqueeze(3).to_broadcast([P, HALF, B, P])).then_inc(s_crow, 1)
            dve.tensor_scalar(bqk[:, 0:2], bqk_in[:, 0:2], 0.25, None, ALU.mult)
            dve.tensor_copy(bqk[:, 2:4], bqk_in[:, 2:4])
            dve.wait_ge(s_lora, 1)
            for m in range(4):
                dst = wqkv[:, m] if m < 3 else woT[:]
                w = dve.scalar_tensor_tensor(dst.rearrange("p k d -> p (k d)"), ps[:, m, :], LORA_SCALE,
                                             wT[:, m].rearrange("p k d -> p (k d)"), ALU.mult, ALU.add)
            w.then_inc(s_weff, 1)
            dve.wait_ge(s_mcol, 1)
            step(dve.tensor_copy(colmod[:].rearrange("p v k b -> p (v k b)"), ps[:, 4, 0:2 * HALF * B]))
            step(dve.tensor_scalar(colmod[:, 1], colmod[:, 1], 1.0, None, ALU.add))
            dve.wait_ge(s_mrow, 1)
            dve.tensor_copy(rowmod[:].rearrange("p b v d -> p (b v d)"),
                            ps[:, 0:4, :].rearrange("p c n -> p (c n)")).then_inc(s_mod, 1)

        def gates_vector(dve, step):
            dve.wait_ge(s_mod, 1)
            dve.tensor_scalar(rowmod[:, :, 2, :], rowmod[:, :, 2, :], 1.0, None, ALU.add)
            for v in (0, 3):
                g, mag, sign = rowmod[:, :, v, :], gtmp[:, 0, :, v // 3, :], gtmp[:, 1, :, v // 3, :]
                dve.tensor_scalar(sign, g, 0.0, 2.0, ALU.is_ge, ALU.mult)
                step(dve.tensor_scalar(mag, g, -1.0, None, ALU.mult))
                step(dve.tensor_tensor(mag, mag, g, ALU.max))
                step(dve.tensor_scalar(mag, mag, 0.25, None, ALU.max))
                step(dve.scalar_tensor_tensor(g, sign, -1.0, mag, ALU.add, ALU.mult))
            dve.tensor_tensor(gbo[:], rowmod[:, :, 0, :], bo_row[:].unsqueeze(1).to_broadcast([P, B, D]), ALU.mult).then_inc(s_gates, 1)

        def project_sync(sp):
            def load(g, u):
                sp.dma_start(x_t[u][:], rows(io["x"], g * TPC, TPC)).then_inc(s_x[u], 16)

            def store(g, b, j):
                for o in range(UQ):
                    half = o % 2
                    sp.wait_ge(s_qf_free, UQ + UQ * g + o + 1)
                    dst = qk_dram[o // 2].rearrange("s (b c) t -> c s b t", b=B)
                    sp.dma_start(dst[half * P:(half + 1) * P, :, bass.ds(b, 1), bass.ds(j * CH, CH)].squeeze(2),
                                 parts[o][:]).then_inc(s_parts[o], 16)

            with sp.Fori(0, NCH // 2 - 1) as i:
                for u in range(2):
                    sp.wait_ge(s_norm, 2 * i + u + 1)
                    load(2 * i + u + 2, u)
                    store(2 * i + u, i // 2, (i % 2) * 2 + u)
            for g in range(NCH - 2, NCH):
                store(g, g // CPB, g % CPB)

        def project_tensor(pe):
            pe.sem_inc(s_v, 1)

            def turn(g, u):
                pe.wait_ge(s_norm, g + 1)
                pe.wait_ge(s_hT, g)
                for k in range(HALF):
                    for t in range(TPC):
                        mm = pe.transpose(ps[:, k, t * P:(t + 1) * P], xn[u][:, t, k * P:(k + 1) * P], ident[:])
                mm.then_inc(s_xn_free, 1)

            def proj(g, u):
                pe.wait_ge(s_hT, g + 1)
                for o in range(4):
                    pe.wait_ge(s_qbank_free, UQ * g + o + 1)
                    for k in range(HALF):
                        mm = pe.matmul(ps[:, 2 + o % 2, :], wqkv[:, o // 2, k, (o % 2) * P:(o % 2 + 1) * P],
                                       hT[u][:, k, :], start=(k == 0), stop=(k == 1))
                    mm.then_inc(s_unit, 1)
                for t in range(TPC):
                    pe.wait_ge(s_vbank_free, TPC * g + t + 1)
                    for k in range(HALF):
                        mm = pe.matmul(ps[:, 4 + t % 2, 0:D], hT[u][:, k, t * P:(t + 1) * P], wqkv[:, 2, k, :],
                                       start=(k == 0), stop=(k == 1))
                    mm.then_inc(s_v, 1)

            pe.wait_ge(s_mod, 1)
            turn(0, 0)
            with pe.Fori(0, NCH // 2 - 1) as i:
                for u in range(2):
                    turn(2 * i + u + 1, 1 - u)
                    proj(2 * i + u, u)
            turn(NCH - 1, 1)
            proj(NCH - 2, 0)
            proj(NCH - 1, 1)

        def project_scalar(act):
            act.sem_inc(s_qbank_free, AHEAD)
            for o in range(UQ):
                act.sem_inc(s_parts[o], 16)
            act.wait_ge(s_mod, 1)

            def modulate(g, u, b):
                act.wait_ge(s_xn_free, g + 1)
                for k in range(HALF):
                    a = act.activation(hT[u][:, k, :], ps[:, k, :], ACT.Identity,
                                       bias=colmod[:, 0, k, bass.ds(b, 1)], scale=colmod[:, 1, k, bass.ds(b, 1)])
                a.then_inc(s_hT, 1)

            def take(g):
                for o in range(UQ):
                    bank, scale = 2 + o % 2, 0.25 if o < 2 else 1.0
                    act.wait_ge(s_unit, UQ * g + o + 1)
                    act.wait_ge(s_qf_free, UQ * g + o + 1)
                    act.activation(qf[o][:], ps[:, bank, :], ACT.Identity, bias=bqk[:, o:o + 1], scale=scale)
                    act.wait_ge(s_parts[o], 16 * (g + 1))
                    act.activation(parts[o][:, 0, :], ps[:, bank, :], ACT.Identity, bias=bqk[:, o:o + 1],
                                   scale=scale).then_inc(s_qbank_free, 1)

            modulate(0, 0, 0)
            with act.Fori(0, NCH // 2 - 1) as i:
                for u in range(2):
                    act.wait_ge(s_v, 1 + TPC * (2 * i + u))
                    modulate(2 * i + u + 1, 1 - u, (i * 2 + u + 1) // CPB)
                    root(act, 2 * i + u + 2)
                    take(2 * i + u)
            act.wait_ge(s_v, 1 + TPC * (NCH - 2))
            modulate(NCH - 1, 1, B - 1)
            take(NCH - 2)
            take(NCH - 1)

        def project_vector(dve, step):
            dve.sem_inc(s_qf_free, UQ)
            dve.sem_inc(s_vbank_free, AHEAD)

            def cut(g):
                for o in range(UQ):
                    dve.wait_ge(s_rest, UQ * g + o + 1)
                    step(dve.tensor_copy(parts[o][:, 1, :], rest[o][:]))
                    dve.tensor_tensor(parts[o][:, 2, :], rest[o][:], parts[o][:, 1, :],
                                      ALU.subtract).then_inc(s_qf_free, 1)
                for t in range(TPC):
                    dve.wait_ge(s_v, 1 + TPC * g + t + 1)
                    dve.tensor_tensor(v_all[:, bass.ds(TPC * g + t, 1), :].squeeze(1), ps[:, 4 + t % 2, 0:D],
                                      bv_row[:], ALU.add).then_inc(s_vbank_free, 1)

            per = 2 * (2 + UQ)
            with dve.Fori(0, NCH // 2 - 1) as i:
                step.turns(i, per)
                for u in range(2):
                    normalize(dve, step, 2 * i + u + 2, u, i + 1)
                    cut(2 * i + u)
            step.close(NCH // 2 - 1, per)
            cut(NCH - 2)
            cut(NCH - 1)

        def project_gpsimd(pool):
            with pool.Fori(0, NCH) as g:
                for o in range(UQ):
                    pool.wait_ge(s_qbank_free, AHEAD + UQ * g + o + 1)
                    pool.tensor_tensor(rest[o][:], qf[o][:], parts[o][:, 0, :], ALU.subtract).then_inc(s_rest, 1)

        num = lambda h: NB * h[0] + h[1]
        nth = lambda h: h[0] + h[1] // NB
        buf = lambda h: h[1] % NB
        plus = lambda h, k: (h[0], h[1] + k)
        half_bank = lambda h: slice(2 * h, 2 * h + 2)

        def inverse_sums(sp, b):
            half = slice(b * P // B, (b + 1) * P // B)
            sp.wait_ge(s_hstore, 16 * (H * (b + 1) + 1))
            sp.dma_start(sums[half, :], o_dram.rearrange("n (j r) t -> (n j) r t", r=32)[half, DH, :]
                         ).then_inc(s_sums, 16)
            sp.wait_ge(s_rl, b + 1)
            sp.dma_start(rl_dram[half, :], sums[half, :]).then_inc(s_rlst, 16)

        def invert(dve, b):
            half = slice(b * P // B, (b + 1) * P // B)
            dve.wait_ge(s_sums, 16 * (b + 1))
            dve.reciprocal(sums[half, :], sums[half, :]).then_inc(s_rl, 1)

        def attend_sync(sp):
            for o in range(UQ):
                sp.wait_ge(s_parts[o], 16 * (NCH + 1))

            def stack(h):
                p = buf(h)
                for which, runs, tile in ((0, Q_RUNS, qs[p]), (1, K_RUNS, ks[p])):
                    for group, part, n in runs:
                        src = qk_dram[which]
                        if which == 0:
                            src = src[part:part + n]
                        else:
                            src = src[part:part + 1].to_broadcast([n, B * D, S])
                        sp.dma_start(tile[group * DH:(group + n) * DH, :],
                                     src[:, bass.ds(num(h) * DH, DH), :]).then_inc(s_stack[p], 16)

            def maxima(h, last=False):
                p = buf(h)
                sp.wait_ge(s_ring, MAXIMA * (num(h) + 1) + (1 if last else 2))
                for m in range(2):
                    sp.dma_start(qs[p][ROWS + m:ROWS + m + 1, :].rearrange("a (t c) -> a t c", t=KT),
                                 mb[p][:, m, :]).then_inc(s_mrows[p], 16)

            def head_store(h):
                sp.wait_ge(s_head, num(h) + 1)
                sp.dma_start(o_dram[bass.ds(num(h), 1)].squeeze(0), head_out[:]).then_inc(s_hstore, 16)

            def turn(h, last):
                if last >= 2:
                    sp.wait_ge(s_score, 2 * KT * num(h))
                    stack(plus(h, 2))
                head_store(plus(h, -1))
                if last >= 1:
                    maxima(plus(h, 1), last == 1)
                if last == 3:
                    inverse_sums(sp, 0)

            for n in range(NB):
                stack((0, n))
            maxima((0, 0))
            maxima((0, 1))
            trips = (NH - 5) // NB
            with sp.Fori(0, trips) as i:
                for u in range(NB):
                    turn((i, 1 + u), 2)
            for n in range(1 + NB * trips, NH):
                turn((0, n), NH - 1 - n)
            head_store((0, NH - 1))

        item = lambda k: k + (k > 0)
        first_head = lambda h: isinstance(h[0], int) and num(h) == 0
        ring_bank = lambda k: 4 + item(k) % RING
        TURNED_BANK = 4 + 1

        def attend_tensor(pe):
            pe.sem_inc(s_max, 1)
            pe.sem_inc(s_prob_free, AHEAD)
            pe.wait_ge(s_ones, 1)
            pe.wait_ge(s_qbank_free, AHEAD + UQ * NCH)
            pe.wait_ge(s_vbank_free, AHEAD + NT)

            def unit(h, k):
                p, t, c = buf(h), k // CPB, k % CPB
                if k == 0:
                    pe.wait_ge(s_stack[p], 96 * (nth(h) + 1))
                if k < 2:
                    wait(pe, s_ring, MAXIMA * num(h) - (1 if k == 0 else 2))
                elif k == 2 and first_head(h):
                    pe.wait_ge(s_ring, 2)
                else:
                    pe.wait_ge(s_ring, MAXIMA * num(h) + item(k) - RING + 1)
                pe.matmul(ps[:, ring_bank(k), :], qs[p][0:ROWS, t * P:(t + 1) * P],
                          ks[p][0:ROWS, c * CH:(c + 1) * CH], start=True, stop=True).then_inc(s_max, 1)

            def turn_maxima(h):
                pe.wait_ge(s_neg, num(h) + 1)
                pe.transpose(ps[0:KT, TURNED_BANK, 0:P], mneg[:, :], ident[:]).then_inc(s_max, 1)

            def scores(h, kt, half):
                p = buf(h)
                if kt == 0 and half == 0:
                    pe.wait_ge(s_mrows[p], 32 * (nth(h) + 2))
                pe.wait_ge(s_exp_free, 2 * KT * num(h) + 2 * kt + half + 1)
                for c in range(2):
                    q = (2 * half + c) * CH
                    mm = pe.matmul(ps[:, 2 * half + c, :], ks[p][0:ROWS + 2, kt * P:(kt + 1) * P],
                                   qs[p][0:ROWS + 2, q:q + CH], start=True, stop=True)
                mm.then_inc(s_score, 1)

            def weigh(h, kt):
                if kt == 0:
                    pe.wait_ge(s_vs, num(h) + 1)
                    pe.wait_ge(s_head, num(h))
                pe.wait_ge(s_exp_free, AHEAD + 2 * KT * num(h) + 2 * kt + 2)
                for j in range(CPB):
                    mm = pe.matmul(ps[32 * j:32 * j + 32, 7, :], vs[buf(h)][:, kt, :],
                                   prob[:, kt % 2, j * CH:(j + 1) * CH], start=(kt == 0), stop=(kt == KT - 1))
                mm.then_inc(s_prob_free, 1)

            def turn(h, after):
                for kt in range(1, KT + 1 if after else KT):
                    s = (h, kt) if kt < KT else (plus(h, 1), 0)
                    first, who = LEAD + CPB * (kt - 1), plus(h, 1)
                    turns = first == UNITS and after >= 1
                    if first >= UNITS:
                        first, who = first - UNITS, plus(h, 2)
                    units = [(who, first + c) for c in range(CPB)]
                    if after < (1 if who == plus(h, 1) else 2):
                        units = []
                    scores(*s, 0)
                    for k in units[:1]:
                        unit(*k)
                    scores(*s, 1)
                    if turns:
                        turn_maxima(plus(h, 1))
                    for k in units[1:2 if turns else 3]:
                        unit(*k)
                    weigh(h, kt - 1)
                    for k in units[2 if turns else 3:]:
                        unit(*k)
                if not after:
                    weigh(h, KT - 1)

            for k in range(UNITS):
                unit((0, 0), k)
            unit((0, 1), 0)
            turn_maxima((0, 0))
            for k in range(1, LEAD):
                unit((0, 1), k)
            for half in range(2):
                scores((0, 0), 0, half)
            with pe.Fori(0, (NH - 2) // NB) as i:
                for u in range(NB):
                    turn((i, u), 2)
            turn((0, NH - 2), 1)
            turn((0, NH - 1), 0)

        def attend_vector(dve, step):
            def unit(h, k):
                dve.wait_ge(s_max, 2 if first_head(h) and k == 0 else MAXIMA * num(h) + item(k) + 1)
                dve.tensor_reduce(mx[:, k // CPB, k % CPB:k % CPB + 1], ps[:, ring_bank(k), :], AX.X,
                                  ALU.max).then_inc(s_ring, 1)

            def head(h, last=False):
                following = MAXIMA * (num(h) + 1)
                for k in range(1, UNITS):
                    unit(h, k)
                dve.wait_ge(s_ring, following)
                dve.tensor_reduce(mneg[:], mx[:], AX.X, ALU.max, negate=True).then_inc(s_neg, 1)
                if not last:
                    dve.wait_ge(s_neg, num(h) + 1)
                    unit(plus(h, 1), 0)
                dve.wait_ge(s_max, following + (1 if last else 2))
                dve.wait_ge(s_mrows[buf(h)], 32 * (nth(h) + 1))
                turned = ps[0:KT, TURNED_BANK, 0:P]
                step(dve.tensor_copy(mb[buf(h)][:, 0, :], turned))
                dve.tensor_tensor(mb[buf(h)][:, 1, :], turned, mb[buf(h)][:, 0, :],
                                  ALU.subtract).then_inc(s_ring, 1)

            dve.sem_inc(s_ring, 1)
            for p in range(NB):
                dve.sem_inc(s_mrows[p], 32)
            unit((0, 0), 0)
            with dve.Fori(0, NH // NB) as i:
                step.turns(i, NB)
                for u in range(NB):
                    head((i, u))
            step.close(NH // NB, NB)
            invert(dve, 0)
            head((0, NH - 2))
            head((0, NH - 1), last=True)

        def attend_scalar(act):
            act.sem_inc(s_exp_free, AHEAD)
            act.sem_inc(s_hstore, 16)

            def exps(n, kt):
                act.wait_ge(s_prob_free, KT * n + kt + 1)
                for half in range(2):
                    act.wait_ge(s_score, 2 * KT * n + 2 * kt + half + 1)
                    act.activation(prob[:, kt % 2, half * 2 * CH:(half + 1) * 2 * CH],
                                   ps[:, half_bank(half), :].rearrange("p c n -> p (c n)"),
                                   ACT.Exp).then_inc(s_exp_free, 1)

            def head_copy(n):
                act.wait_ge(s_prob_free, AHEAD + KT * (n + 1))
                act.wait_ge(s_hstore, 16 * (n + 1))
                act.copy(head_out[:], ps[:, 7, :]).then_inc(s_head, 1)

            for kt in range(KT):
                exps(0, kt)
            with act.Fori(1, NH) as n:
                for kt in range(KT):
                    exps(n, kt)
                    if kt == 0:
                        head_copy(n - 1)
            head_copy(NH - 1)

        def attend_gpsimd(pool, step):
            pool.wait_ge(s_rest, UQ * NCH)
            for p in range(NB):
                step(pool.memset(ks[p][ROWS:ROWS + 2, :], 1.0))
                step(pool.memset(vs[p][:], 0.0))
                step(pool.memset(vs[p][:, :, DH:DH + 1], 1.0))
            pool.sem_inc(s_ones, 1)
            pool.wait_ge(s_vbank_free, AHEAD + NT)

            def stage(h):
                n = num(h)
                pool.tensor_copy(vs[buf(h)][:, :, 0:DH],
                                 v_all[:, bass.ds(n // H * KT, KT), bass.ds(n % H * DH, DH)]).then_inc(s_vs, 1)

            for n in range(NB):
                stage((0, n))
            for o in range(UQ):
                pool.wait_ge(s_parts[o], 16 * (NCH + 1))
            padded = xs_dram.rearrange("(n p) d -> p n d", p=P)

            def zero(piece):
                pool.dma_start(padded[:, bass.ds(piece * ZERO, ZERO), :],
                               zero_row[:].unsqueeze(1).to_broadcast([P, ZERO, XW])).then_inc(s_zero, 16)

            with pool.Fori(0, E) as i:
                for u in range(NB):
                    pool.wait_ge(s_prob_free, AHEAD + KT * (NB * i + u + 1))
                    stage((i, NB + u))
                    dst, name = ((rgT, "rgT"), (ruT, "ruT"), (rdT, "rdT"))[u]
                    pool.dma_start(dst[:, bass.ds(i, 1)], io[name][:, bass.ds(i, 1)]).then_inc(s_expert, 16)
                zero(i)
            for n in range(NB * (E + 1), NH):
                pool.wait_ge(s_prob_free, AHEAD + KT * (n - NB + 1))
                stage((0, n))
                zero(n - NB * (E + 1) + E)

        def merge_sync(sp):
            sp.wait_ge(s_hstore, 16 * (NH + 1))
            sp.wait_ge(s_rlst, 16)

            def load(g, u, b, j):
                for k in range(HALF):
                    heads = o_dram[bass.ds(b * H + k * (H // HALF), H // HALF)]
                    rows_of = heads[:, bass.ds(32 * j, 32), :]
                    sp.dma_start(o_in[u][:, k, :], rows_of[:, 0:DH, :]).then_inc(s_oin[u], 16)
                    inv = rl_dram.rearrange("(n j) t -> n j t", j=CPB)[bass.ds(b * H + k * (H // HALF), H // HALF)]
                    sp.dma_start(l_in[u][:, k, :], inv[:, bass.ds(j, 1), :].to_broadcast(
                        [H // HALF, DH, CH])).then_inc(s_oin[u], 16)
                sp.dma_start(x_in[u][:], rows(io["x"], g * TPC, TPC)).then_inc(s_oin[u], 16)

            def store(g, u):
                sp.wait_ge(s_x1, g + 1)
                sp.dma_start(rows(x1_dram, g * TPC, TPC), x1[u][:]).then_inc(s_x1st[u], 16)
                sp.wait_ge(s_h2, g + 1)
                sp.dma_start(rows(h2_dram, g * TPC, TPC), h2[u][:]).then_inc(s_h2st[u], 16)

            load(0, 0, 0, 0)
            load(1, 1, 0, 1)
            inverse_sums(sp, 1)
            for g in range(2):
                sp.wait_ge(s_x1, g + 1)
                load(g + 2, g, 0, g + 2)
                store(g, g)
            sp.wait_ge(s_rlst, 32)
            with sp.Fori(1, NCH // 2 - 1) as i:
                for u in range(2):
                    sp.wait_ge(s_x1, 2 * i + u + 1)
                    load(2 * i + u + 2, u, (i + 1) // 2, (i + 1) % 2 * 2 + u)
                    store(2 * i + u, u)
            store(NCH - 2, 0)
            store(NCH - 1, 1)

        OUT_BANK = (0, 5)

        def merge_tensor(pe):
            pe.wait_ge(s_exp_free, AHEAD + 2 * KT * NH)
            pe.wait_ge(s_ring, MAXIMA * NH + 1)

            def out_proj(g, u):
                pe.wait_ge(s_on, g + 1)
                wait(pe, s_x1, g - 1)
                for t in range(TPC):
                    for k in range(HALF):
                        mm = pe.matmul(ps[:, OUT_BANK[u] + t // 2, t % 2 * D:(t % 2 + 1) * D], o_in[u][:, k, t * P:(t + 1) * P],
                                       woT[:, k, :], start=(k == 0), stop=(k == 1))
                mm.then_inc(s_op, 1)

            def turn(g, u):
                pe.wait_ge(s_h2, g + 1)
                pe.wait_ge(s_h2T, g + 1)
                for k in range(HALF):
                    for t in range(TPC):
                        mm = pe.transpose(ps[:, 2 + k, t * P:(t + 1) * P], h2[u][:, t, k * P:(k + 1) * P], ident[:])
                mm.then_inc(s_h2_free, 1)

            def route_logits(g, u):
                pe.wait_ge(s_h2T, g + 2)
                pe.wait_ge(s_lg, g + 1)
                for t in range(TPC):
                    for k in range(HALF):
                        mm = pe.matmul(ps[:, 4, t * E:(t + 1) * E], h2Tc[u][:, k, t * P:(t + 1) * P],
                                       gateT[:, k, :], start=(k == 0), stop=(k == 1))
                mm.then_inc(s_lgp, 1)

            out_proj(0, 0)
            out_proj(1, 1)
            with pe.Fori(0, NCH // 2 - 1) as i:
                for u in range(2):
                    turn(2 * i + u, u)
                    out_proj(2 * i + u + 2, u)
                    route_logits(2 * i + u, u)
            for g in range(NCH - 2, NCH):
                turn(g, g % 2)
                route_logits(g, g % 2)

        def merge_vector(dve, step):
            def divide(g, u, nth):
                dve.wait_ge(s_oin[u], 80 * (nth + 1))
                dve.tensor_tensor(o_in[u][:], o_in[u][:], l_in[u][:], ALU.mult).then_inc(s_on, 1)

            def residual(g, u, nth, b):
                dve.wait_ge(s_op, g + 1)
                dve.wait_ge(s_x1st[u], 16 * (nth + 1))
                step(dve.tensor_tensor(x1[u][:], ps[:, OUT_BANK[u]:OUT_BANK[u] + 2, :].rearrange(
                                           "p c (t d) -> p (c t) d", d=D),
                                       rowmod[:, bass.ds(b, 1), 0, :].to_broadcast([P, TPC, D]), ALU.mult))
                dve.wait_ge(s_xb, g + 1)
                dve.tensor_tensor(x1[u][:], x1[u][:], x_in[u][:], ALU.add).then_inc(s_x1, 1)
                dve.wait_ge(s_x1, g + 1)
                for t in range(TPC):
                    st = dve.bn_stats(stats2[:, t, :], x1[u][:, t, :])
                step(st)
                hold(dve)
                for t in range(TPC):
                    a = dve.bn_aggr(mv2[:, t, :], stats2[:, t, :])
                a.then_inc(s_var2, 1)
                dve.wait_ge(s_std2, g + 1)
                step(dve.reciprocal(std2[:], std2[:]))
                wait(dve, s_h2_free, g - 1)
                dve.wait_ge(s_h2st[u], 16 * (nth + 1))
                for t in range(TPC):
                    a = dve.tensor_scalar(h2[u][:, t, :], x1[u][:, t, :], mv2[:, t, 0:1], std2[:, t:t + 1],
                                          ALU.subtract, ALU.mult)
                a.then_inc(s_n2, 1)

            for u in range(2):
                dve.sem_inc(s_x1st[u], 16)
                dve.sem_inc(s_h2st[u], 16)
            divide(0, 0, 0)
            divide(1, 1, 0)
            invert(dve, 1)
            residual(0, 0, 0, 0)
            per = 2 * 3
            with dve.Fori(0, NCH // 2 - 1) as i:
                step.turns(i, per)
                for u in range(2):
                    divide(2 * i + u + 2, u, i + 1)
                    residual(2 * i + u + 1, 1 - u, i + u, (2 * i + u + 1) // CPB)
            step.close(NCH // 2 - 1, per)
            residual(NCH - 1, 1, NCH // 2 - 1, B - 1)

        def merge_gpsimd(pool, step):
            def bias(g, u, nth, b):
                pool.wait_ge(s_oin[u], 80 * (nth + 1))
                hold(pool)
                pool.tensor_tensor(x_in[u][:], x_in[u][:], gbo[:, bass.ds(b, 1), :].to_broadcast([P, TPC, D]),
                                   ALU.add).then_inc(s_xb, 1)

            def modulate(g, u, b):
                pool.wait_ge(s_n2, g + 1)
                hold(pool)
                step(pool.tensor_tensor(h2[u][:], h2[u][:], rowmod[:, bass.ds(b, 1), 2, :].to_broadcast(
                    [P, TPC, D]), ALU.mult))
                hold(pool)
                pool.tensor_tensor(h2[u][:], h2[u][:], rowmod[:, bass.ds(b, 1), 1, :].to_broadcast(
                    [P, TPC, D]), ALU.add).then_inc(s_h2, 1)

            pool.wait_ge(s_gates, 1)
            bias(0, 0, 0, 0)
            bias(1, 1, 0, 0)
            modulate(0, 0, 0)
            with pool.Fori(0, NCH // 2 - 1) as i:
                step.turns(i, 2)
                for u in range(2):
                    bias(2 * i + u + 2, u, i + 1, (i + 1) // (CPB // 2))
                    modulate(2 * i + u + 1, 1 - u, (2 * i + u + 1) // CPB)
            step.close(NCH // 2 - 1, 2)
            modulate(NCH - 1, 1, B - 1)

        def merge_scalar(act):
            act.sem_inc(s_h2T, 1)
            act.sem_inc(s_lg, 1)

            def root2(g):
                act.wait_ge(s_var2, g + 1)
                act.activation(std2[:], mv2[:, :, 1], ACT.Sqrt, bias=eps[:, 0:1]).then_inc(s_std2, 1)

            def take(g, u):
                act.wait_ge(s_h2_free, g + 1)
                for k in range(HALF):
                    act.copy(h2T[:, k, bass.ds(g * CH, CH)], ps[:, 2 + k, :])
                    a = act.copy(h2Tc[u][:, k, :], ps[:, 2 + k, :])
                a.then_inc(s_h2T, 1)

            def take_logits(g):
                act.wait_ge(s_lgp, g + 1)
                act.copy(logits[:, bass.ds(TPC * g, TPC), :].rearrange("p t e -> p (t e)"),
                         ps[:, 4, 0:TPC * E]).then_inc(s_lg, 1)

            root2(0)
            with act.Fori(0, NCH // 2 - 1) as i:
                for u in range(2):
                    take(2 * i + u, u)
                    root2(2 * i + u + 1)
                    take_logits(2 * i + u)
            for g in range(NCH - 2, NCH):
                take(g, g % 2)
                if g == NCH - 2:
                    root2(NCH - 1)
                take_logits(g)

        def route_vector(dve, step):
            by_tile = lambda a: a.unsqueeze(2).to_broadcast([P, NT, E])
            by_expert = lambda a: a.unsqueeze(1).to_broadcast([P, NT, E])
            less8, firsts, count40 = iotas[:, 0:E], iotas[:, E:E + NT], iotas[:, E + NT:E + NT + 40]
            dve.wait_ge(s_lg, NCH + 1)
            for u in range(2):
                dve.wait_ge(s_x1st[u], 16 * (NCH // 2 + 1))
                dve.wait_ge(s_h2st[u], 16 * (NCH // 2 + 1))
            step(dve.tensor_reduce(rmax[:], logits[:], AX.X, ALU.max))
            step(dve.tensor_tensor(rt[:], logits[:], by_tile(rmax[:]), ALU.is_ge))
            step(dve.tensor_tensor(rt[:], rt[:], by_expert(less8), ALU.mult))
            step(dve.tensor_reduce(rix[:], rt[:], AX.X, ALU.min))
            dve.tensor_tensor(onehot[:], by_expert(less8), by_tile(rix[:]), ALU.is_equal).then_inc(s_oh, 1)
            dve.wait_ge(s_rank, 1)
            in_tile = ps[:, 0, 0:NT * E].rearrange("p (t e) -> p t e", e=E)
            totals = ps[:, 1, 0:NT * E].rearrange("p (t e) -> p t e", e=E)
            a, b = ra, rb
            step(dve.tensor_copy(a[:], totals))
            for s in (1, 2, 4, 8, 16):
                dve.tensor_copy(b[:, 0:s, :], a[:, 0:s, :])
                step(dve.tensor_tensor(b[:, s:, :], a[:, s:, :], a[:, :NT - s, :], ALU.add))
                a, b = b, a
            step(dve.tensor_tensor(cmp8[:], a[:, NT - 1, :].unsqueeze(2).to_broadcast([P, E, NT]),
                                   firsts.unsqueeze(1).to_broadcast([P, E, NT]), ALU.is_gt))
            need, p, q, at = (segs[:, k, :] for k in range(4))
            step(dve.tensor_reduce(need, cmp8[:], AX.X, ALU.add))
            step(dve.tensor_copy(p, need))
            for s in (1, 2, 4):
                dve.tensor_copy(q[:, 0:s], p[:, 0:s])
                step(dve.tensor_tensor(q[:, s:], p[:, s:], p[:, :E - s], ALU.add))
                p, q = q, p
            step(dve.tensor_tensor(at, p, need, ALU.subtract))
            step(dve.tensor_scalar(at, at, float(P), None, ALU.mult))
            step(dve.tensor_tensor(rt[:], a[:], totals, ALU.subtract))
            step(dve.tensor_tensor(rt[:], rt[:], in_tile, ALU.add))
            step(dve.tensor_tensor(rt[:], rt[:], by_expert(at), ALU.add))
            step(dve.tensor_tensor(rt[:], rt[:], onehot[:], ALU.mult))
            step(dve.tensor_reduce(rix[:], rt[:], AX.X, ALU.add))
            dve.tensor_copy(slot[:], rix[:])
            step(dve.tensor_tensor(tcmp[:], count40.unsqueeze(2).to_broadcast([P, 40, E]),
                                   p.unsqueeze(1).to_broadcast([P, 40, E]), ALU.is_ge))
            step(dve.tensor_reduce(tile_f[:], tcmp[:], AX.X, ALU.add))
            dve.tensor_scalar(tile_e[:], tile_f[:], float(E - 1), None, ALU.min).then_inc(s_route, 1)

        def route_tensor(pe):
            pe.wait_ge(s_oh, 1)
            pe.matmul(ps[:, 0, 0:NT * E], before[:], onehot[:].rearrange("p t e -> p (t e)"), start=True, stop=True)
            pe.matmul(ps[:, 1, 0:NT * E], ones[:], onehot[:].rearrange("p t e -> p (t e)"),
                      start=True, stop=True).then_inc(s_rank, 1)

        def route_scalar(act):
            act.wait_ge(s_oh, 1)
            act.activation(score[:], rmax[:], ACT.Sigmoid).then_inc(s_sig, 1)

        def shared_sync(sp):
            sp.wait_ge(s_route, 1)
            for u in range(2):
                sp.wait_ge(s_h2st[u], 16 * (NCH // 2 + 1))
                sp.wait_ge(s_x1st[u], 16 * (NCH // 2 + 1))

            def load(g, u):
                sp.dma_start(xr[u][:], rows(x1_dram, g * TPC, TPC)).then_inc(s_xr[u], 16)

            def token_rows(i, u):
                wait(sp, s_scat[u], 16 * i)
                sp.dma_start(sc_x[u][:, 0:D], h2_dram[bass.ds((NSC * i + u) * P, P), :]).then_inc(s_scx[u], 16)

            for u in range(NSC):
                token_rows(0, u)
            load(0, 0)
            load(1, 1)

            def store(g, u):
                sp.wait_ge(s_x2, g + 2)
                sp.dma_start(rows(x2_dram, g * TPC, TPC), xr[u][:]).then_inc(s_x2st[u], 16)

            with sp.Fori(0, NCH // 2 - 1) as i:
                for u in range(2):
                    for v in range(NSC):
                        token_rows(2 * i + u + 1, v)
                    store(2 * i + u, u)
                    sp.wait_ge(s_x2st[u], 16 * (i + 1))
                    load(2 * i + u + 2, u)
            for v in range(NSC):
                token_rows(NCH - 1, v)
            for u in range(2):
                store(NCH - 2 + u, u)

        def scatter_gpsimd(pool, step):
            pool.wait_ge(s_route, 1)
            pool.wait_ge(s_sig, 1)
            pool.wait_ge(s_zero, 16 * NTILE // ZERO)

            def scatter(i, u):
                pool.wait_ge(s_scx[u], 16 * (i + 1))
                hold(pool)
                pool.tensor_copy(sc_ix[u][:], slot[:, bass.ds(NSC * i + u, 1)])
                step(pool.tensor_copy(sc_x[u][:, D:XW], score[:, bass.ds(NSC * i + u, 1)]))
                hold(pool)
                pool.indirect_dma_start(xs_dram, bass.IndirectOffsetOnAxis(sc_ix[u][:, 0:1], 0), sc_x[u][:],
                                        None).then_inc(s_scat[u], 16)

            with pool.Fori(0, NT // NSC) as i:
                step.turns(i, NSC)
                for u in range(NSC):
                    scatter(i, u)
            step.close(NT // NSC, NSC)

        def shared_tensor(pe):
            pe.wait_ge(s_shared, 48)
            pe.sem_inc(s_gu_free, AHEAD)
            pe.wait_ge(s_lg, NCH + 1)

            def gate_up(g):
                for fc in range(FC):
                    pe.wait_ge(s_gu_free, FC * g + fc + 1)
                    for w, bank in ((wgT, 2 + 2 * (fc % 2)), (wuT, 3 + 2 * (fc % 2))):
                        for k in range(HALF):
                            mm = pe.matmul(ps[:, bank, :], w[:, k, fc * P:(fc + 1) * P],
                                           h2T[:, k, bass.ds(g * CH, CH)], start=(k == 0), stop=(k == 1))
                    mm.then_inc(s_gu, 1)

            def down(g, u):
                pe.wait_ge(s_gu_free, AHEAD + FC * (g + 1))
                pe.wait_ge(s_x2, g + 1)
                for t in range(TPC):
                    for fc in range(FC):
                        mm = pe.matmul(ps[:, 6 + t // 2, t % 2 * D:(t % 2 + 1) * D], hid[u][:, fc, t * P:(t + 1) * P],
                                       wdT[:, fc, :], start=(fc == 0), stop=(fc == FC - 1))
                mm.then_inc(s_y, 1)

            gate_up(0)
            with pe.Fori(0, NCH // 2 - 1) as i:
                for u in range(2):
                    gate_up(2 * i + u + 1)
                    down(2 * i + u, u)
            gate_up(NCH - 1)
            down(NCH - 2, 0)
            down(NCH - 1, 1)

        def shared_scalar(act):
            act.wait_ge(s_route, 1)
            with act.Fori(0, NCH) as g:
                for fc in range(FC):
                    u = fc % 2
                    act.wait_ge(s_gu, FC * g + fc + 1)
                    act.wait_ge(s_gu_free, FC * g + fc + 1)
                    act.activation(sgate[u][:], ps[:, 2 + 2 * u, :], ACT.Silu).then_inc(s_silu, 1)

        def shared_vector(dve, step):
            def hidden(g, u):
                for fc in range(FC):
                    dve.wait_ge(s_silu, FC * g + fc + 1)
                    if fc == 0:
                        wait(dve, s_y, g - 1)
                    dve.tensor_tensor(hid[u][:, fc, :], sgate[fc % 2][:], ps[:, 3 + 2 * (fc % 2), :],
                                      ALU.mult).then_inc(s_gu_free, 1)

            def residual(g, u, nth, b):
                dve.wait_ge(s_y, g + 1)
                step(dve.tensor_tensor(ymod[:], ps[:, 6:8, :].rearrange("p c (t d) -> p (c t) d", d=D),
                                       rowmod[:, bass.ds(b, 1), 3, :].to_broadcast([P, TPC, D]), ALU.mult))
                dve.wait_ge(s_xr[u], 16 * (nth + 1))
                dve.tensor_tensor(xr[u][:], xr[u][:], ymod[:], ALU.add).then_inc(s_x2, 1)
                dve.wait_ge(s_x2, g + 2)

            dve.sem_inc(s_x2, 1)
            hidden(0, 0)
            hidden(1, 1)
            with dve.Fori(0, NCH // 2 - 1) as i:
                step.turns(i, 2)
                for u in range(2):
                    residual(2 * i + u, u, i, i // 2)
                    hidden(2 * i + u + 2, u)
            step.close(NCH // 2 - 1, 2)
            residual(NCH - 2, 0, NCH // 2 - 1, B - 1)
            residual(NCH - 1, 1, NCH // 2 - 1, B - 1)

        LAST = NTILE - 3

        def routed_sync(sp):
            for u in range(NSC):
                sp.wait_ge(s_scat[u], 16 * (NT // NSC))
            sp.wait_ge(s_y, NCH)

            def load(k, u):
                sp.wait_ge(s_xs_free, k + 1)
                sp.dma_start(xs[u][:], xs_dram[bass.ds(k * P, P), :]).then_inc(s_xs[u], 16)

            def store(k, u):
                sp.wait_ge(s_eout, k + 2)
                sp.dma_start(ys_dram[bass.ds(k * P, P), :], eout[u][:]).then_inc(s_est[u], 16)

            load(0, 0)
            load(1, 1)
            load(2, 0)
            with sp.Fori(0, LAST // 2) as i:
                for u in range(2):
                    load(2 * i + u + 3, 1 - u)
                    store(2 * i + u, u)
            for k in range(LAST, NTILE):
                store(k, k % 2)

        def routed_tensor(pe):
            pe.sem_inc(s_xs_free, AHEAD)
            pe.wait_ge(s_x2, NCH + 1)
            pe.wait_ge(s_expert, 48 * E)

            def turn_in(k, u):
                pe.wait_ge(s_xsc, k + 1)
                pe.wait_ge(s_xsT, k)
                for c in range(HALF):
                    mm = pe.transpose(ps[:, 0, c * P:(c + 1) * P], xs[u][:, c * P:(c + 1) * P], ident[:])
                mm.then_inc(s_xs_free, 1)

            def gate_up(k, u):
                e = pe.value_load(tile_e[0:1, bass.ds(k, 1)], min_val=0, max_val=E - 1)
                pe.wait_ge(s_xsT, k + 1)
                wait(pe, s_ehid, k)
                for w, bank in ((rgT, 1 + 2 * u), (ruT, 2 + 2 * u)):
                    for c in range(HALF):
                        mm = pe.matmul(ps[:, bank, :], xsT[u][:, c, :], w[:, bass.ds(e, 1), c, :].squeeze(1),
                                       start=(c == 0), stop=(c == 1))
                mm.then_inc(s_egu, 1)
                return e

            def turn_hidden(k, u):
                pe.wait_ge(s_ehid, k + 2)
                pe.wait_ge(s_ehT, k + 1)
                for c in range(FC):
                    mm = pe.transpose(ps[:, 5, c * P:(c + 1) * P], ehid[u][:, c * P:(c + 1) * P], ident[:])
                mm.then_inc(s_ehTp, 1)

            def down(k, u):
                e = pe.value_load(tile_e[0:1, bass.ds(k, 1)], min_val=0, max_val=E - 1)
                pe.wait_ge(s_ehT, k + 2)
                pe.wait_ge(s_eout, k + 1)
                for c in range(FC):
                    mm = pe.matmul(ps[:, 6, 0:D], ehT[u][:, c, :], rdT[:, bass.ds(e, 1), c, :].squeeze(1),
                                   start=(c == 0), stop=(c == FC - 1))
                mm.then_inc(s_ey, 1)

            turn_in(0, 0)
            gate_up(0, 0)
            turn_in(1, 1)
            with pe.Fori(0, LAST // 2) as i:
                for u in range(2):
                    gate_up(2 * i + u + 1, 1 - u)
                    turn_hidden(2 * i + u, u)
                    turn_in(2 * i + u + 2, u)
                    down(2 * i + u, u)
            for k in range(LAST, NTILE):
                if k + 1 < NTILE:
                    gate_up(k + 1, (k + 1) % 2)
                turn_hidden(k, k % 2)
                if k + 2 < NTILE:
                    turn_in(k + 2, k % 2)
                down(k, k % 2)

        def routed_scalar(act):
            def silu(k, u):
                act.wait_ge(s_egu, k + 1)
                wait(act, s_ehid, k)
                act.activation(esig[u][:], ps[:, 1 + 2 * u, :], ACT.Silu).then_inc(s_esig, 1)

            def take(k, u):
                act.wait_ge(s_ehTp, k + 1)
                wait(act, s_ey, k - 1)
                act.copy(ehT[u][:].rearrange("p c n -> p (c n)"), ps[:, 5, :]).then_inc(s_ehT, 1)

            act.sem_inc(s_ehT, 1)
            silu(0, 0)
            silu(1, 1)
            take(0, 0)
            silu(2, 0)
            take(1, 1)
            with act.Fori(1, LAST // 2) as i:
                for u in range(2):
                    silu(2 * i + u + 1, 1 - u)
                    take(2 * i + u, u)
            for k in range(LAST, NTILE):
                if k + 1 < NTILE:
                    silu(k + 1, (k + 1) % 2)
                take(k, k % 2)

        def routed_vector(dve):
            dve.wait_ge(s_x2, NCH + 1)
            dve.sem_inc(s_ehid, 1)
            dve.sem_inc(s_eout, 1)

            def weigh_rows(k, u, nth):
                dve.wait_ge(s_xs[u], 16 * (nth + 1))
                dve.tensor_scalar(xs[u][:, 0:D], xs[u][:, 0:D], xs[u][:, D:XW], None, ALU.mult).then_inc(s_xsc, 1)

            def rows_in(k, u):
                dve.wait_ge(s_xs_free, AHEAD + k + 1)
                wait(dve, s_egu, k - 1)
                dve.tensor_copy(xsT[u][:].rearrange("p c n -> p (c n)"), ps[:, 0, 0:D]).then_inc(s_xsT, 1)

            def hidden(k, u):
                dve.wait_ge(s_esig, k + 1)
                wait(dve, s_ehTp, k - 1)
                dve.tensor_tensor(ehid[u][:], esig[u][:], ps[:, 2 + 2 * u, :], ALU.mult).then_inc(s_ehid, 1)

            def take(k, u, nth):
                dve.wait_ge(s_ey, k + 1)
                dve.wait_ge(s_est[u], 16 * nth)
                dve.tensor_copy(eout[u][:], ps[:, 6, 0:D]).then_inc(s_eout, 1)

            weigh_rows(0, 0, 0)
            weigh_rows(1, 1, 0)
            rows_in(0, 0)
            rows_in(1, 1)
            weigh_rows(2, 0, 1)
            hidden(0, 0)
            hidden(1, 1)
            rows_in(2, 0)
            weigh_rows(3, 1, 1)
            take(0, 0, 0)
            hidden(2, 0)
            rows_in(3, 1)
            weigh_rows(4, 0, 2)
            take(1, 1, 0)
            with dve.Fori(1, LAST // 2) as i:
                for u in range(2):
                    hidden(2 * i + u + 1, 1 - u)
                    rows_in(2 * i + u + 2, u)
                    weigh_rows(2 * i + u + 3, 1 - u, i + 1 + u)
                    take(2 * i + u, u, i)
            for k in range(LAST, NTILE):
                if k + 1 < NTILE:
                    hidden(k + 1, (k + 1) % 2)
                if k + 2 < NTILE:
                    rows_in(k + 2, k % 2)
                take(k, k % 2, k // 2)

        def combine_sync(sp):
            for u in range(2):
                sp.wait_ge(s_x2st[u], 16 * NCH // 2)

            def load(i, u):
                sp.dma_start(cx[u][:], x2_dram[bass.ds((NG * i + u) * P, P), :]).then_inc(s_cx[u], 16)

            def store(i, u):
                sp.wait_ge(s_out, NG * i + u + 1)
                sp.dma_start(out[bass.ds((NG * i + u) * P, P), :], cx[u][:]).then_inc(s_ost[u], 16)

            for u in range(NG):
                load(0, u)
            with sp.Fori(1, NT // NG) as i:
                for u in range(NG):
                    store(i - 1, u)
                for u in range(NG):
                    sp.wait_ge(s_ost[u], 16 * i)
                    load(i, u)
            for u in range(NG):
                store(NT // NG - 1, u)
            for u in range(NG):
                sp.wait_ge(s_ost[u], 16 * (NT // NG))
                sp.wait_ge(s_est[u % 2], 16 * ((NTILE + 1 - u % 2) // 2))

        def combine_gpsimd(pool):
            for u in range(2):
                pool.wait_ge(s_est[u], 16 * ((NTILE + 1 - u) // 2))
            with pool.Fori(0, NT // NG) as i:
                for u in range(NG):
                    pool.wait_ge(s_ix, NG * i + u + 1)
                    hold(pool)
                    pool.indirect_dma_start(cy[u][:], None, ys_dram,
                                            bass.IndirectOffsetOnAxis(cix[u][:, 0:1], 0)).then_inc(s_cy[u], 16)

        def combine_vector(dve, step):
            def index(t, u):
                dve.tensor_copy(cix[u][:], slot[:, bass.ds(t, 1)]).then_inc(s_ix, 1)

            def tile(i, u):
                dve.wait_ge(s_cy[u], 16 * (i + 1))
                step(dve.tensor_tensor(cy[u][:], cy[u][:], rowmod[:, bass.ds(i // (NT // NG // B), 1), 3, :]
                                       .squeeze(1), ALU.mult))
                dve.wait_ge(s_cx[u], 16 * (i + 1))
                dve.tensor_tensor(cx[u][:], cx[u][:], cy[u][:], ALU.add).then_inc(s_out, 1)
                dve.wait_ge(s_out, NG * i + u + 1)

            for u in range(NG):
                index(u, u)
            with dve.Fori(0, NT // NG - 1) as i:
                step.turns(i, NG)
                for u in range(NG):
                    tile(i, u)
                    index(NG * (i + 1) + u, u)
            step.close(NT // NG - 1, NG)
            for u in range(NG):
                tile(NT // NG - 1, u)

        @block.sync
        def _(sp):
            setup_sync(sp)
            project_sync(sp)
            attend_sync(sp)
            merge_sync(sp)
            shared_sync(sp)
            routed_sync(sp)
            combine_sync(sp)

        @block.tensor
        def _(pe):
            setup_tensor(pe)
            project_tensor(pe)
            attend_tensor(pe)
            merge_tensor(pe)
            route_tensor(pe)
            shared_tensor(pe)
            routed_tensor(pe)

        @block.scalar
        def _(act):
            setup_scalar(act)
            project_scalar(act)
            attend_scalar(act)
            merge_scalar(act)
            route_scalar(act)
            shared_scalar(act)
            routed_scalar(act)

        @block.vector
        def _(dve):
            step = Steps(dve, s_chain["dve"])
            setup_vector(dve, step)
            project_vector(dve, step)
            gates_vector(dve, step)
            attend_vector(dve, step)
            merge_vector(dve, step)
            route_vector(dve, step)
            shared_vector(dve, step)
            routed_vector(dve)
            combine_vector(dve, step)

        @block.gpsimd
        def _(pool):
            step = Steps(pool, s_chain["pool"])
            project_gpsimd(pool)
            attend_gpsimd(pool, step)
            merge_gpsimd(pool, step)
            scatter_gpsimd(pool, step)
            combine_gpsimd(pool)


def laid_out(a):
    def by_rows(w):
        return w.T.reshape(-1, P, w.shape[0]).transpose(1, 0, 2)

    def experts(w):
        return w.transpose(2, 0, 1).reshape(-1, P, E, w.shape[1]).transpose(1, 2, 0, 3)

    names = ("q", "k", "v", "o")
    at = lambda n: a["L0_attn_" + n]
    ffn = lambda n: a["L0_ffn_" + n]
    return {
        "x": at("x").reshape(T, D),
        "cT": a["L0_c"].T.reshape(HALF, P, B).transpose(1, 0, 2),
        "wmod": a["L0_wmod"].reshape(HALF, P, 6 * D).transpose(1, 0, 2),
        "loA": np.stack([at("A" + n) for n in names], 1),
        "loB": np.stack([at("B" + n).T for n in names], 1),
        "wT": np.stack([by_rows(at("W" + n)) for n in names], 1),
        "bqk": np.concatenate([at("bq").reshape(HALF, P), at("bk").reshape(HALF, P)]).T,
        "bv": at("bv"),
        "bo": at("bo"),
        "gateT": by_rows(ffn("gate_w")),
        "wgT": by_rows(ffn("shared_gate")),
        "wuT": by_rows(ffn("shared_up")),
        "wdT": by_rows(ffn("shared_down")),
        "rgT": experts(ffn("r_gate")),
        "ruT": experts(ffn("r_up")),
        "rdT": experts(ffn("r_down")),
        "ident": np.eye(P, dtype=np.float32),
        "before": np.triu(np.ones((P, P), np.float32), 1),
        "iotas": np.tile(np.concatenate([np.arange(E) - E, P * np.arange(NT), np.arange(40)]), (P, 1)).astype(np.float32),
    }


def kernel(**inputs):
    import concourse.bacc as bacc
    from concourse.bass_utils import run_bass_kernel_spmd

    nc = bacc.Bacc("TRN2", target_bir_lowering=False, num_devices=1)
    arrays, io = {}, {}
    for name, a in laid_out({k: np.asarray(v) for k, v in inputs.items()}).items():
        a = np.ascontiguousarray(a)
        arrays["in_" + name] = a
        io[name] = nc.dram_tensor("in_" + name, a.shape, mybir.dt.from_np(a.dtype), kind="ExternalInput").ap()
    out = nc.dram_tensor("out", (T, D), F32, kind="ExternalOutput").ap()
    block_kernel(nc, io, out)
    got = run_bass_kernel_spmd(nc, [arrays], core_ids=[0]).results[0]["out"]
    return got.reshape(B, S, D)
```

```python
from contextlib import ExitStack

import numpy as np

import concourse.bass as bass
from concourse import mybir

F32 = mybir.dt.float32
BF16 = mybir.dt.bfloat16
U32 = mybir.dt.uint32
ALU = mybir.AluOpType
ACT = mybir.ActivationFunctionType
AX = mybir.AxisListType

P = 128
B, S, D = 2, 2048, 256
H, DH = 16, 16
R = 8
LORA_SCALE = 2.0
F, E = 512, 8
T = B * S
HALF = D // P
FC = F // P
CH = 512
NCH = T // CH
CPB = S // CH
TPC = CH // P
NT = T // P
KT = S // P
NH = B * H
ROWS = 6 * DH
NTILE = NT + E - 1
NSLOT = NTILE * P
ZERO = 3
EPS = 1e-5
AHEAD = 2
Q_RUNS = ((0, 0, 3), (3, 0, 2), (5, 0, 1))
K_RUNS = ((0, 0, 3), (3, 1, 2), (5, 2, 1))
UNITS = KT * CPB
LEAD = 4 * CPB
UQ = 2 * D // P
TAGS = 4
XW = D + TAGS
MAXIMA = UNITS + 1
RING = 3
NSC = 4
NX = 4
NB = 3


def wait(eng, semaphore, n):
    if not isinstance(n, int) or n > 0:
        eng.wait_ge(semaphore, n)


class Region:

    def __init__(self, nc, start, end):
        self.nc, self.at, self.end = nc, start, end

    def __call__(self, name, shape, dt=F32):
        size = int(np.prod(shape[1:])) * (2 if dt == BF16 else 4)
        t = self.nc.alloc_sbuf_tensor_at(name, shape, dt, offset=self.at)
        self.at += -(-size // 32) * 32
        assert self.at <= self.end, name
        return t


class Steps:

    def __init__(self, eng, sem):
        self.eng, self.sem, self.count, self.loop = eng, sem, 0, None

    def __call__(self, ins):
        ins.then_inc(self.sem, 1)
        self.count += 1
        self.eng.wait_ge(self.sem, self.count if self.loop is None else self.loop + self.count)

    def turns(self, index, per):
        self.loop, self.first = index * per, self.count

    def close(self, trips, per):
        assert self.count == self.first + per, (self.count, self.first, per)
        self.count, self.loop = self.first + trips * per, None


def buffers(name, shape, dt, region, n=2):
    return [region(f"{name}{i}", shape, dt) for i in range(n)]


def block_kernel(nc, io, out):
    with ExitStack() as ctx:
        def sem(name):
            return ctx.enter_context(nc.semaphore(name))

        ps = ctx.enter_context(nc.psum_tensor("ps", [P, 8, 512], F32))

        def scratch(name, shape, dt=F32):
            return nc.dram_tensor(name, shape, dt, kind="Internal").ap()

        qk_dram = scratch("qk_parts", (2, 3, B * D, S), BF16)
        o_dram = scratch("head_out", (NH, P, CH))
        rl_dram = scratch("inverse_sums", (NH * CPB, CH))
        h2_dram = scratch("h2_rows", (T, D))
        x1_dram = scratch("x1_rows", (T, D))
        x2_dram = scratch("x2_rows", (T + P, D))
        xs_dram = scratch("sorted_in", (NSLOT, XW))

        top = nc.sbuf_usable_end // 32 * 32
        expert_bytes = E * 4 * (2 * HALF * F + FC * D)
        experts_at = top - expert_bytes
        held = Region(nc, -(-nc.sbuf_base // 32) * 32, experts_at)
        ident = held("ident", [P, P])
        eps = held("eps", [P, 1])
        woT = held("woT", [P, HALF, D])
        gateT = held("gateT", [P, HALF, E])
        rowmod = held("rowmod", [P, B, 4, D])
        gbo = held("gbo", [P, B, D])
        wgT = held("wgT", [P, HALF, F])
        wuT = held("wuT", [P, HALF, F])
        wdT = held("wdT", [P, FC, D])
        ones = held("ones", [P, P])
        zero_row = held("zero_row", [P, XW])
        sums = held("sums", [P, CH])
        tags = held("tags", [P, NT + 1, TAGS])
        iotas = held("iotas", [P, E + NT + NTILE])
        stage_at = held.at

        r = Region(nc, stage_at, experts_at)
        v_all = r("v_all", [P, NT, D])
        order = ((NH - 2) % NB, (NH - 3) % NB, (NH - 1) % NB)
        vs = {n: r(f"vs{n}", [P, KT, 32]) for n in order[:2]}
        qs, ks = {}, {}
        for n in order:
            qs[n], ks[n] = r(f"qs{n}", [P, S], BF16), r(f"ks{n}", [P, S], BF16)
        vs[order[2]] = r(f"vs{order[2]}", [P, KT, 32])
        mb = buffers("mb", [KT, 2, P], BF16, r, NB)
        head_out = r("head_out_sb", [P, CH])
        prob_at = r.at
        prob = r("prob", [P, 2, S])
        mx = r("mx", [P, KT, CPB])
        mneg = r("mneg", [P, KT])

        r = Region(nc, experts_at, top)
        cT = r("cT", [P, HALF, B])
        cS = r("cS", [P, HALF, B])
        cB = r("cB", [P, HALF, B, P])
        wmod = r("wmod", [P, HALF, 6 * D])
        loA = r("loA", [R, 4, D])
        loB = r("loB", [R, 4, D])
        wT = r("wT", [P, 4, HALF, D])
        wqkv = r("wqkv", [P, 3, HALF, D])
        bqk = r("bqk", [P, 4])
        bqk_in = r("bqk_in", [P, 4])
        bv_row = r("bv_row", [P, D])
        bo_row = r("bo_row", [P, D])
        colmod = r("colmod", [P, 2, HALF, B])
        gtmp = r("gtmp", [P, 2, B, 2, D])
        x_t = buffers("x_t", [P, TPC, D], F32, r)
        xn = buffers("xn", [P, TPC, D], F32, r)
        hT = buffers("hT", [P, HALF, CH], F32, r)
        qf = buffers("qf", [P, CH], F32, r, UQ)
        parts = buffers("parts", [P, 3, CH], BF16, r, UQ)
        stats = r("stats", [P, TPC, 6])
        mv = r("mv", [P, TPC, 2])
        std = r("std", [P, TPC])

        rest = buffers("rest", [P, CH], F32, Region(nc, prob_at, experts_at), UQ)

        r = Region(nc, experts_at, top)
        rgT = r("rgT", [P, E, HALF, F])
        ruT = r("ruT", [P, E, HALF, F])
        rdT = r("rdT", [P, E, FC, D])

        late_at = experts_at - 4 * (P + NT * E)
        r = Region(nc, late_at, experts_at)
        before = r("before", [P, P])
        logits = r("logits", [P, NT, E])

        r = Region(nc, stage_at, late_at)
        h2T = r("h2T", [P, HALF, T])
        after_h2T = r.at
        o_in, l_in, x_in = [], [], []
        for u in range(2):
            o_in.append(r(f"o_in{u}", [P, HALF, CH]))
            l_in.append(r(f"l_in{u}", [P, HALF, CH]))
            x_in.append(r(f"x_in{u}", [P, TPC, D]))
        x1 = buffers("x1", [P, TPC, D], F32, r)
        h2 = buffers("h2", [P, TPC, D], F32, r)
        h2Tc = buffers("h2Tc", [P, HALF, CH], F32, r)
        stats2 = r("stats2", [P, TPC, 6])
        mv2 = r("mv2", [P, TPC, 2])
        std2 = r("std2", [P, TPC])

        r = Region(nc, after_h2T, late_at)
        sgate = buffers("sgate", [P, CH], F32, r)
        hid = buffers("hid", [P, FC, CH], F32, r)
        onehot = r("onehot", [P, NT, E])
        ra = r("ra", [P, NT, E])
        rb = r("rb", [P, NT, E])
        rt = r("rt", [P, NT, E])
        rmax = r("rmax", [P, NT])
        rix = r("rix", [P, NT])
        slot = r("slot", [P, NT], U32)
        cmp8 = r("cmp8", [P, E, NT])
        segs = r("segs", [P, 4, E])
        tcmp = r("tcmp", [P, NTILE, E])
        tile_f = r("tile_f", [P, NTILE])
        tile_e = r("tile_e", [P, NTILE], U32)
        sc_x = buffers("sc_x", [P, XW], F32, r, NSC)
        sc_ix = buffers("sc_ix", [P, 1], U32, r, NSC)
        ymod = r("ymod", [P, TPC, D])
        xr = buffers("xr", [P, TPC, D], F32, r)
        xs = buffers("xs", [P, XW], F32, r, NX)

        r = Region(nc, stage_at, experts_at)
        xsT = buffers("xsT", [P, HALF, P], F32, r)
        esig = buffers("esig", [P, F], F32, r)
        ehid = buffers("ehid", [P, F], F32, r)
        ehT = buffers("ehT", [P, FC, P], F32, r)
        eout = buffers("eout", [P, D], F32, r, NX)
        x2_in = buffers("x2_in", [P, D], F32, r, NX)
        cix = buffers("cix", [P, 1], U32, r, NX)
        gsel = buffers("gsel", [P, D], F32, r)
        assert r.at <= after_h2T

        block = ctx.enter_context(nc.Block())

        s_chain = {e: sem(f"chain_{e}") for e in ("dve", "pool")}
        s_hold = sem("s_hold")
        s_eps = sem("s_eps")
        s_const = sem("s_const")
        s_bv = sem("s_bv")
        s_wT = sem("s_wT")
        s_wmod = sem("s_wmod")
        s_wrow = sem("s_wrow")
        s_late = sem("s_late")
        s_shared = sem("s_shared")
        s_csilu = sem("s_csilu")
        s_crow = sem("s_crow")
        s_lora = sem("s_lora")
        s_weff = sem("s_weff")
        s_mrow = sem("s_mrow")
        s_mcol = sem("s_mcol")
        s_colmod = sem("s_colmod")
        s_mod = sem("s_mod")
        s_gates = sem("s_gates")
        s_x = [sem(f"s_xload{u}") for u in range(2)]
        s_var = sem("s_var")
        s_std = sem("s_std")
        s_norm = sem("s_norm")
        s_xn_free = sem("s_xn_free")
        s_hT = sem("s_hT")
        s_unit = sem("s_unit")
        s_qbank_free = sem("s_qbank_free")
        s_rest = sem("s_rest")
        s_mid = sem("s_mid")
        s_qf_free = sem("s_qf_free")
        s_parts = [sem(f"s_parts{o}") for o in range(UQ)]
        s_v = sem("s_v")
        s_vbank_free = sem("s_vbank_free")
        s_stack = [sem(f"s_stack{p}") for p in range(NB)]
        s_rows = sem("s_rows")
        s_ones = sem("s_ones")
        s_vs = sem("s_vs")
        s_max = sem("s_max")
        s_ring = sem("s_ring")
        s_neg = sem("s_neg")
        s_mrows = [sem(f"s_mrows{p}") for p in range(NB)]
        s_score = sem("s_score")
        s_exp_free = sem("s_exp_free")
        s_prob_free = sem("s_prob_free")
        s_head = sem("s_head")
        s_hstore = sem("s_hstore")
        s_expert = sem("s_expert")
        s_zero = sem("s_zero")
        s_sums = sem("s_sums")
        s_rl = sem("s_rl")
        s_rlst = sem("s_rlst")
        s_oin = [sem(f"s_oin{u}") for u in range(2)]
        s_xin = [sem(f"s_xin{u}") for u in range(2)]
        s_on = sem("s_on")
        s_op = sem("s_op")
        s_xb = sem("s_xb")
        s_x1 = sem("s_x1")
        s_x1st = [sem(f"s_x1st{u}") for u in range(2)]
        s_var2 = sem("s_var2")
        s_std2 = sem("s_std2")
        s_n2 = sem("s_n2")
        s_h2 = sem("s_h2")
        s_h2st = [sem(f"s_h2st{u}") for u in range(2)]
        s_h2_free = sem("s_h2_free")
        s_h2T = sem("s_h2T")
        s_lgp = sem("s_lgp")
        s_lg = sem("s_lg")
        s_before = sem("s_before")
        s_oh = sem("s_oh")
        s_rank = sem("s_rank")
        s_route = sem("s_route")
        s_sig = sem("s_sig")
        s_scx = [sem(f"s_scx{u}") for u in range(NSC)]
        s_scat = [sem(f"s_scat{u}") for u in range(NSC)]
        s_xr = [sem(f"s_xr{u}") for u in range(2)]
        s_gu = sem("s_gu")
        s_silu = sem("s_silu")
        s_gu_free = sem("s_gu_free")
        s_y = sem("s_y")
        s_x2 = sem("s_x2")
        s_x2st = [sem(f"s_x2st{u}") for u in range(2)]
        s_xs = [sem(f"s_xs{u}") for u in range(NX)]
        s_xsc = sem("s_xsc")
        s_xs_free = sem("s_xs_free")
        s_xsT = sem("s_xsT")
        s_egate = sem("s_egate")
        s_eup = sem("s_eup")
        s_esig = sem("s_esig")
        s_ehid = sem("s_ehid")
        s_ehTp = sem("s_ehTp")
        s_ehT = sem("s_ehT")
        s_ey = sem("s_ey")
        s_eout = sem("s_eout")
        s_sel = sem("s_sel")
        s_ix = sem("s_ix")
        s_x2in = [sem(f"s_x2in{u}") for u in range(NX)]
        s_out = sem("s_out")
        s_ost = [sem(f"s_ost{u}") for u in range(NX)]

        def hold(eng):
            eng.sem_inc(s_hold, 1)

        first_loads = [(loA, io["loA"]), (loB, io["loB"]), (cT, io["cT"]), (ident, io["ident"]),
                       (bqk_in, io["bqk"]), (bv_row, io["bv"].partition_broadcast(P))]
        late_loads = [(bo_row, io["bo"].partition_broadcast(P)), (gateT, io["gateT"]), (tags, io["tags"]),
                      (iotas, io["iotas"])]
        rows = lambda dram, t, n: dram[bass.ds(t * P, n * P), :].rearrange("(t p) d -> p t d", p=P)

        def root(act, g):
            act.wait_ge(s_var, g + 1)
            act.activation(std[:], mv[:, :, 1], ACT.Sqrt, bias=eps[:, 0:1]).then_inc(s_std, 1)

        def moments(dve, step, g, u, nth):
            dve.wait_ge(s_x[u], 16 * (nth + 1))
            for t in range(TPC):
                st = dve.bn_stats(stats[:, t, :], x_t[u][:, t, :])
            step(st)
            hold(dve)
            for t in range(TPC):
                a = dve.bn_aggr(mv[:, t, :], stats[:, t, :])
            a.then_inc(s_var, 1)

        def normalize(dve, step, g, u):
            dve.wait_ge(s_std, g + 1)
            step(dve.reciprocal(std[:], std[:]))
            wait(dve, s_xn_free, g - 1)
            for t in range(TPC):
                a = dve.tensor_scalar(xn[u][:, t, :], x_t[u][:, t, :], mv[:, t, 0:1], std[:, t:t + 1],
                                      ALU.subtract, ALU.mult)
            a.then_inc(s_norm, 1)

        def setup_sync(sp):
            for dst, src in first_loads[:-1]:
                sp.dma_start(dst[:], src).then_inc(s_const, 16)
            sp.dma_start(wT[:], io["wT"]).then_inc(s_wT, 16)
            sp.dma_start(x_t[1][:], rows(io["x"], TPC, TPC)).then_inc(s_x[1], 16)
            dst, src = first_loads[-1]
            sp.dma_start(dst[:], src).then_inc(s_bv, 16)
            sp.wait_ge(s_norm, 1)
            sp.dma_start(x_t[0][:], rows(io["x"], 2 * TPC, TPC)).then_inc(s_x[0], 16)
            sp.dma_start(wmod[:, :, 512:], io["wmod"][:, :, 512:]).then_inc(s_wrow, 16)

        def setup_scalar(act):
            act.dma_start(x_t[0][:], rows(io["x"], 0, TPC)).then_inc(s_x[0], 16)
            act.dma_start(wmod[:, :, 0:512], io["wmod"][:, :, 0:512]).then_inc(s_wmod, 16)
            act.wait_ge(s_eps, 1)
            root(act, 0)
            act.wait_ge(s_const, 16 * (len(first_loads) - 1))
            act.activation(cS[:], cT[:], ACT.Silu).then_inc(s_csilu, 1)
            root(act, 1)

        def setup_tensor(pe):
            pe.wait_ge(s_const, 16 * (len(first_loads) - 1))
            for m in range(4):
                for k in range(HALF):
                    mm = pe.matmul(ps[:, 4 + m, k * D:(k + 1) * D], loA[:, m, k * P:(k + 1) * P], loB[:, m, :],
                                   start=True, stop=True)
            mm.then_inc(s_lora, 1)
            pe.wait_ge(s_wmod, 16)
            pe.wait_ge(s_csilu, 1)
            for v in range(2 * HALF):
                for k in range(HALF):
                    mm = pe.matmul(ps[:, 2, v * B:(v + 1) * B], wmod[:, k, v * P:(v + 1) * P], cS[:, k, :],
                                   start=(k == 0), stop=(k == 1))
            mm.then_inc(s_mcol, 1)

        def setup_vector(dve, step):
            step(dve.memset(eps[:], EPS))
            dve.memset(ones[:], 1.0)
            step(dve.memset(zero_row[:, 0:D], 0.0))
            dve.sem_inc(s_eps, 1)
            moments(dve, step, 0, 0, 0)
            normalize(dve, step, 0, 0)
            dve.wait_ge(s_const, 16 * (len(first_loads) - 1))
            dve.tensor_scalar(bqk[:, 0:2], bqk_in[:, 0:2], 0.25, None, ALU.mult)
            dve.tensor_copy(bqk[:, 2:4], bqk_in[:, 2:4])
            dve.wait_ge(s_wT, 16)
            dve.wait_ge(s_lora, 1)
            for m in range(4):
                dst = wqkv[:, m] if m < 3 else woT[:]
                w = dve.scalar_tensor_tensor(dst.rearrange("p k d -> p (k d)"), ps[:, 4 + m, :], LORA_SCALE,
                                             wT[:, m].rearrange("p k d -> p (k d)"), ALU.mult, ALU.add)
            w.then_inc(s_weff, 1)
            dve.wait_ge(s_mcol, 1)
            step(dve.tensor_copy(colmod[:].rearrange("p v k b -> p (v k b)"), ps[:, 2, 0:2 * HALF * B]))
            dve.tensor_scalar(colmod[:, 1], colmod[:, 1], 1.0, None, ALU.add).then_inc(s_colmod, 1)
            moments(dve, step, 1, 1, 0)
            normalize(dve, step, 1, 1)
            dve.wait_ge(s_csilu, 1)
            dve.tensor_copy(cB[:], cS[:].unsqueeze(3).to_broadcast([P, HALF, B, P])).then_inc(s_crow, 1)

        def gates(pool, step):
            pool.wait_ge(s_mod, 4)
            step(pool.tensor_scalar(rowmod[:, :, 2, :], rowmod[:, :, 2, :], 1.0, None, ALU.add))
            for v in (0, 3):
                g, mag, sign = rowmod[:, :, v, :], gtmp[:, 0, :, v // 3, :], gtmp[:, 1, :, v // 3, :]
                step(pool.tensor_scalar(sign, g, 0.0, 2.0, ALU.is_ge, ALU.mult))
                step(pool.tensor_scalar(sign, sign, -1.0, None, ALU.add))
                step(pool.tensor_tensor(mag, sign, g, ALU.mult))
                step(pool.tensor_scalar(mag, mag, 0.25, None, ALU.max))
                step(pool.tensor_tensor(g, sign, mag, ALU.mult))
            pool.tensor_tensor(gbo[:], rowmod[:, :, 0, :], bo_row[:].unsqueeze(1).to_broadcast([P, B, D]),
                               ALU.mult).then_inc(s_gates, 1)
            pool.wait_ge(s_gates, 1)

        def project_sync(sp):
            def load(g, u):
                sp.dma_start(x_t[u][:], rows(io["x"], g * TPC, TPC)).then_inc(s_x[u], 16)

            def store(g, b, j):
                for o in range(UQ):
                    half = o % 2
                    sp.wait_ge(s_qf_free, UQ + UQ * g + o + 1)
                    dst = qk_dram[o // 2].rearrange("s (b c) t -> c s b t", b=B)
                    sp.dma_start(dst[half * P:(half + 1) * P, :, bass.ds(b, 1), bass.ds(j * CH, CH)].squeeze(2),
                                 parts[o][:]).then_inc(s_parts[o], 16)

            with sp.Fori(0, CPB // 2) as i:
                for u in range(2):
                    g = 2 * i + u
                    sp.wait_ge(s_norm, g + 2)
                    load(g + 3, 1 - u)
                    store(g, 0, g)
            sp.wait_ge(s_norm, NCH - 2)
            load(NCH - 1, 1)
            for o in range(UQ):
                sp.wait_ge(s_parts[o], 16 * (CPB + 1))
            sp.wait_ge(s_rows, 1)
            stack(sp, (0, 0))
            store(CPB, 1, 0)
            stack(sp, (0, 1))
            for dst, src in late_loads:
                sp.dma_start(dst[:], src).then_inc(s_late, 16)
            store(CPB + 1, 1, 1)
            stack(sp, (0, 2))
            for dst, name in ((wgT, "wgT"), (wuT, "wuT"), (wdT, "wdT")):
                sp.dma_start(dst[:], io[name]).then_inc(s_shared, 16)
            for g in range(CPB + 2, NCH):
                store(g, 1, g % CPB)

        BESIDE = {CPB: 4, CPB + 1: 16, CPB + 2: 22, CPB + 3: UNITS - 42}

        def units_beside(g):
            if g not in BESIDE:
                return iter(()), [0] * 7
            first = sum(n for c, n in BESIDE.items() if c < g)
            n = BESIDE[g]
            share = [0, 0, 0, 0, 0, 0, n] if g == CPB else [n * (i + 1) // 7 - n * i // 7 for i in range(7)]
            return iter(range(first, first + n)), share

        def project_tensor(pe):
            pe.sem_inc(s_v, 1)
            pe.sem_inc(s_max, 1)

            def turn(g, u):
                pe.wait_ge(s_norm, g + 1)
                wait(pe, s_hT, g)
                for k in range(HALF):
                    for t in range(TPC):
                        mm = pe.transpose(ps[:, k, t * P:(t + 1) * P], xn[u][:, t, k * P:(k + 1) * P], ident[:])
                mm.then_inc(s_xn_free, 1)

            def qk(g, u, o):
                pe.wait_ge(s_qbank_free, UQ * g + o + 1)
                for k in range(HALF):
                    mm = pe.matmul(ps[:, 2 + o % 2, :], wqkv[:, o // 2, k, (o % 2) * P:(o % 2 + 1) * P],
                                   hT[u][:, k, :], start=(k == 0), stop=(k == 1))
                mm.then_inc(s_unit, 1)

            def v(g, u, half):
                pe.wait_ge(s_vbank_free, 2 * g + half + 1)
                for c in range(2):
                    t = 2 * half + c
                    for k in range(HALF):
                        mm = pe.matmul(ps[:, 7, c * D:(c + 1) * D], hT[u][:, k, t * P:(t + 1) * P],
                                       wqkv[:, 2, k, :], start=(k == 0), stop=(k == 1))
                mm.then_inc(s_v, 1)

            def chunk(g, u):
                static = isinstance(g, int)
                units, share = units_beside(g if static else None)

                def beside(step):
                    for _ in range(share[step]):
                        max_unit(pe, (0, 0), next(units))

                if not static or g + 1 < NCH:
                    turn(g + 1, 1 - u)
                beside(0)
                pe.wait_ge(s_hT, g + 1)
                for step, (work, n) in enumerate(((qk, 0), (qk, 1), (v, 0), (qk, 2), (qk, 3), (v, 1))):
                    work(g, u, n)
                    beside(step + 1)

            turn(0, 0)
            pe.wait_ge(s_weff, 1)
            with pe.Fori(0, CPB // 2) as i:
                for u in range(2):
                    chunk(2 * i + u, u)
            for g in range(CPB, NCH):
                chunk(g, g % 2)

        def project_scalar(act):
            act.sem_inc(s_qbank_free, AHEAD)
            for o in range(UQ):
                act.sem_inc(s_parts[o], 16)
            act.wait_ge(s_colmod, 1)

            def modulate(g, u, b):
                act.wait_ge(s_xn_free, g + 1)
                wait(act, s_v, 1 + 2 * (g - 1))
                for k in range(HALF):
                    a = act.activation(hT[u][:, k, :], ps[:, k, :], ACT.Identity,
                                       bias=colmod[:, 0, k, bass.ds(b, 1)], scale=colmod[:, 1, k, bass.ds(b, 1)])
                a.then_inc(s_hT, 1)

            def take(g, o):
                bank, scale = 2 + o % 2, 0.25 if o < 2 else 1.0
                act.wait_ge(s_unit, UQ * g + o + 1)
                act.wait_ge(s_qf_free, UQ * g + o + 1)
                act.activation(qf[o][:], ps[:, bank, :], ACT.Identity, bias=bqk[:, o:o + 1], scale=scale)
                act.wait_ge(s_parts[o], 16 * (g + 1))
                act.activation(parts[o][:, 0, :], ps[:, bank, :], ACT.Identity, bias=bqk[:, o:o + 1],
                               scale=scale).then_inc(s_qbank_free, 1)

            def middle(g, o):
                act.wait_ge(s_rest, UQ * g + o + 1)
                act.copy(parts[o][:, 1, :], rest[o][:]).then_inc(s_mid, 1)

            def chunk(g, u, b, more, more2):
                if more:
                    modulate(g + 1, 1 - u, b)
                take(g, 0)
                take(g, 1)
                middle(g, 0)
                if more2:
                    root(act, g + 2)
                take(g, 2)
                middle(g, 1)
                take(g, 3)
                middle(g, 2)
                middle(g, 3)

            modulate(0, 0, 0)
            with act.Fori(0, CPB // 2) as i:
                for u in range(2):
                    chunk(2 * i + u, u, (2 * i + u + 1) // CPB, True, True)
            for g in range(CPB, NCH):
                chunk(g, g % 2, 1, g + 1 < NCH, g + 2 < NCH)

        def project_vector(dve, step):
            dve.sem_inc(s_vbank_free, 1)
            dve.wait_ge(s_bv, 16)
            dve.sem_inc(s_ring, 1)

            def v(g, half):
                dve.wait_ge(s_v, 2 * g + half + 2)
                dve.tensor_tensor(v_all[:, bass.ds(TPC * g + 2 * half, 2), :],
                                  ps[:, 7, :].rearrange("p (c d) -> p c d", d=D),
                                  bv_row[:].unsqueeze(1).to_broadcast([P, 2, D]), ALU.add).then_inc(s_vbank_free, 1)

            def chunk(g, u, nth, more2):
                units, share = units_beside(g if isinstance(g, int) else None)

                def beside(*steps):
                    for s in steps:
                        for _ in range(share[s]):
                            reduce_unit(dve, (0, 0), next(units))

                if more2:
                    moments(dve, step, g + 2, u, nth + 1)
                beside(0, 1, 2)
                v(g, 0)
                beside(3)
                if more2:
                    normalize(dve, step, g + 2, u)
                beside(4, 5)
                v(g, 1)
                beside(6)

            with dve.Fori(0, CPB // 2) as i:
                step.turns(i, 4)
                for u in range(2):
                    chunk(2 * i + u, u, i, True)
            step.close(CPB // 2, 4)
            for g in range(CPB, NCH):
                chunk(g, g % 2, g // 2, g + 2 < NCH)

        def project_gpsimd(pool, step):
            for p in range(NB):
                step(pool.memset(ks[p][ROWS:ROWS + 2, :], 1.0))
                step(pool.memset(vs[p][:], 0.0))
                step(pool.memset(vs[p][:, :, DH:DH + 1], 1.0))
            pool.sem_inc(s_rows, 1)
            pool.sem_inc(s_qf_free, UQ)

            def remainder(g, o):
                pool.wait_ge(s_qbank_free, AHEAD + UQ * g + o + 1)
                pool.tensor_tensor(rest[o][:], qf[o][:], parts[o][:, 0, :], ALU.subtract).then_inc(s_rest, 1)

            def last_part(g, o):
                pool.wait_ge(s_mid, UQ * g + o + 1)
                pool.tensor_tensor(parts[o][:, 2, :], rest[o][:], parts[o][:, 1, :],
                                   ALU.subtract).then_inc(s_qf_free, 1)

            with pool.Fori(0, NCH) as g:
                remainder(g, 0)
                remainder(g, 1)
                last_part(g, 0)
                remainder(g, 2)
                last_part(g, 1)
                remainder(g, 3)
                last_part(g, 2)
                last_part(g, 3)

        num = lambda h: NB * h[0] + h[1]
        nth = lambda h: h[0] + h[1] // NB
        buf = lambda h: h[1] % NB
        plus = lambda h, k: (h[0], h[1] + k)

        def sum_halves(b):
            n, w = P // 2, CH // 2
            pairs = slice(b * n, (b + 1) * n)
            return [(sums[h * n:(h + 1) * n, b * w:(b + 1) * w], pairs, slice(h * w, (h + 1) * w))
                    for h in range(2)]

        def fetch_sums(sp, b):
            sp.wait_ge(s_hstore, 16 * (H * (b + 1) + 1))
            for dst, pairs, cols in sum_halves(b):
                sp.dma_start(dst, o_dram.rearrange("n (j r) t -> (n j) r t", r=32)[pairs, DH, cols]
                             ).then_inc(s_sums, 16)

        def store_inverse(sp, b):
            sp.wait_ge(s_rl, b + 1)
            for src, pairs, cols in sum_halves(b):
                sp.dma_start(rl_dram[pairs, cols], src).then_inc(s_rlst, 16)

        def invert(dve, b):
            mine = sums[:, b * CH // 2:(b + 1) * CH // 2]
            dve.wait_ge(s_sums, 32 * (b + 1))
            dve.reciprocal(mine, mine).then_inc(s_rl, 1)

        def stack(sp, h):
            p = buf(h)
            for which, runs, tile in ((0, Q_RUNS, qs[p]), (1, K_RUNS, ks[p])):
                for group, part, n in runs:
                    src = qk_dram[which]
                    if which == 0:
                        src = src[part:part + n]
                    else:
                        src = src[part:part + 1].to_broadcast([n, B * D, S])
                    sp.dma_start(tile[group * DH:(group + n) * DH, :],
                                 src[:, bass.ds(num(h) * DH, DH), :]).then_inc(s_stack[p], 16)

        def attend_sync(sp):
            for o in range(UQ):
                sp.wait_ge(s_parts[o], 16 * (NCH + 1))

            def maxima(h, last=False):
                p = buf(h)
                sp.wait_ge(s_ring, MAXIMA * (num(h) + 1) + (1 if last else 2))
                for m in range(2):
                    sp.dma_start(qs[p][ROWS + m:ROWS + m + 1, :].rearrange("a (t c) -> a t c", t=KT),
                                 mb[p][:, m, :]).then_inc(s_mrows[p], 16)

            def head_store(h):
                sp.wait_ge(s_head, num(h) + 1)
                sp.dma_start(o_dram[bass.ds(num(h), 1)].squeeze(0), head_out[:]).then_inc(s_hstore, 16)

            def turn(h, last):
                if last >= 2:
                    sp.wait_ge(s_score, 2 * KT * num(h))
                    stack(sp, plus(h, 2))
                head_store(plus(h, -1))
                if last >= 1:
                    maxima(plus(h, 1), last == 1)
                if last == 1:
                    fetch_sums(sp, 0)
                    store_inverse(sp, 0)

            maxima((0, 0))
            maxima((0, 1))
            trips = (NH - 5) // NB
            with sp.Fori(0, trips) as i:
                for u in range(NB):
                    turn((i, 1 + u), 2)
            for n in range(1 + NB * trips, NH):
                turn((0, n), NH - 1 - n)
            sp.wait_ge(s_rlst, 32)
            sp.wait_ge(s_prob_free, AHEAD + KT * (NH - 1))
            merge_load(sp, 0, 0, 0, 0)
            merge_load_x(sp, 0, 0)
            merge_load(sp, 1, 1, 0, 1)
            head_store((0, NH - 1))

        item = lambda k: k + (k > 0)
        first_head = lambda h: isinstance(h[0], int) and num(h) == 0
        ring_bank = lambda k: 4 + item(k) % RING
        TURNED_BANK = 4 + 1

        def max_unit(pe, h, k):
            p, t, c = buf(h), k // CPB, k % CPB
            if k == 0:
                pe.wait_ge(s_stack[p], 96 * (nth(h) + 1))
            if k < 2:
                wait(pe, s_ring, MAXIMA * num(h) - (1 if k == 0 else 2))
            elif k == 2 and first_head(h):
                pe.wait_ge(s_ring, 2)
            else:
                pe.wait_ge(s_ring, MAXIMA * num(h) + item(k) - RING + 1)
            pe.matmul(ps[:, ring_bank(k), :], qs[p][0:ROWS, t * P:(t + 1) * P],
                      ks[p][0:ROWS, c * CH:(c + 1) * CH], start=True, stop=True).then_inc(s_max, 1)

        def attend_tensor(pe):
            pe.sem_inc(s_prob_free, AHEAD)
            pe.wait_ge(s_qbank_free, AHEAD + UQ * NCH)
            pe.wait_ge(s_vbank_free, 1 + 2 * NCH)

            unit = lambda h, k: max_unit(pe, h, k)

            def turn_maxima(h):
                pe.wait_ge(s_neg, num(h) + 1)
                pe.transpose(ps[0:KT, TURNED_BANK, 0:P], mneg[:, :], ident[:]).then_inc(s_max, 1)

            def scores(h, kt, half):
                p = buf(h)
                if kt == 0 and half == 0:
                    pe.wait_ge(s_mrows[p], 32 * (nth(h) + 2))
                pe.wait_ge(s_exp_free, 2 * KT * num(h) + 2 * kt + half + 1)
                for c in range(2):
                    q = (2 * half + c) * CH
                    mm = pe.matmul(ps[:, 2 * half + c, :], ks[p][0:ROWS + 2, kt * P:(kt + 1) * P],
                                   qs[p][0:ROWS + 2, q:q + CH], start=True, stop=True)
                mm.then_inc(s_score, 1)

            def weigh(h, kt):
                if kt == 0:
                    pe.wait_ge(s_vs, num(h) + 1)
                    pe.wait_ge(s_head, num(h))
                pe.wait_ge(s_exp_free, AHEAD + 2 * KT * num(h) + 2 * kt + 2)
                for j in range(CPB):
                    mm = pe.matmul(ps[32 * j:32 * j + 32, 7, :], vs[buf(h)][:, kt, :],
                                   prob[:, kt % 2, j * CH:(j + 1) * CH], start=(kt == 0), stop=(kt == KT - 1))
                mm.then_inc(s_prob_free, 1)

            def turn(h, after):
                for kt in range(1, KT + 1 if after else KT):
                    s = (h, kt) if kt < KT else (plus(h, 1), 0)
                    first, who = LEAD + CPB * (kt - 1), plus(h, 1)
                    turns = first == UNITS and after >= 1
                    if first >= UNITS:
                        first, who = first - UNITS, plus(h, 2)
                    units = [(who, first + c) for c in range(CPB)]
                    if after < (1 if who == plus(h, 1) else 2):
                        units = []
                    scores(*s, 0)
                    for k in units[:1]:
                        unit(*k)
                    scores(*s, 1)
                    if turns:
                        turn_maxima(plus(h, 1))
                    for k in units[1:2 if turns else 3]:
                        unit(*k)
                    weigh(h, kt - 1)
                    for k in units[2 if turns else 3:]:
                        unit(*k)
                if not after:
                    weigh(h, KT - 1)

            pe.wait_ge(s_rows, 1)
            pe.wait_ge(s_crow, 1)
            pe.wait_ge(s_wrow, 16)
            unit((0, 1), 0)
            turn_maxima((0, 0))
            for b in range(B):
                for c in range(2):
                    for k in range(HALF):
                        mm = pe.matmul(ps[:, 2 * b + c, :], cB[:, k, b, :],
                                       wmod[:, k, (c + 1) * 512:(c + 2) * 512], start=(k == 0), stop=(k == 1))
                    mm.then_inc(s_mrow, 1)
                    for k in range(4 * (2 * b + c), 4 * (2 * b + c + 1)):
                        if k:
                            unit((0, 1), k)
            pe.wait_ge(s_mod, 4)
            for half in range(2):
                scores((0, 0), 0, half)
            with pe.Fori(0, (NH - 2) // NB) as i:
                for u in range(NB):
                    turn((i, u), 2)
            turn((0, NH - 2), 1)
            turn((0, NH - 1), 0)

        def reduce_unit(dve, h, k):
            dve.wait_ge(s_max, 2 if first_head(h) and k == 0 else MAXIMA * num(h) + item(k) + 1)
            dve.tensor_reduce(mx[:, k // CPB, k % CPB:k % CPB + 1], ps[:, ring_bank(k), :], AX.X,
                              ALU.max).then_inc(s_ring, 1)

        def attend_vector(dve, step):
            unit = lambda h, k: reduce_unit(dve, h, k)

            def head(h, last=False, units=range(1, UNITS)):
                following = MAXIMA * (num(h) + 1)
                for k in units:
                    unit(h, k)
                dve.wait_ge(s_ring, following)
                dve.tensor_reduce(mneg[:], mx[:], AX.X, ALU.max, negate=True).then_inc(s_neg, 1)
                if not last:
                    dve.wait_ge(s_neg, num(h) + 1)
                    unit(plus(h, 1), 0)
                dve.wait_ge(s_max, following + (1 if last else 2))
                dve.wait_ge(s_mrows[buf(h)], 32 * (nth(h) + 1))
                turned = ps[0:KT, TURNED_BANK, 0:P]
                step(dve.tensor_copy(mb[buf(h)][:, 0, :], turned))
                dve.tensor_tensor(mb[buf(h)][:, 1, :], turned, mb[buf(h)][:, 0, :],
                                  ALU.subtract).then_inc(s_ring, 1)

            for p in range(NB):
                dve.sem_inc(s_mrows[p], 32)
            head((0, 0), units=())
            with dve.Fori(0, (NH - 2) // NB) as i:
                step.turns(i, NB)
                for u in range(NB):
                    head((i, 1 + u))
            step.close((NH - 2) // NB, NB)
            for n in range(1 + (NH - 2) // NB * NB, NH - 1):
                head((0, n))
            head((0, NH - 1), last=True)
            invert(dve, 0)

        def attend_scalar(act):
            act.sem_inc(s_exp_free, AHEAD)
            act.sem_inc(s_hstore, 16)

            def exps(n, kt):
                act.wait_ge(s_prob_free, KT * n + kt + 1)
                for half in range(2):
                    act.wait_ge(s_score, 2 * KT * n + 2 * kt + half + 1)
                    act.activation(prob[:, kt % 2, half * 2 * CH:(half + 1) * 2 * CH],
                                   ps[:, 2 * half:2 * half + 2, :].rearrange("p c n -> p (c n)"),
                                   ACT.Exp).then_inc(s_exp_free, 1)

            def head_copy(n):
                act.wait_ge(s_prob_free, AHEAD + KT * (n + 1))
                act.wait_ge(s_hstore, 16 * (n + 1))
                act.copy(head_out[:], ps[:, 7, :]).then_inc(s_head, 1)

            for c in range(4):
                act.wait_ge(s_mrow, c + 1)
                act.copy(rowmod[:].rearrange("p b v d -> p (b v d)")[:, c * 512:(c + 1) * 512],
                         ps[:, c, :]).then_inc(s_mod, 1)
            for kt in range(KT):
                exps(0, kt)
            with act.Fori(1, NH) as n:
                for kt in range(KT):
                    exps(n, kt)
                    if kt == 0:
                        head_copy(n - 1)
            head_copy(NH - 1)

        def attend_gpsimd(pool, step):
            pool.wait_ge(s_late, 16 * len(late_loads))
            pool.tensor_copy(zero_row[:, D:XW], tags[:, NT, :]).then_inc(s_ones, 1)
            pool.wait_ge(s_ones, 1)
            pool.wait_ge(s_vbank_free, 1 + 2 * NCH)

            def stage(h):
                n = num(h)
                pool.tensor_copy(vs[buf(h)][:, :, 0:DH],
                                 v_all[:, bass.ds(n // H * KT, KT), bass.ds(n % H * DH, DH)]).then_inc(s_vs, 1)

            for n in range(NB):
                stage((0, n))
            for o in range(UQ):
                pool.wait_ge(s_parts[o], 16 * (NCH + 1))
            gates(pool, step)
            padded = xs_dram.rearrange("(n p) d -> p n d", p=P)

            def zero(piece):
                pool.dma_start(padded[:, bass.ds(piece * ZERO, ZERO), :],
                               zero_row[:].unsqueeze(1).to_broadcast([P, ZERO, XW])).then_inc(s_zero, 16)

            pool.dma_start(x2_dram[T:T + P, :], zero_row[:, 0:D]).then_inc(s_zero, 16)
            with pool.Fori(0, E) as i:
                for u in range(NB):
                    pool.wait_ge(s_prob_free, AHEAD + KT * (NB * i + u + 1))
                    stage((i, NB + u))
                    dst, name = ((rgT, "rgT"), (ruT, "ruT"), (rdT, "rdT"))[u]
                    pool.dma_start(dst[:, bass.ds(i, 1)], io[name][:, bass.ds(i, 1)]).then_inc(s_expert, 16)
                zero(i)
            for n in range(NB * (E + 1), NH):
                pool.wait_ge(s_prob_free, AHEAD + KT * (n - NB + 1))
                stage((0, n))
                zero(n - NB * (E + 1) + E)

        def merge_load(sp, g, u, b, j):
            for k in range(HALF):
                heads = o_dram[bass.ds(b * H + k * (H // HALF), H // HALF)]
                rows_of = heads[:, bass.ds(32 * j, 32), :]
                sp.dma_start(o_in[u][:, k, :], rows_of[:, 0:DH, :]).then_inc(s_oin[u], 16)
                inv = rl_dram.rearrange("(n j) t -> n j t", j=CPB)[bass.ds(b * H + k * (H // HALF), H // HALF)]
                sp.dma_start(l_in[u][:, k, :], inv[:, bass.ds(j, 1), :].to_broadcast(
                    [H // HALF, DH, CH])).then_inc(s_oin[u], 16)

        def merge_load_x(sp, g, u):
            sp.dma_start(x_in[u][:], rows(io["x"], g * TPC, TPC)).then_inc(s_xin[u], 16)

        def merge_sync(sp):
            load = lambda *chunk: merge_load(sp, *chunk)

            def following(g, u, b, j):
                sp.wait_ge(s_op, g + 1)
                load(g + 2, u, b, j)
                sp.wait_ge(s_x1, g + 1)
                merge_load_x(sp, g + 2, u)
                store(g, u)

            def store(g, u):
                sp.wait_ge(s_x1, g + 1)
                sp.dma_start(rows(x1_dram, g * TPC, TPC), x1[u][:]).then_inc(s_x1st[u], 16)

            sp.wait_ge(s_head, NH)
            merge_load_x(sp, 1, 1)
            sp.wait_ge(s_op, 1)
            load(2, 0, 0, 2)
            fetch_sums(sp, 1)
            sp.dma_start(before[:], io["before"]).then_inc(s_before, 16)
            sp.wait_ge(s_x1, 1)
            merge_load_x(sp, 2, 0)
            store(0, 0)
            following(1, 1, 0, 3)
            store_inverse(sp, 1)
            sp.wait_ge(s_rlst, 64)
            with sp.Fori(1, NCH // 2 - 1) as i:
                for u in range(2):
                    following(2 * i + u, u, (i + 1) // 2, (i + 1) % 2 * 2 + u)
            store(NCH - 2, 0)
            store(NCH - 1, 1)

        GATE_BANK = (4, 0)
        DOWN_BANK = (6, 2)
        RANK_BANK = 6

        def gate_up(pe, g, fc):
            bank = GATE_BANK[fc % 2]
            pe.wait_ge(s_gu_free, FC * g + fc + 1)
            for w, at in ((wgT, bank), (wuT, bank + 1)):
                for k in range(HALF):
                    mm = pe.matmul(ps[:, at, :], w[:, k, fc * P:(fc + 1) * P],
                                   h2T[:, k, bass.ds(g * CH, CH)], start=(k == 0), stop=(k == 1))
            mm.then_inc(s_gu, 1)

        def route_ranks(pe):
            pe.wait_ge(s_before, 16)
            pe.wait_ge(s_oh, 1)
            for k, counted in enumerate((before, ones)):
                mm = pe.matmul(ps[:, RANK_BANK, k * NT * E:(k + 1) * NT * E], counted[:],
                               onehot[:].rearrange("p t e -> p (t e)"), start=True, stop=True)
            mm.then_inc(s_rank, 1)

        OUT_BANK = (0, 5)

        def merge_tensor(pe):
            pe.wait_ge(s_late, 16 * len(late_loads))
            pe.wait_ge(s_exp_free, AHEAD + 2 * KT * NH)
            pe.wait_ge(s_ring, MAXIMA * NH + 1)

            def out_proj(g, u):
                pe.wait_ge(s_on, g + 1)
                wait(pe, s_x1, g - 1)
                for t in range(TPC):
                    for k in range(HALF):
                        mm = pe.matmul(ps[:, OUT_BANK[u] + t // 2, t % 2 * D:(t % 2 + 1) * D],
                                       o_in[u][:, k, t * P:(t + 1) * P],
                                       woT[:, k, :], start=(k == 0), stop=(k == 1))
                mm.then_inc(s_op, 1)

            def turn(g, u):
                pe.wait_ge(s_h2, g + 1)
                pe.wait_ge(s_h2T, g + 1)
                for k in range(HALF):
                    for t in range(TPC):
                        mm = pe.transpose(ps[:, 2 + k, t * P:(t + 1) * P], h2[u][:, t, k * P:(k + 1) * P], ident[:])
                mm.then_inc(s_h2_free, 1)

            def route_logits(g, u):
                pe.wait_ge(s_h2T, g + 2)
                pe.wait_ge(s_lg, g + 1)
                for t in range(TPC):
                    for k in range(HALF):
                        mm = pe.matmul(ps[:, 7, t * E:(t + 1) * E], h2Tc[u][:, k, t * P:(t + 1) * P],
                                       gateT[:, k, :], start=(k == 0), stop=(k == 1))
                mm.then_inc(s_lgp, 1)

            out_proj(0, 0)
            out_proj(1, 1)
            out_proj(2, 0)
            turn(0, 0)
            out_proj(3, 1)
            turn(1, 1)
            route_logits(0, 0)
            with pe.Fori(0, NCH // 2 - 2) as i:
                for u in range(2):
                    out_proj(2 * i + u + 4, u)
                    turn(2 * i + u + 2, u)
                    route_logits(2 * i + u + 1, 1 - u)
            pe.wait_ge(s_shared, 48)
            pe.sem_inc(s_gu_free, AHEAD)
            pe.wait_ge(s_x1, NCH)
            gate_up(pe, 0, 0)
            turn(NCH - 2, 0)
            route_logits(NCH - 3, 1)
            gate_up(pe, 0, 1)
            turn(NCH - 1, 1)
            route_logits(NCH - 2, 0)
            route_logits(NCH - 1, 1)
            gate_up(pe, 0, 2)
            route_ranks(pe)

        def merge_vector(dve, step):
            def divide(g, u, nth):
                dve.wait_ge(s_oin[u], 64 * (nth + 1))
                dve.tensor_tensor(o_in[u][:], o_in[u][:], l_in[u][:], ALU.mult).then_inc(s_on, 1)

            def residual(g, u, nth, b):
                dve.wait_ge(s_op, g + 1)
                dve.wait_ge(s_x1st[u], 16 * (nth + 1))
                step(dve.tensor_tensor(x1[u][:], ps[:, OUT_BANK[u]:OUT_BANK[u] + 2, :].rearrange(
                                           "p c (t d) -> p (c t) d", d=D),
                                       rowmod[:, bass.ds(b, 1), 0, :].to_broadcast([P, TPC, D]), ALU.mult))
                dve.wait_ge(s_xb, g + 1)
                dve.tensor_tensor(x1[u][:], x1[u][:], x_in[u][:], ALU.add).then_inc(s_x1, 1)
                dve.wait_ge(s_x1, g + 1)
                for t in range(TPC):
                    st = dve.bn_stats(stats2[:, t, :], x1[u][:, t, :])
                step(st)
                hold(dve)
                for t in range(TPC):
                    a = dve.bn_aggr(mv2[:, t, :], stats2[:, t, :])
                a.then_inc(s_var2, 1)

            def normalize2(g, u, nth):
                dve.wait_ge(s_std2, g + 1)
                step(dve.reciprocal(std2[:], std2[:]))
                wait(dve, s_h2_free, g - 1)
                dve.wait_ge(s_h2st[u], 16 * (nth + 1))
                for t in range(TPC):
                    a = dve.tensor_scalar(h2[u][:, t, :], x1[u][:, t, :], mv2[:, t, 0:1], std2[:, t:t + 1],
                                          ALU.subtract, ALU.mult)
                a.then_inc(s_n2, 1)

            for u in range(2):
                dve.sem_inc(s_x1st[u], 16)
                dve.sem_inc(s_h2st[u], 16)
            divide(0, 0, 0)
            divide(1, 1, 0)
            residual(0, 0, 0, 0)
            dve.wait_ge(s_hstore, 16 * (NH + 1))
            normalize2(0, 0, 0)
            def turn(i, u):
                divide(2 * i + u + 2, u, i + 1)
                residual(2 * i + u + 1, 1 - u, i + u, (2 * i + u + 1) // CPB)
                normalize2(2 * i + u + 1, 1 - u, i + u)

            turn(0, 0)
            invert(dve, 1)
            turn(0, 1)
            per = 2 * 3
            with dve.Fori(0, NCH // 2 - 2) as i:
                step.turns(i, per)
                for u in range(2):
                    turn(i + 1, u)
            step.close(NCH // 2 - 2, per)
            residual(NCH - 1, 1, NCH // 2 - 1, B - 1)
            normalize2(NCH - 1, 1, NCH // 2 - 1)

        def merge_gpsimd(pool, step):
            def bias(g, u, nth, b):
                pool.wait_ge(s_xin[u], 16 * (nth + 1))
                hold(pool)
                pool.tensor_tensor(x_in[u][:], x_in[u][:], gbo[:, bass.ds(b, 1), :].to_broadcast([P, TPC, D]),
                                   ALU.add).then_inc(s_xb, 1)

            def modulate(g, u, b):
                pool.wait_ge(s_n2, g + 1)
                hold(pool)
                step(pool.tensor_tensor(h2[u][:], h2[u][:], rowmod[:, bass.ds(b, 1), 2, :].to_broadcast(
                    [P, TPC, D]), ALU.mult))
                hold(pool)
                pool.tensor_tensor(h2[u][:], h2[u][:], rowmod[:, bass.ds(b, 1), 1, :].to_broadcast(
                    [P, TPC, D]), ALU.add).then_inc(s_h2, 1)

            pool.wait_ge(s_gates, 1)
            bias(0, 0, 0, 0)
            bias(1, 1, 0, 0)
            modulate(0, 0, 0)
            with pool.Fori(0, NCH // 2 - 1) as i:
                step.turns(i, 2)
                for u in range(2):
                    bias(2 * i + u + 2, u, i + 1, (i + 1) // (CPB // 2))
                    modulate(2 * i + u + 1, 1 - u, (2 * i + u + 1) // CPB)
            step.close(NCH // 2 - 1, 2)
            modulate(NCH - 1, 1, B - 1)

        def merge_scalar(act):
            act.sem_inc(s_h2T, 1)
            act.sem_inc(s_lg, 1)

            def root2(g):
                act.wait_ge(s_var2, g + 1)
                act.activation(std2[:], mv2[:, :, 1], ACT.Sqrt, bias=eps[:, 0:1]).then_inc(s_std2, 1)

            def take(g, u):
                act.wait_ge(s_h2, g + 1)
                act.dma_start(rows(h2_dram, g * TPC, TPC), h2[u][:]).then_inc(s_h2st[u], 16)
                act.wait_ge(s_h2_free, g + 1)
                for k in range(HALF):
                    act.copy(h2T[:, k, bass.ds(g * CH, CH)], ps[:, 2 + k, :])
                    a = act.copy(h2Tc[u][:, k, :], ps[:, 2 + k, :])
                a.then_inc(s_h2T, 1)

            def take_logits(g):
                act.wait_ge(s_lgp, g + 1)
                act.copy(logits[:, bass.ds(TPC * g, TPC), :].rearrange("p t e -> p (t e)"),
                         ps[:, 7, 0:TPC * E]).then_inc(s_lg, 1)

            root2(0)
            root2(1)
            take(0, 0)
            with act.Fori(0, NCH // 2 - 2) as i:
                for u in range(2):
                    root2(2 * i + u + 2)
                    take(2 * i + u + 1, 1 - u)
                    take_logits(2 * i + u)
            for g in range(NCH - 3, NCH):
                if g == NCH - 3:
                    root2(NCH - 2)
                if g == NCH - 2:
                    root2(NCH - 1)
                if g == NCH - 2:
                    act.wait_ge(s_x1, NCH)
                    shared_silu(act, 0, 0)
                take(g, g % 2)
                take_logits(g - 1)
                if g == NCH - 2:
                    shared_silu(act, 0, 1)
            take_logits(NCH - 1)

        def shared_hidden(dve, g, u, fc):
            dve.wait_ge(s_silu, FC * g + fc + 1)
            if fc == 0:
                wait(dve, s_y, g - 1)
            dve.tensor_tensor(hid[u][:, fc, :], sgate[fc % 2][:], ps[:, GATE_BANK[fc % 2] + 1, :],
                              ALU.mult).then_inc(s_gu_free, 1)

        def route_vector(dve, step):
            shared_hidden(dve, 0, 0, 0)
            shared_hidden(dve, 0, 0, 1)
            by_tile = lambda a: a.unsqueeze(2).to_broadcast([P, NT, E])
            by_expert = lambda a: a.unsqueeze(1).to_broadcast([P, NT, E])
            less8, firsts, tiles = iotas[:, 0:E], iotas[:, E:E + NT], iotas[:, E + NT:E + NT + NTILE]
            dve.wait_ge(s_lg, NCH + 1)
            for u in range(2):
                dve.wait_ge(s_x1st[u], 16 * (NCH // 2 + 1))
                dve.wait_ge(s_h2st[u], 16 * (NCH // 2 + 1))
            step(dve.tensor_reduce(rmax[:], logits[:], AX.X, ALU.max))
            step(dve.tensor_tensor(rt[:], logits[:], by_tile(rmax[:]), ALU.is_ge))
            step(dve.tensor_tensor(rt[:], rt[:], by_expert(less8), ALU.mult))
            step(dve.tensor_reduce(rix[:], rt[:], AX.X, ALU.min))
            dve.tensor_tensor(onehot[:], by_expert(less8), by_tile(rix[:]), ALU.is_equal).then_inc(s_oh, 1)
            shared_hidden(dve, 0, 0, 2)
            dve.wait_ge(s_rank, 1)
            in_tile, totals = (ps[:, RANK_BANK, k * NT * E:(k + 1) * NT * E].rearrange("p (t e) -> p t e", e=E)
                               for k in range(2))
            a, b = ra, rb
            step(dve.tensor_copy(a[:], totals))
            for s in (1, 2, 4, 8, 16):
                dve.tensor_copy(b[:, 0:s, :], a[:, 0:s, :])
                step(dve.tensor_tensor(b[:, s:, :], a[:, s:, :], a[:, :NT - s, :], ALU.add))
                a, b = b, a
            step(dve.tensor_tensor(cmp8[:], a[:, NT - 1, :].unsqueeze(2).to_broadcast([P, E, NT]),
                                   firsts.unsqueeze(1).to_broadcast([P, E, NT]), ALU.is_gt))
            need, p, q, at = (segs[:, k, :] for k in range(4))
            step(dve.tensor_reduce(need, cmp8[:], AX.X, ALU.add))
            step(dve.tensor_copy(p, need))
            for s in (1, 2, 4):
                dve.tensor_copy(q[:, 0:s], p[:, 0:s])
                step(dve.tensor_tensor(q[:, s:], p[:, s:], p[:, :E - s], ALU.add))
                p, q = q, p
            step(dve.tensor_tensor(at, p, need, ALU.subtract))
            shared_hidden(dve, 0, 0, 3)
            step(dve.tensor_scalar(at, at, float(P), None, ALU.mult))
            step(dve.tensor_tensor(rt[:], a[:], totals, ALU.subtract))
            step(dve.tensor_tensor(rt[:], rt[:], in_tile, ALU.add))
            step(dve.tensor_tensor(rt[:], rt[:], by_expert(at), ALU.add))
            step(dve.tensor_tensor(rt[:], rt[:], onehot[:], ALU.mult))
            step(dve.tensor_reduce(rix[:], rt[:], AX.X, ALU.add))
            dve.tensor_copy(slot[:], rix[:])
            step(dve.tensor_tensor(tcmp[:], tiles.unsqueeze(2).to_broadcast([P, NTILE, E]),
                                   p.unsqueeze(1).to_broadcast([P, NTILE, E]), ALU.is_ge))
            step(dve.tensor_reduce(tile_f[:], tcmp[:], AX.X, ALU.add))
            dve.tensor_scalar(tile_e[:], tile_f[:], float(E - 1), None, ALU.min).then_inc(s_route, 1)

        def route_scalar(act):
            act.wait_ge(s_oh, 1)
            act.activation(tags[:, 0:NT, 0], rmax[:], ACT.Sigmoid).then_inc(s_sig, 1)

        def shared_sync(sp):
            sp.wait_ge(s_route, 1)
            for u in range(2):
                sp.wait_ge(s_h2st[u], 16 * (NCH // 2 + 1))
                sp.wait_ge(s_x1st[u], 16 * (NCH // 2 + 1))

            def load(g, u):
                sp.dma_start(xr[u][:], rows(x1_dram, g * TPC, TPC)).then_inc(s_xr[u], 16)

            def token_rows(i, u):
                wait(sp, s_scat[u], 16 * i)
                sp.dma_start(sc_x[u][:, 0:D], h2_dram[bass.ds((NSC * i + u) * P, P), :]).then_inc(s_scx[u], 16)

            for u in range(NSC):
                token_rows(0, u)
            load(0, 0)
            load(1, 1)

            def store(g, u):
                sp.wait_ge(s_x2, g + 2)
                sp.dma_start(rows(x2_dram, g * TPC, TPC), xr[u][:]).then_inc(s_x2st[u], 16)

            with sp.Fori(0, NCH // 2 - 1) as i:
                for u in range(2):
                    for v in range(NSC):
                        token_rows(2 * i + u + 1, v)
                    store(2 * i + u, u)
                    sp.wait_ge(s_x2st[u], 16 * (i + 1))
                    load(2 * i + u + 2, u)
            for v in range(NSC):
                token_rows(NCH - 1, v)
            store(NCH - 2, 0)
            for u in range(NSC):
                sp.wait_ge(s_scat[u], 16 * (NT // NSC))
            for n in range(NX):
                routed_load(sp, (0, n))
            store(NCH - 1, 1)

        def scatter_gpsimd(pool, step):
            pool.wait_ge(s_route, 1)
            pool.wait_ge(s_sig, 1)
            pool.wait_ge(s_zero, 16 * (NTILE // ZERO + 1))

            def scatter(i, u):
                pool.wait_ge(s_scx[u], 16 * (i + 1))
                hold(pool)
                pool.tensor_copy(sc_ix[u][:], slot[:, bass.ds(NSC * i + u, 1)])
                step(pool.tensor_copy(sc_x[u][:, D:XW], tags[:, bass.ds(NSC * i + u, 1), :].squeeze(1)))
                hold(pool)
                pool.indirect_dma_start(xs_dram, bass.IndirectOffsetOnAxis(sc_ix[u][:, 0:1], 0), sc_x[u][:],
                                        None).then_inc(s_scat[u], 16)

            with pool.Fori(0, NT // NSC) as i:
                step.turns(i, NSC)
                for u in range(NSC):
                    scatter(i, u)
            step.close(NT // NSC, NSC)

        def shared_tensor(pe):
            def down(g, u):
                pe.wait_ge(s_gu_free, AHEAD + FC * (g + 1))
                for t in range(TPC):
                    for fc in range(FC):
                        mm = pe.matmul(ps[:, DOWN_BANK[u] + t // 2, t % 2 * D:(t % 2 + 1) * D],
                                       hid[u][:, fc, t * P:(t + 1) * P],
                                       wdT[:, fc, :], start=(fc == 0), stop=(fc == FC - 1))
                mm.then_inc(s_y, 1)

            def gate_up_all(g):
                for fc in range(FC):
                    gate_up(pe, g, fc)

            gate_up(pe, 0, FC - 1)
            with pe.Fori(0, NCH // 2 - 1) as i:
                for u in range(2):
                    gate_up_all(2 * i + u + 1)
                    down(2 * i + u, u)
            gate_up_all(NCH - 1)
            down(NCH - 2, 0)
            down(NCH - 1, 1)

        def shared_silu(act, g, fc):
            act.wait_ge(s_gu, FC * g + fc + 1)
            act.wait_ge(s_gu_free, FC * g + fc + 1)
            act.activation(sgate[fc % 2][:], ps[:, GATE_BANK[fc % 2], :], ACT.Silu).then_inc(s_silu, 1)

        def shared_scalar(act):
            for fc in range(2, FC):
                shared_silu(act, 0, fc)
            route_scalar(act)
            with act.Fori(1, NCH) as g:
                for fc in range(FC):
                    shared_silu(act, g, fc)

        def shared_vector(dve, step):
            def hidden(g, u):
                for fc in range(FC):
                    shared_hidden(dve, g, u, fc)

            def residual(g, u, nth, b):
                dve.wait_ge(s_y, g + 1)
                step(dve.tensor_tensor(ymod[:], ps[:, DOWN_BANK[u]:DOWN_BANK[u] + 2, :].rearrange(
                                           "p c (t d) -> p (c t) d", d=D),
                                       rowmod[:, bass.ds(b, 1), 3, :].to_broadcast([P, TPC, D]), ALU.mult))
                dve.wait_ge(s_xr[u], 16 * (nth + 1))
                dve.tensor_tensor(xr[u][:], xr[u][:], ymod[:], ALU.add).then_inc(s_x2, 1)
                dve.wait_ge(s_x2, g + 2)

            dve.sem_inc(s_x2, 1)
            hidden(1, 1)
            with dve.Fori(0, NCH // 2 - 1) as i:
                step.turns(i, 2)
                for u in range(2):
                    residual(2 * i + u, u, i, i // 2)
                    hidden(2 * i + u + 2, u)
            step.close(NCH // 2 - 1, 2)
            residual(NCH - 2, 0, NCH // 2 - 1, B - 1)
            return lambda: residual(NCH - 1, 1, NCH // 2 - 1, B - 1)

        tnum = lambda k: NX * k[0] + k[1]
        tnth = lambda k: k[0] + k[1] // NX
        tbuf = lambda k: k[1] % NX
        pair = lambda k: k[1] % 2
        egate_bank = lambda k: 1 + pair(k)
        eup_bank = lambda k: 4 - pair(k)

        def turns(eng, turn, lead, step=None):
            trips = (NTILE - 3) // NX
            for n in range(-lead, NX):
                turn((0, n))
            with eng.Fori(0, trips - 1) as i:
                if step:
                    step.turns(i, NX)
                for u in range(NX):
                    turn((i + 1, u))
            if step:
                step.close(trips - 1, NX)
            for n in range(NX * trips, NTILE):
                turn((0, n))

        def later(k, n):
            t = (k[0], k[1] + n)
            return t if not isinstance(k[0], int) or 0 <= tnum(t) < NTILE else None

        def routed_load(sp, k):
            u = tbuf(k)
            wait(sp, s_xs_free, tnum(k) - NX + 1)
            wait(sp, s_sel, tnum(k) - NX + 1)
            sp.dma_start(xs[u][:], xs_dram[bass.ds(tnum(k) * P, P), :]).then_inc(s_xs[u], 16)

        def routed_sync(sp):
            with sp.Fori(1, NTILE // NX) as i:
                for u in range(NX):
                    routed_load(sp, (i, u))
            for n in range(NTILE // NX * NX, NTILE):
                routed_load(sp, (0, n))
            for u in range(NX):
                sp.wait_ge(s_ost[u], 16 * ((NTILE - u + NX - 1) // NX))

        def routed_tensor(pe):
            pe.wait_ge(s_expert, 48 * E)

            def turn_in(k):
                pe.wait_ge(s_xsc, tnum(k) + 1)
                wait(pe, s_xsT, tnum(k))
                for c in range(HALF):
                    mm = pe.transpose(ps[:, 0, c * P:(c + 1) * P], xs[tbuf(k)][:, c * P:(c + 1) * P], ident[:])
                mm.then_inc(s_xs_free, 1)

            def gate_or_up(k, e, w, bank, done):
                u = pair(k)
                if isinstance(k[0], int) and tnum(k) == 1 and w is rgT:
                    pe.wait_ge(s_x2, NCH + 1)
                for c in range(HALF):
                    mm = pe.matmul(ps[:, bank, :], xsT[u][:, c, :], w[:, bass.ds(e, 1), c, :].squeeze(1),
                                   start=(c == 0), stop=(c == 1))
                mm.then_inc(done, 1)

            def turn_hidden(k):
                u = pair(k)
                pe.wait_ge(s_ehid, tnum(k) + 1)
                wait(pe, s_ehT, tnum(k))
                for c in range(FC):
                    mm = pe.transpose(ps[:, 5, c * P:(c + 1) * P], ehid[u][:, c * P:(c + 1) * P], ident[:])
                mm.then_inc(s_ehTp, 1)

            def down(k):
                u = pair(k)
                e = expert_of(k)
                pe.wait_ge(s_ehT, tnum(k) + 1)
                wait(pe, s_eout, tnum(k) - 1)
                for c in range(FC):
                    mm = pe.matmul(ps[:, 6 + u, 0:D], ehT[u][:, c, :], rdT[:, bass.ds(e, 1), c, :].squeeze(1),
                                   start=(c == 0), stop=(c == FC - 1))
                mm.then_inc(s_ey, 1)

            def expert_of(k):
                return pe.value_load(tile_e[0:1, bass.ds(tnum(k), 1)], min_val=0, max_val=E - 1)

            def turn(k):
                this, next1, next2 = (later(k, n) for n in range(3))
                if next1:
                    e = expert_of(next1)
                    pe.wait_ge(s_xsT, tnum(next1) + 1)
                    wait(pe, s_esig, tnum(next1) - 1)
                    gate_or_up(next1, e, rgT, egate_bank(next1), s_egate)
                if this:
                    turn_hidden(this)
                if next1:
                    wait(pe, s_ehid, tnum(next1) - 1)
                    gate_or_up(next1, e, ruT, eup_bank(next1), s_eup)
                if next2:
                    turn_in(next2)
                if this:
                    down(this)

            turns(pe, turn, 2)

        def routed_scalar(act):
            def silu(k):
                u = pair(k)
                act.wait_ge(s_egate, tnum(k) + 1)
                wait(act, s_ehid, tnum(k) - 1)
                act.activation(esig[u][:], ps[:, egate_bank(k), :], ACT.Silu).then_inc(s_esig, 1)

            def take(k):
                u = pair(k)
                act.wait_ge(s_ehTp, tnum(k) + 1)
                wait(act, s_ey, tnum(k) - 1)
                act.copy(ehT[u][:].rearrange("p c n -> p (c n)"), ps[:, 5, :]).then_inc(s_ehT, 1)

            def turn(k):
                if later(k, 1):
                    silu(later(k, 1))
                if later(k, 0):
                    take(k)

            turns(act, turn, 1)

        def routed_vector(dve, step, last_residual):
            def weigh_rows(k):
                u = tbuf(k)
                dve.wait_ge(s_xs[u], 16 * (tnth(k) + 1))
                dve.tensor_scalar(xs[u][:, 0:D], xs[u][:, 0:D], xs[u][:, D:D + 1], None,
                                  ALU.mult).then_inc(s_xsc, 1)

            def rows_in(k):
                dve.wait_ge(s_xs_free, tnum(k) + 1)
                wait(dve, s_eup, tnum(k) - 1)
                dve.tensor_copy(xsT[pair(k)][:].rearrange("p c n -> p (c n)"), ps[:, 0, 0:D]).then_inc(s_xsT, 1)

            def hidden(k):
                u = pair(k)
                dve.wait_ge(s_esig, tnum(k) + 1)
                dve.wait_ge(s_eup, tnum(k) + 1)
                wait(dve, s_ehTp, tnum(k) - 1)
                dve.tensor_tensor(ehid[u][:], esig[u][:], ps[:, eup_bank(k), :], ALU.mult).then_inc(s_ehid, 1)

            def select(k):
                u, flag = pair(k), xs[tbuf(k)][:, D + 2:D + 4]
                wait(dve, s_eout, tnum(k) - 1)
                step(dve.tensor_scalar(gsel[u][:], rowmod[:, 0, 3, :], flag[:, 0:1], None, ALU.mult))
                dve.scalar_tensor_tensor(gsel[u][:], rowmod[:, 1, 3, :], flag[:, 1:2], gsel[u][:], ALU.mult,
                                         ALU.add).then_inc(s_sel, 1)

            def index(k):
                u = tbuf(k)
                wait(dve, s_ost[u], 16 * tnth(k))
                dve.tensor_copy(cix[u][:], xs[u][:, D + 1:D + 2]).then_inc(s_ix, 1)

            def take(k):
                dve.wait_ge(s_ey, tnum(k) + 1)
                dve.wait_ge(s_sel, tnum(k) + 1)
                dve.wait_ge(s_ix, tnum(k) + 1)
                dve.tensor_tensor(eout[tbuf(k)][:], ps[:, 6 + pair(k), 0:D], gsel[pair(k)][:],
                                  ALU.mult).then_inc(s_eout, 1)

            def finish(k):
                u = tbuf(k)
                dve.wait_ge(s_eout, tnum(k) + 1)
                dve.wait_ge(s_x2in[u], 16 * (tnth(k) + 1))
                dve.tensor_tensor(eout[u][:], eout[u][:], x2_in[u][:], ALU.add).then_inc(s_out, 1)

            def turn(k):
                this, next1, next2, next3 = (later(k, n) for n in range(4))
                if next1:
                    hidden(next1)
                if next2:
                    rows_in(next2)
                if next3:
                    weigh_rows(next3)
                if next1:
                    index(next1)
                    select(next1)
                if this:
                    take(this)
                    finish(this)
                if isinstance(k[0], int) and tnum(k) == -2:
                    last_residual()

            turns(dve, turn, 3, step)

        def routed_gpsimd(pool):
            for u in range(2):
                pool.wait_ge(s_x2st[u], 16 * NCH // 2)

            def gather(k):
                u = tbuf(k)
                pool.wait_ge(s_ix, tnum(k) + 1)
                wait(pool, s_out, tnum(k) - NX + 1)
                hold(pool)
                pool.indirect_dma_start(x2_in[u][:], None, x2_dram, bass.IndirectOffsetOnAxis(cix[u][:, 0:1], 0)
                                        ).then_inc(s_x2in[u], 16)

            def scatter(k):
                u = tbuf(k)
                before_k = (k[0], k[1] - 1)
                wait(pool, s_ost[tbuf(before_k)], 16 * (tnth(before_k) + 1))
                pool.wait_ge(s_out, tnum(k) + 1)
                hold(pool)
                pool.indirect_dma_start(out, bass.IndirectOffsetOnAxis(cix[u][:, 0:1], 0), eout[u][:], None
                                        ).then_inc(s_ost[u], 16)

            def turn(k):
                if later(k, 1):
                    gather(later(k, 1))
                if later(k, 0):
                    scatter(k)

            turns(pool, turn, 1)

        @block.sync
        def _(sp):
            setup_sync(sp)
            project_sync(sp)
            attend_sync(sp)
            merge_sync(sp)
            shared_sync(sp)
            routed_sync(sp)

        @block.tensor
        def _(pe):
            setup_tensor(pe)
            project_tensor(pe)
            attend_tensor(pe)
            merge_tensor(pe)
            shared_tensor(pe)
            routed_tensor(pe)

        @block.scalar
        def _(act):
            setup_scalar(act)
            project_scalar(act)
            attend_scalar(act)
            merge_scalar(act)
            shared_scalar(act)
            routed_scalar(act)

        @block.vector
        def _(dve):
            step = Steps(dve, s_chain["dve"])
            setup_vector(dve, step)
            project_vector(dve, step)
            dve.wait_ge(s_late, 16 * len(late_loads))
            attend_vector(dve, step)
            merge_vector(dve, step)
            route_vector(dve, step)
            last_residual = shared_vector(dve, step)
            routed_vector(dve, step, last_residual)

        @block.gpsimd
        def _(pool):
            step = Steps(pool, s_chain["pool"])
            project_gpsimd(pool, step)
            attend_gpsimd(pool, step)
            merge_gpsimd(pool, step)
            scatter_gpsimd(pool, step)
            routed_gpsimd(pool)


def laid_out(a):
    def by_rows(w):
        return w.T.reshape(-1, P, w.shape[0]).transpose(1, 0, 2)

    def experts(w):
        return w.transpose(2, 0, 1).reshape(-1, P, E, w.shape[1]).transpose(1, 2, 0, 3)

    names = ("q", "k", "v", "o")
    at = lambda n: a["L0_attn_" + n]
    ffn = lambda n: a["L0_ffn_" + n]
    token = (np.arange(P)[:, None] + P * np.arange(NT + 1))[:, :, None]
    return {
        "x": at("x").reshape(T, D),
        "cT": a["L0_c"].T.reshape(HALF, P, B).transpose(1, 0, 2),
        "wmod": a["L0_wmod"].reshape(HALF, P, 6 * D).transpose(1, 0, 2),
        "loA": np.stack([at("A" + n) for n in names], 1),
        "loB": np.stack([at("B" + n).T for n in names], 1),
        "wT": np.stack([by_rows(at("W" + n)) for n in names], 1),
        "bqk": np.concatenate([at("bq").reshape(HALF, P), at("bk").reshape(HALF, P)]).T,
        "bv": at("bv"),
        "bo": at("bo"),
        "gateT": by_rows(ffn("gate_w")),
        "wgT": by_rows(ffn("shared_gate")),
        "wuT": by_rows(ffn("shared_up")),
        "wdT": by_rows(ffn("shared_down")),
        "rgT": experts(ffn("r_gate")),
        "ruT": experts(ffn("r_up")),
        "rdT": experts(ffn("r_down")),
        "ident": np.eye(P, dtype=np.float32),
        "before": np.triu(np.ones((P, P), np.float32), 1),
        "tags": np.concatenate([token * 0, token, token < S, (token >= S) & (token < T)], 2).astype(np.float32),
        "iotas": np.tile(np.concatenate([np.arange(E) - E, P * np.arange(NT), np.arange(NTILE)]),
                         (P, 1)).astype(np.float32),
    }


def kernel(**inputs):
    import concourse.bacc as bacc
    from concourse.bass_utils import run_bass_kernel_spmd

    nc = bacc.Bacc("TRN2", target_bir_lowering=False, num_devices=1)
    arrays, io = {}, {}
    for name, a in laid_out({k: np.asarray(v) for k, v in inputs.items()}).items():
        a = np.ascontiguousarray(a)
        arrays["in_" + name] = a
        io[name] = nc.dram_tensor("in_" + name, a.shape, mybir.dt.from_np(a.dtype), kind="ExternalInput").ap()
    out = nc.dram_tensor("out", (T + P, D), F32, kind="ExternalOutput").ap()
    block_kernel(nc, io, out)
    got = run_bass_kernel_spmd(nc, [arrays], core_ids=[0]).results[0]["out"]
    return got[:T].reshape(B, S, D)
```
